# Optimizing a Trainium2 kernel written in Bass

```python
import numpy as np
import jax
import jax.numpy as jnp

def _softmax(x, axis=-1):
    return jax.nn.softmax(x, axis=axis)

def _gelu(x):
    return jax.nn.gelu(x, approximate=True)

def _silu(x):
    return jax.nn.silu(x)

def _sigmoid(x):
    return jax.nn.sigmoid(x)

def _layernorm(x, axis=-1, eps=1e-05):
    m = jnp.mean(x, axis=axis, keepdims=True)
    v = jnp.var(x, axis=axis, keepdims=True)
    return (x - m) / jnp.sqrt(v + eps)

def _scatter_add(tgt, idx, src, axis=0):
    return tgt.at[idx].add(src)

def _segment_sum(src, seg, n):
    return jax.ops.segment_sum(src, seg, n)
kernel_name = 'mk_xattn_ffn_d2_seqx_r8_1cbab2'

def setup_inputs(seed: int=0):
    np.random.seed(seed)
    _w = jnp.asarray

    def _rec_inputs():
        import jax
        import jax.numpy as jnp
        _rk = jax.random.key(seed)
        x = -0.0003929 + 0.9999 * jax.random.normal(jax.random.fold_in(_rk, 1), (4, 256, 256), jnp.float32)
        _lenS = 256 - jax.random.randint(jax.random.fold_in(_rk, 7), (4,), 0, max(1, 256 // 4) + 1, jnp.int32)
        _lenS2 = 256 - jax.random.randint(jax.random.fold_in(_rk, 8), (4,), 0, max(1, 256 // 4) + 1, jnp.int32)
        _ctx_1024P = jax.random.normal(jax.random.fold_in(_rk, 11), (4, 16, 128), jnp.float32)
        _ctx_1024c = jax.random.dirichlet(jax.random.fold_in(_rk, 511), 0.3 * jnp.ones((16,), jnp.float32), (4, 256))
        _ctx_1024t = jnp.einsum('bsk,bkd->bsd', _ctx_1024c, _ctx_1024P)
        _ctx_1024t = _ctx_1024t * jax.lax.rsqrt(jnp.mean(jnp.square(_ctx_1024t)) + 1e-12) * 0.953939
        ctx_1024 = -0.000494167 + 1.00018 * (_ctx_1024t + 0.3 * jax.random.normal(jax.random.fold_in(_rk, 611), (4, 256, 128), jnp.float32))
        _validS = jnp.arange(256)[None, :] < _lenS[:, None]
        _validS2 = jnp.arange(256)[None, :] < _lenS2[:, None]
        _causal = jnp.tril(jnp.ones((256, 256), dtype=bool))
        mask_BxS2_bf1 = jnp.ones((4, 256), dtype=bool)
        return (x, ctx_1024, mask_BxS2_bf1)
    x, ctx_1024, mask_BxS2_bf1 = _rec_inputs()

    def _L0_xattn_setup():
        import jax, jax.numpy as jnp
        import numpy as np
        N_HEADS = 16
        N_KV_HEADS = 8
        HEAD_DIM = 128
        D_TEXT = 256
        D_VISION = 128
        GROUPS = N_HEADS // N_KV_HEADS
        key = jax.random.key(seed)
        ks = jax.random.split(key, 6)
        B, T_text, T_vis = (4, 256, 72)
        text_hidden = jax.random.normal(ks[0], (B, T_text, D_TEXT), dtype=jnp.float32)
        vision_tokens = jax.random.normal(ks[1], (B, T_vis, D_VISION), dtype=jnp.float32)
        vision_mask = jnp.ones((B, T_vis), dtype=bool)
        s = 0.02
        Wq = jax.random.normal(ks[2], (D_TEXT, N_HEADS * HEAD_DIM), dtype=jnp.float32) * s
        Wk = jax.random.normal(ks[3], (D_VISION, N_KV_HEADS * HEAD_DIM), dtype=jnp.float32) * s
        Wv = jax.random.normal(ks[4], (D_VISION, N_KV_HEADS * HEAD_DIM), dtype=jnp.float32) * s
        Wo = jax.random.normal(ks[5], (N_HEADS * HEAD_DIM, D_TEXT), dtype=jnp.float32) * s
        return {'text_hidden': text_hidden, 'vision_tokens': vision_tokens, 'vision_mask': vision_mask, 'Wq': Wq, 'Wk': Wk, 'Wv': Wv, 'Wo': Wo}
    _L0_xattn_all = _L0_xattn_setup()
    _L0_xattn_in = {k: v for k, v in _L0_xattn_all.items() if k in ('Wq', 'Wk', 'Wv', 'Wo')}
    del _L0_xattn_all

    def _L0_ffn_setup():
        import jax, jax.numpy as jnp
        import numpy as np
        B, T, D = (2, 128, 256)
        E, K, H = (64, 4, 64)
        S, HS = (2, H * K)
        CAP = 64
        key = jax.random.key(seed)
        ks = jax.random.split(key, 9)
        scale = 0.02
        return {'x': jax.random.normal(ks[0], (B, T, D), jnp.float32), 'Wr': jax.random.normal(ks[1], (D, E), jnp.float32) * scale, 'router_bias': jnp.zeros((E,), jnp.float32), 'Wg': jax.random.normal(ks[2], (E, D, H), jnp.float32) * scale, 'Wu': jax.random.normal(ks[3], (E, D, H), jnp.float32) * scale, 'Wd': jax.random.normal(ks[4], (E, H, D), jnp.float32) * scale, 'Sg': jax.random.normal(ks[5], (S, D, HS), jnp.float32) * scale, 'Su': jax.random.normal(ks[6], (S, D, HS), jnp.float32) * scale, 'Sd': jax.random.normal(ks[7], (S, HS, D), jnp.float32) * scale}
    _L0_ffn_all = _L0_ffn_setup()
    _L0_ffn_in = {k: v for k, v in _L0_ffn_all.items() if k in ('Wr', 'router_bias', 'Wg', 'Wu', 'Wd', 'Sg', 'Su', 'Sd')}
    del _L0_ffn_all

    def _L1_xattn_setup():
        import jax, jax.numpy as jnp
        import numpy as np
        B_, L_, D_MODEL = (4, 256, 128)
        D_STATE, D_CONV, EXPAND = (16, 4, 2)
        D_INNER = EXPAND * D_MODEL
        DT_RANK = (D_MODEL + 15) // 16

        def silu(x):
            return x * jax.nn.sigmoid(x)
        key = jax.random.key(seed)
        ks = jax.random.split(key, 10)
        f32 = jnp.float32
        hidden_states = jax.random.normal(ks[0], (B_, L_, D_MODEL), dtype=f32)
        z = jax.random.normal(ks[1], (B_, D_INNER, L_), dtype=f32)
        in_proj_w = jax.random.normal(ks[2], (D_INNER, D_MODEL), dtype=f32) * 0.02
        conv_w = jax.random.normal(ks[3], (D_INNER, 1, D_CONV), dtype=f32) * 0.1
        conv_b = jax.random.normal(ks[4], (D_INNER,), dtype=f32) * 0.02
        x_proj_w = jax.random.normal(ks[5], (DT_RANK + 2 * D_STATE, D_INNER), dtype=f32) * 0.02
        dt_proj_w = jax.random.uniform(ks[6], (D_INNER, DT_RANK), dtype=f32, minval=-DT_RANK ** (-0.5), maxval=DT_RANK ** (-0.5))
        dt = jnp.exp(jax.random.uniform(ks[7], (D_INNER,), dtype=f32, minval=np.log(0.001), maxval=np.log(0.1)))
        dt_proj_b = jnp.log(jnp.expm1(dt))
        A_log = jnp.log(jnp.broadcast_to(jnp.arange(1, D_STATE + 1, dtype=f32), (D_INNER, D_STATE)))
        D = jnp.ones((D_INNER,), f32)
        return {'hidden_states': hidden_states, 'z': z, 'in_proj_w': in_proj_w, 'conv_w': conv_w, 'conv_b': conv_b, 'x_proj_w': x_proj_w, 'dt_proj_w': dt_proj_w, 'dt_proj_b': dt_proj_b, 'A_log': A_log, 'D': D}
    _L1_xattn_all = _L1_xattn_setup()
    _L1_xattn_in = {k: v for k, v in _L1_xattn_all.items() if k in ('in_proj_w', 'conv_w', 'conv_b', 'x_proj_w', 'dt_proj_w', 'dt_proj_b', 'A_log', 'D')}
    del _L1_xattn_all

    def _L1_ffn_setup():
        import jax, jax.numpy as jnp
        import numpy as np
        HIDDEN = 256
        NUM_EXPERTS = 32
        TOP_K = 4
        D_MOE = 96
        D_SHARED = 512
        B, S = (1, 256)

        def _moe_forward(hidden_states, gate_w, gate_up_proj, down_proj, shared_gate_w, shared_up_w, shared_down_w, shared_expert_gate_w):
            Bb, Ss, d = hidden_states.shape
            x = hidden_states.reshape(-1, d)
            T = x.shape[0]
            router_logits = x @ gate_w.T
            routing_weights = jax.nn.softmax(router_logits.astype(jnp.float32), axis=-1)
            topk_w, topk_idx = jax.lax.top_k(routing_weights, TOP_K)
            topk_w = topk_w / (jnp.sum(topk_w, axis=-1, keepdims=True) + 1e-20)
            topk_w = topk_w.astype(x.dtype)
            comb = jnp.zeros((T, NUM_EXPERTS), x.dtype).at[jnp.arange(T)[:, None], topk_idx].add(topk_w)
            sh = jax.nn.silu(x @ shared_gate_w.T) * (x @ shared_up_w.T)
            shared_out = sh @ shared_down_w.T
            shared_gate = jax.nn.sigmoid(x @ shared_expert_gate_w.T)
            out0 = shared_gate * shared_out

            def body(acc, inp):
                gu_w, dn_w, w_e = inp
                gu = x @ gu_w.T
                gate, up = (gu[:, :D_MOE], gu[:, D_MOE:])
                h = jax.nn.silu(gate) * up
                y = h @ dn_w.T
                return (acc + w_e[:, None] * y, None)
            out, _ = jax.lax.scan(body, out0, (gate_up_proj, down_proj, comb.T))
            return out.reshape(Bb, Ss, d)
        key = jax.random.key(seed)
        ks = jax.random.split(key, 8)
        sc = 0.02
        return {'hidden_states': jax.random.normal(ks[0], (B, S, HIDDEN), jnp.float32), 'gate_w': jax.random.normal(ks[1], (NUM_EXPERTS, HIDDEN), jnp.float32) * sc, 'gate_up_proj': jax.random.normal(ks[2], (NUM_EXPERTS, 2 * D_MOE, HIDDEN), jnp.float32) * sc, 'down_proj': jax.random.normal(ks[3], (NUM_EXPERTS, HIDDEN, D_MOE), jnp.float32) * sc, 'shared_gate_w': jax.random.normal(ks[4], (D_SHARED, HIDDEN), jnp.float32) * sc, 'shared_up_w': jax.random.normal(ks[5], (D_SHARED, HIDDEN), jnp.float32) * sc, 'shared_down_w': jax.random.normal(ks[6], (HIDDEN, D_SHARED), jnp.float32) * sc, 'shared_expert_gate_w': jax.random.normal(ks[7], (1, HIDDEN), jnp.float32) * sc}
    _L1_ffn_all = _L1_ffn_setup()
    _L1_ffn_in = {k: v for k, v in _L1_ffn_all.items() if k in ('gate_w', 'gate_up_proj', 'down_proj', 'shared_gate_w', 'shared_up_w', 'shared_down_w', 'shared_expert_gate_w')}
    del _L1_ffn_all
    return {'x': x, 'ctx_1024': ctx_1024, 'mask_BxS2_bf1': mask_BxS2_bf1, 'L0_xattn_Wq': _L0_xattn_in['Wq'], 'L0_xattn_Wk': _L0_xattn_in['Wk'], 'L0_xattn_Wv': _L0_xattn_in['Wv'], 'L0_xattn_Wo': _L0_xattn_in['Wo'], 'L0_ffn_Wr': _L0_ffn_in['Wr'], 'L0_ffn_router_bias': _L0_ffn_in['router_bias'], 'L0_ffn_Wg': _L0_ffn_in['Wg'], 'L0_ffn_Wu': _L0_ffn_in['Wu'], 'L0_ffn_Wd': _L0_ffn_in['Wd'], 'L0_ffn_Sg': _L0_ffn_in['Sg'], 'L0_ffn_Su': _L0_ffn_in['Su'], 'L0_ffn_Sd': _L0_ffn_in['Sd'], 'L1_xattn_in_proj_w': _L1_xattn_in['in_proj_w'], 'L1_xattn_conv_w': _L1_xattn_in['conv_w'], 'L1_xattn_conv_b': _L1_xattn_in['conv_b'], 'L1_xattn_x_proj_w': _L1_xattn_in['x_proj_w'], 'L1_xattn_dt_proj_w': _L1_xattn_in['dt_proj_w'], 'L1_xattn_dt_proj_b': _L1_xattn_in['dt_proj_b'], 'L1_xattn_A_log': _L1_xattn_in['A_log'], 'L1_xattn_D': _L1_xattn_in['D'], 'L1_ffn_gate_w': _L1_ffn_in['gate_w'], 'L1_ffn_gate_up_proj': _L1_ffn_in['gate_up_proj'], 'L1_ffn_down_proj': _L1_ffn_in['down_proj'], 'L1_ffn_shared_gate_w': _L1_ffn_in['shared_gate_w'], 'L1_ffn_shared_up_w': _L1_ffn_in['shared_up_w'], 'L1_ffn_shared_down_w': _L1_ffn_in['shared_down_w'], 'L1_ffn_shared_expert_gate_w': _L1_ffn_in['shared_expert_gate_w']}

def reference(x, ctx_1024, mask_BxS2_bf1, L0_xattn_Wq, L0_xattn_Wk, L0_xattn_Wv, L0_xattn_Wo, L0_ffn_Wr, L0_ffn_router_bias, L0_ffn_Wg, L0_ffn_Wu, L0_ffn_Wd, L0_ffn_Sg, L0_ffn_Su, L0_ffn_Sd, L1_xattn_in_proj_w, L1_xattn_conv_w, L1_xattn_conv_b, L1_xattn_x_proj_w, L1_xattn_dt_proj_w, L1_xattn_dt_proj_b, L1_xattn_A_log, L1_xattn_D, L1_ffn_gate_w, L1_ffn_gate_up_proj, L1_ffn_down_proj, L1_ffn_shared_gate_w, L1_ffn_shared_up_w, L1_ffn_shared_down_w, L1_ffn_shared_expert_gate_w):
    import jax
    import jax.numpy as jnp

    def _L0_xattn_ref(text_hidden, vision_tokens, vision_mask, Wq, Wk, Wv, Wo):
        import jax, jax.numpy as jnp
        import numpy as np
        N_HEADS = 16
        N_KV_HEADS = 8
        HEAD_DIM = 128
        D_TEXT = 256
        D_VISION = 128
        GROUPS = N_HEADS // N_KV_HEADS
        B, T_text, _ = text_hidden.shape
        T_vis = vision_tokens.shape[1]
        scale = jnp.float32(np.sqrt(HEAD_DIM))
        q = (text_hidden @ Wq).reshape(B, T_text, N_HEADS, HEAD_DIM).transpose(0, 2, 1, 3)
        k = (vision_tokens @ Wk).reshape(B, T_vis, N_KV_HEADS, HEAD_DIM).transpose(0, 2, 1, 3)
        v = (vision_tokens @ Wv).reshape(B, T_vis, N_KV_HEADS, HEAD_DIM).transpose(0, 2, 1, 3)
        k = jnp.repeat(k, GROUPS, axis=1)
        v = jnp.repeat(v, GROUPS, axis=1)
        scores = jnp.einsum('bhtd,bhsd->bhts', q, k) / scale
        mask = vision_mask[:, None, None, :]
        scores = jnp.where(mask, scores, -jnp.inf)
        attn = jax.nn.softmax(scores, axis=-1)
        attn = jnp.nan_to_num(attn, nan=0.0)
        out = jnp.einsum('bhts,bhsd->bhtd', attn, v)
        out = out.transpose(0, 2, 1, 3).reshape(B, T_text, N_HEADS * HEAD_DIM)
        return out @ Wo

    def _L0_ffn_ref(x, Wr, router_bias, Wg, Wu, Wd, Sg, Su, Sd):
        import jax, jax.numpy as jnp
        import numpy as np
        B, T, D = (2, 128, 256)
        E, K, H = (64, 4, 64)
        S, HS = (2, H * K)
        CAP = 64
        Bx, Tx, Dx = x.shape
        N = Bx * Tx
        flat = x.reshape(N, Dx)
        logits = flat @ Wr + router_bias
        scores = jax.nn.softmax(logits, axis=-1)
        topk_scores, topk_idx = jax.lax.top_k(scores, K)
        topk_scores = topk_scores / topk_scores.sum(-1, keepdims=True)
        eid = topk_idx.reshape(-1)
        w = topk_scores.reshape(-1)
        tok = jnp.repeat(jnp.arange(N), K)
        oh = jax.nn.one_hot(eid, E, dtype=jnp.int32)
        pos = (jnp.cumsum(oh, axis=0) * oh).sum(-1) - 1
        valid = pos < CAP
        xb = jnp.zeros((E, CAP, Dx), x.dtype).at[eid, pos].set(flat[tok], mode='drop')
        h = jax.nn.silu(jnp.einsum('ecd,edh->ech', xb, Wg)) * jnp.einsum('ecd,edh->ech', xb, Wu)
        yb = jnp.einsum('ech,ehd->ecd', h, Wd)
        y = yb[eid, jnp.minimum(pos, CAP - 1)] * (w * valid)[:, None]
        out = jnp.zeros((N, Dx), x.dtype).at[tok].add(y)
        hs = jax.nn.silu(jnp.einsum('nd,sdh->nsh', flat, Sg)) * jnp.einsum('nd,sdh->nsh', flat, Su)
        out = out + jnp.einsum('nsh,shd->nd', hs, Sd)
        return out.reshape(Bx, Tx, Dx)

    def _L1_xattn_ref(hidden_states, z, in_proj_w, conv_w, conv_b, x_proj_w, dt_proj_w, dt_proj_b, A_log, D):
        import jax, jax.numpy as jnp
        import numpy as np
        B_, L_, D_MODEL = (4, 256, 128)
        D_STATE, D_CONV, EXPAND = (16, 4, 2)
        D_INNER = EXPAND * D_MODEL
        DT_RANK = (D_MODEL + 15) // 16

        def silu(x):
            return x * jax.nn.sigmoid(x)
        Bsz, L, _ = hidden_states.shape
        d_inner, _, d_conv = conv_w.shape
        dt_rank = dt_proj_w.shape[1]
        d_state = A_log.shape[1]
        x = jnp.einsum('bld,ed->bel', hidden_states, in_proj_w)
        xc = jax.lax.conv_general_dilated(x, conv_w, window_strides=(1,), padding=[(d_conv - 1, 0)], feature_group_count=d_inner, dimension_numbers=('NCH', 'OIH', 'NCH'))
        x = silu(xc + conv_b[None, :, None])
        x_dbl = jnp.einsum('bdl,ed->bel', x, x_proj_w)
        dt_low, Bm, Cm = jnp.split(x_dbl, [dt_rank, dt_rank + d_state], axis=1)
        dt = jnp.einsum('brl,dr->bdl', dt_low, dt_proj_w)
        dt = jax.nn.softplus(dt + dt_proj_b[None, :, None])
        A = -jnp.exp(A_log)
        dt_t = jnp.moveaxis(dt, -1, 0)
        B_t = jnp.moveaxis(Bm, -1, 0)
        C_t = jnp.moveaxis(Cm, -1, 0)
        u_t = jnp.moveaxis(x, -1, 0)

        def step(state, inp):
            d, b, c, u = inp
            dA = jnp.exp(d[..., None] * A)
            state = state * dA + (d * u)[..., None] * b[:, None, :]
            y = jnp.einsum('bdn,bn->bd', state, c)
            return (state, y)
        state0 = jnp.zeros((Bsz, d_inner, d_state), x.dtype)
        _, ys = jax.lax.scan(step, state0, (dt_t, B_t, C_t, u_t))
        y = jnp.moveaxis(ys, 0, 2)
        y = y + D[None, :, None] * x
        y = y * silu(z)
        return jnp.swapaxes(y, 1, 2)

    def _L1_ffn_ref(hidden_states, gate_w, gate_up_proj, down_proj, shared_gate_w, shared_up_w, shared_down_w, shared_expert_gate_w):
        import jax, jax.numpy as jnp
        import numpy as np
        HIDDEN = 256
        NUM_EXPERTS = 32
        TOP_K = 4
        D_MOE = 96
        D_SHARED = 512
        B, S = (1, 256)

        def _moe_forward(hidden_states, gate_w, gate_up_proj, down_proj, shared_gate_w, shared_up_w, shared_down_w, shared_expert_gate_w):
            Bb, Ss, d = hidden_states.shape
            x = hidden_states.reshape(-1, d)
            T = x.shape[0]
            router_logits = x @ gate_w.T
            routing_weights = jax.nn.softmax(router_logits.astype(jnp.float32), axis=-1)
            topk_w, topk_idx = jax.lax.top_k(routing_weights, TOP_K)
            topk_w = topk_w / (jnp.sum(topk_w, axis=-1, keepdims=True) + 1e-20)
            topk_w = topk_w.astype(x.dtype)
            comb = jnp.zeros((T, NUM_EXPERTS), x.dtype).at[jnp.arange(T)[:, None], topk_idx].add(topk_w)
            sh = jax.nn.silu(x @ shared_gate_w.T) * (x @ shared_up_w.T)
            shared_out = sh @ shared_down_w.T
            shared_gate = jax.nn.sigmoid(x @ shared_expert_gate_w.T)
            out0 = shared_gate * shared_out

            def body(acc, inp):
                gu_w, dn_w, w_e = inp
                gu = x @ gu_w.T
                gate, up = (gu[:, :D_MOE], gu[:, D_MOE:])
                h = jax.nn.silu(gate) * up
                y = h @ dn_w.T
                return (acc + w_e[:, None] * y, None)
            out, _ = jax.lax.scan(body, out0, (gate_up_proj, down_proj, comb.T))
            return out.reshape(Bb, Ss, d)
        return _moe_forward(hidden_states, gate_w, gate_up_proj, down_proj, shared_gate_w, shared_up_w, shared_down_w, shared_expert_gate_w)
    x = x + _L0_xattn_ref(_layernorm(x, axis=-1), ctx_1024, mask_BxS2_bf1, L0_xattn_Wq, L0_xattn_Wk, L0_xattn_Wv, L0_xattn_Wo)
    x = x + _L0_ffn_ref(_layernorm(x, axis=-1), L0_ffn_Wr, L0_ffn_router_bias, L0_ffn_Wg, L0_ffn_Wu, L0_ffn_Wd, L0_ffn_Sg, L0_ffn_Su, L0_ffn_Sd)
    x = x + _L1_xattn_ref(ctx_1024, _layernorm(x, axis=-1), L1_xattn_in_proj_w, L1_xattn_conv_w, L1_xattn_conv_b, L1_xattn_x_proj_w, L1_xattn_dt_proj_w, L1_xattn_dt_proj_b, L1_xattn_A_log, L1_xattn_D)
    x = x + _L1_ffn_ref(_layernorm(x, axis=-1), L1_ffn_gate_w, L1_ffn_gate_up_proj, L1_ffn_down_proj, L1_ffn_shared_gate_w, L1_ffn_shared_up_w, L1_ffn_shared_down_w, L1_ffn_shared_expert_gate_w)
    return x

_drawn_inputs = setup_inputs


def setup_inputs(seed=0):
    import zlib

    import numpy as np

    out = dict(_drawn_inputs(seed))
    spreads = {'L0_ffn_router_bias': (0.0, 0.8), 'L1_xattn_D': (1.0, 0.6)}
    factors = {'L0_xattn_Wq': 8.0,
     'L0_xattn_Wk': 8.0,
     'L0_ffn_Wr': 8.0,
     'L0_ffn_Wg': 8.0,
     'L0_ffn_Wu': 8.0,
     'L0_ffn_Wd': 8.0,
     'L1_xattn_in_proj_w': 4.43,
     'L1_xattn_conv_w': 4.584,
     'L1_xattn_conv_b': 8.0,
     'L1_xattn_x_proj_w': 8.0,
     'L1_xattn_dt_proj_w': 8.0,
     'L1_xattn_dt_proj_b': 8.0,
     'L1_xattn_A_log': 8.0,
     'L1_ffn_gate_w': 8.0,
     'L1_ffn_gate_up_proj': 8.0,
     'L1_ffn_down_proj': 8.0,
     'L1_ffn_shared_gate_w': 4.741,
     'L1_ffn_shared_up_w': 4.677,
     'L1_ffn_shared_down_w': 4.65,
     'L1_ffn_shared_expert_gate_w': 8.0}
    for name, (base, spread) in spreads.items():
        noise = np.random.default_rng([zlib.crc32(name.encode()), seed]).standard_normal(out[name].shape)
        drawn = base * np.exp(spread * noise) if base else spread * noise
        out[name] = jnp.asarray(drawn.astype(out[name].dtype))
    for name, factor in factors.items():
        out[name] = (out[name] * factor).astype(out[name].dtype)
    return out
```

```python
from contextlib import ExitStack

import concourse.bass as bass
from concourse import mybir

F32 = mybir.dt.float32
BF16 = mybir.dt.bfloat16
I32 = mybir.dt.int32
U32 = mybir.dt.uint32
U8 = mybir.dt.uint8
ALU = mybir.AluOpType
ACT = mybir.ActivationFunctionType
AX = mybir.AxisListType.X

P = 128
BATCH = 4
SEQ = 256
TOKENS = BATCH * SEQ
D = 256
DC = D // P
TILES = TOKENS // P
CTX = 128
HEADS = 16
GROUPS = 8
PAIR = HEADS // GROUPS
EPS = 1e-5
MASKED = -1e9

STATE = 16
RANK = 8
CONV = 4
INNER = 256
IC = INNER // P
PAD = 4

TOPK = 4
E0, H0, CAP = 64, 64, 64
E1, H1 = 32, 96
SHARED = 512
SC = SHARED // P
ROWS0 = E0 * CAP
BLOCK = 128
BLOCKS = E1 + (TOKENS * TOPK - E1) // BLOCK
BLOCKS += -BLOCKS % 8
ROWS1 = BLOCKS * BLOCK
STEP = 2 * P
AHEAD = 4
KT = TOPK * TILES
UNDERFLOW = -104.0
CONSTS = 6
SKIP = float(1 << 20)

PREP_FOLD = 2 * PAIR * D + 2 * CTX
SMALL = CONV + 3 + STATE
ATTN_SCALE = float(CTX) ** -0.5


class Steps:

    def __init__(self, engine, semaphore):
        self.engine, self.semaphore, self.count = engine, semaphore, 0

    def mark(self, instruction):
        instruction.then_inc(self.semaphore, 1)
        self.count += 1
        return self.count

    def wait(self, instruction):
        self.engine.wait_ge(self.semaphore, self.mark(instruction))

    def settle(self):
        self.engine.wait_ge(self.semaphore, self.count)


def program(nc, t, out, stop=9):
    with ExitStack() as ctx:
        def sem(name):
            return ctx.enter_context(nc.semaphore(name))

        def sb(name, shape, dt=F32, stack=ctx):
            return stack.enter_context(nc.sbuf_tensor(name, shape, dt))

        def dram(name, shape, dt=F32):
            return nc.dram_tensor(name, shape, dt).ap()

        bank = [ctx.enter_context(nc.psum_tensor(f"bank{i}", [P, 512], F32)) for i in range(8)]

        bc_dram = dram("bc_dram", (2 * STATE, TOKENS))
        xb0_dram = dram("xb0_dram", (ROWS0, D))
        yb0_dram = dram("yb0_dram", (ROWS0, D))
        xb1_dram = dram("xb1_dram", (ROWS1, D))
        yb1_dram = dram("yb1_dram", (ROWS1, D))

        xr = sb("xr", [P, TILES, D])
        xn = sb("xn", [P, TILES, D])
        xnT = sb("xnT", [P, DC, TOKENS])
        y_ssm = sb("y_ssm", [P, IC, TOKENS])
        shared_w = sb("shared_w", [P, 3072])
        route_w = sb("route_w", [P, DC, E0])
        route_bias = sb("route_bias", [P, E0])
        route1_w = sb("route1_w", [P, DC, E1 + 1])
        ident = sb("ident", [P, P])
        earlier = sb("earlier", [P, P], BF16)
        ones_bf = sb("ones_bf", [P, P], BF16)
        zeros = sb("zeros", [P, D])
        iota_e = sb("iota_e", [P, E0])
        iota_blk = sb("iota_blk", [P, TILES])
        iota_j = sb("iota_j", [1, BLOCKS])
        stats = sb("stats", [P, TILES, 6])
        moments = sb("moments", [P, TILES, 2])
        rstd = sb("rstd", [P, TILES])
        eps_col = sb("eps_col", [P, 1])
        pace = sb("pace", [P, 1])

        phase1 = ctx.enter_context(ExitStack())
        ctxT = sb("ctxT", [P, TOKENS], stack=phase1)
        ctxN = sb("ctxN", [P, TILES, CTX], stack=phase1)
        ctxN_cur = sb("ctxN_cur", [P, 2, CTX], stack=phase1)
        mask_u8 = sb("mask_u8", [P, BATCH, SEQ], U8, stack=phase1)
        mask_all = sb("mask_all", [P, BATCH, SEQ + 1], stack=phase1)
        mask_cur = sb("mask_cur", [P, SEQ + 1], stack=phase1)
        fold_w = sb("fold_w", [P, 2, PREP_FOLD], stack=phase1)
        qk_w = sb("qk_w", [P, GROUPS, PAIR, DC, CTX], stack=phase1)
        vo_w = sb("vo_w", [P, GROUPS, PAIR, D], stack=phase1)
        in_w = sb("in_w", [P, INNER], stack=phase1)
        xproj_w = sb("xproj_w", [P, IC, 2 * STATE + RANK], stack=phase1)
        dtproj_w = sb("dtproj_w", [2 * STATE + RANK, INNER], stack=phase1)
        small_w = sb("small_w", [P, IC, SMALL], stack=phase1)
        a_neg = sb("a_neg", [P, IC, STATE], stack=phase1)
        xpad = sb("xpad", [P, IC, BATCH, PAD + SEQ], stack=phase1)
        u_in = sb("u_in", [P, IC, TOKENS], stack=phase1)
        dt_sb = sb("dt_sb", [P, IC, TOKENS], stack=phase1)
        du_sb = sb("du_sb", [P, IC, TOKENS], stack=phase1)
        xdbl = sb("xdbl", [2 * STATE + RANK, TOKENS], stack=phase1)
        decay = sb("decay", [P, 2, TOKENS], stack=phase1)
        drive = sb("drive", [P, 2, TOKENS], stack=phase1)
        b_bc = sb("b_bc", [P, 2, TOKENS], stack=phase1)
        c_bc = sb("c_bc", [P, 2, TOKENS], stack=phase1)
        qT = sb("qT", [P, 2, PAIR * SEQ], stack=phase1)
        probs = sb("probs", [P, 2, 4, SEQ], stack=phase1)
        probsT = sb("probsT", [P, 2, 2, PAIR * SEQ], stack=phase1)
        attT = sb("attT", [P, 2, PAIR * SEQ], stack=phase1)
        rowmax = sb("rowmax", [P, 2, 4], stack=phase1)
        negmax = sb("negmax", [P, 2, 4], stack=phase1)
        rowsum = sb("rowsum", [P, 2, 4], stack=phase1)
        rowinv = sb("rowinv", [P, 2, 4], stack=phase1)
        phase1.close()

        hshT = sb("hshT", [P, SC, TOKENS])
        sh_silu = sb("sh_silu", [P, 2, 512])
        logits = sb("logits", [P, TILES, E0])
        expl = sb("expl", [P, TILES, E0])
        tmax = sb("tmax", [P, TILES])
        top_v = sb("top_v", [P, TILES, 8])
        top_i = sb("top_i", [P, TILES, 8], U32)
        top_e = sb("top_e", [P, TILES, 8])
        zsum = sb("zsum", [P, TILES])
        psum4 = sb("psum4", [P, TILES])
        wts = sb("wts", [P, TOPK, TILES])
        idxf = sb("idxf", [P, TOPK, TILES])
        onehot = sb("onehot", [P, KT, E0])
        prod = sb("prod", [P, KT, E0])
        chosen = sb("chosen", [P, TILES * E0], BF16)
        cum = sb("cum", [P, TILES, E0])
        pos = sb("pos", [P, KT])
        over = sb("over", [P, KT])
        slot = sb("slot", [P, KT])
        slot_put = sb("slot_put", [P, KT], U32)
        slot_get = sb("slot_get", [P, KT], U32)
        counts = sb("counts", [P, E1])
        above = sb("above", [P, E1, TILES])
        nblk = sb("nblk", [P, E1])
        blk_end = sb("blk_end", [P, E1])
        first_slot = sb("first_slot", [P, E1])
        ones_row = sb("ones_row", [P, E1])
        behind = sb("behind", [1, BLOCKS, E1])
        blk_ef = sb("blk_ef", [1, BLOCKS])
        blk_e = sb("blk_e", [1, BLOCKS], I32)
        sgate = sb("sgate", [P, TILES])
        xb = sb("xb", [P, AHEAD, 2, D])
        ew = sb("ew", [P, AHEAD, 1536])
        xbT = sb("xbT", [P, 2, DC, STEP])
        h_silu = sb("h_silu", [P, 2, 2, P])
        hT = sb("hT", [P, 2, 2, P])
        yb = sb("yb", [P, 2, 2, D])
        yg = sb("yg", [P, 2, TOPK, D])

        ld_x, ld_ctx, ld_mask, ld_ssm, ld_route = (sem(f"ld_{n}") for n in ("x", "ctx", "mask", "ssm", "route"))
        ld_fold = [sem("ld_fold_even"), sem("ld_fold_odd")]
        ld_shared, ld_shared1 = sem("ld_shared"), sem("ld_shared1")
        zero_filled = sem("zero_filled")
        consts_set, zeros_set = sem("consts_set"), sem("zeros_set")
        dve_step, act_step, pool_step = sem("dve_step"), sem("act_step"), sem("pool_step")
        ln_var, ln_std, ln_out, lnT_done, lnT_copied = (
            sem(f"ln_{n}") for n in ("var", "std", "out", "transposed", "copied"))
        fold_done, m_copied, g_copied = sem("fold_done"), sem("m_copied"), sem("g_copied")
        xin_done, xin_copied, conv_done, u_ready, xdbl_done, xdbl_copied, bc_stored = (
            sem(n) for n in ("xin_done", "xin_copied", "conv_done", "u_ready", "xdbl_done",
                             "xdbl_copied", "bc_stored"))
        dt_done, sp_neg, sp_exp, sp_one, sp_ln, a_exp, a_ready, dt_ready = (
            sem(n) for n in ("dt_done", "sp_neg", "sp_exp", "sp_one", "sp_ln", "a_exp", "a_ready",
                             "dt_ready"))
        bc_loaded = [sem("bc_loaded_even"), sem("bc_loaded_odd")]
        decay_free, decay_set, drive_set, product_set, y_added = (
            sem(n) for n in ("decay_free", "decay_set", "drive_set", "product_set", "y_added"))
        scan_done = sem("scan_done")
        mask_set, ctx_set, inv_made = sem("mask_set"), sem("ctx_set"), sem("inv_made")
        q_done, q_copied, s_done, s_masked, max_ready, exp_done, inv_ready, p_ready = (
            sem(n) for n in ("q_done", "q_copied", "s_done", "s_masked", "max_ready", "exp_done",
                             "inv_ready", "p_ready"))
        t_done, pt_copied, pv_done, u_copied, o_done, o_taken = (
            sem(n) for n in ("t_done", "pt_copied", "pv_done", "u_copied", "o_done", "o_taken"))
        z_ready, z_gated, zT_done, z_added = (sem(n) for n in ("z_ready", "z_gated", "zT_done", "z_added"))
        out_stored = sem("out_stored")

        class Moe:

            def __init__(self, n, experts, rows, xb, yb):
                self.experts, self.rows, self.steps = experts, rows, rows // STEP
                self.xb, self.yb = xb, yb
                self.logits_done = sem(f"logits_done{n}")
                self.key_ready = sem(f"key_ready{n}")
                self.exp_ready = sem(f"exp_ready{n}")
                self.chosen_ready = sem(f"chosen_ready{n}")
                self.cum_done = sem(f"cum_done{n}")
                self.cum_copied = sem(f"cum_copied{n}")
                self.slots_ready = sem(f"slots_ready{n}")
                self.scattered = sem(f"scattered{n}")
                self.sh_gu_done = sem(f"sh_gu_done{n}")
                self.sh_silu_done = sem(f"sh_silu_done{n}")
                self.sh_h_ready = sem(f"sh_h_ready{n}")
                self.sh_y_done = sem(f"sh_y_done{n}")
                self.sh_y_added = sem(f"sh_y_added{n}")
                self.xt_done = sem(f"xt_done{n}")
                self.xt_copied = sem(f"xt_copied{n}")
                self.gu_done = sem(f"gu_done{n}")
                self.silu_done = sem(f"silu_done{n}")
                self.h_ready = sem(f"h_ready{n}")
                self.y_done = sem(f"y_done{n}")
                self.y_copied = sem(f"y_copied{n}")
                self.blocks_ready = sem(f"blocks_ready{n}")
                self.tokens_loaded = [sem(f"tokens_loaded{n}_{k}") for k in range(AHEAD)]
                self.weights_loaded = [sem(f"weights_loaded{n}_{k}") for k in range(AHEAD)]
                self.stored = [sem(f"y_stored_even{n}"), sem(f"y_stored_odd{n}")]
                self.gathered = [sem(f"gathered_even{n}"), sem(f"gathered_odd{n}")]
                self.combined = sem(f"combined{n}")

        moe0 = Moe(0, E0, ROWS0, xb0_dram, yb0_dram)
        moe1 = Moe(1, E1, ROWS1, xb1_dram, yb1_dram)

        def dst_tokens(ap):
            return ap.rearrange("(a p) d -> p a d", p=P)

        block = ctx.enter_context(nc.Block())

        @block.sync
        def _(sp):
            sp.dma_start(xr[:], dst_tokens(t["x"])).then_inc(ld_x, 16)
            sp.dma_start(ctxT[:], t["ctxT"]).then_inc(ld_ctx, 16)
            sp.dma_start(in_w[:], t["in_w"]).then_inc(ld_ssm, 16)
            sp.dma_start(small_w[:], t["small_w"]).then_inc(ld_ssm, 16)
            sp.dma_start(xproj_w[:], t["xproj_w"]).then_inc(ld_ssm, 16)
            sp.dma_start(dtproj_w[2 * STATE:, :], t["dtproj_w"]).then_inc(ld_ssm, 16)

            for g in range(2):
                sp.dma_start(fold_w[:, g, :], t["fold_w"][g]).then_inc(ld_fold[g], 16)
            sp.dma_start(ctxN[:], dst_tokens(t["ctx"])).then_inc(ld_ctx, 16)
            sp.dma_start(mask_u8[:].rearrange("p b s -> p (b s)"),
                         t["mask"].broadcast_to([P, TOKENS])).then_inc(ld_mask, 16)
            with sp.Fori(0, GROUPS // 2 - 1) as m:
                for g in range(2):
                    sp.wait_ge(fold_done, 2 * m + g + 1)
                    sp.dma_start(fold_w[:, g, :], t["fold_w"][bass.ds(2 * m + (g + 2), 1)]
                                 .rearrange("a p f -> (a p) f")).then_inc(ld_fold[g], 16)

            sp.dma_start(shared_w[:], t["shared0_w"]).then_inc(ld_shared, 16)
            sp.dma_start(route_w[:], t["route0_w"]).then_inc(ld_route, 16)
            sp.dma_start(route_bias[:], t["route0_bias"].broadcast_to([P, E0])).then_inc(ld_route, 16)
            sp.dma_start(route1_w[:], t["route1_w"]).then_inc(ld_route, 16)

            sp.wait_ge(xdbl_copied, 2)
            sp.dma_start(bc_dram, xdbl[0:2 * STATE, :]).then_inc(bc_stored, 16)
            sp.wait_ge(bc_stored, 16)

            def spread(n, parity):
                for row, dst in ((n, b_bc), (n + STATE, c_bc)):
                    sp.dma_start(dst[:, parity, :], bc_dram[bass.ds(row, 1), :].broadcast_to([P, TOKENS])
                                 ).then_inc(bc_loaded[parity], 16)

            for n in range(2):
                spread(n, n)
            sp.wait_ge(zeros_set, 1)
            for table, rows in ((xb0_dram, ROWS0), (xb1_dram, ROWS1)):
                for r in range(0, rows, 2048):
                    sp.dma_start(dst_tokens(table[r:r + min(2048, rows - r), :]),
                                 zeros[:].unsqueeze(1).broadcast_to([P, min(2048, rows - r) // P, D])
                                 ).then_inc(zero_filled, 16)
            with sp.Fori(0, STATE // 2 - 1) as m:
                for n in range(2):
                    sp.wait_ge(y_added, 4 * m + (2 * n + 3))
                    spread(2 * m + (n + 2), n)

            def expert_loads(moe, load_weights):
                def load_tokens(s, k):
                    sp.dma_start(xb[:, k], dst_tokens(moe.xb[bass.ds(s * STEP, STEP), :])
                                 ).then_inc(moe.tokens_loaded[k], 16)

                def store(s, parity):
                    sp.wait_ge(moe.y_copied, s + 1)
                    sp.dma_start(dst_tokens(moe.yb[bass.ds(s * STEP, STEP), :]), yb[:, parity]
                                 ).then_inc(moe.stored[parity], 16)

                if moe is moe0:
                    sp.wait_ge(o_taken, BATCH + 1)
                else:
                    sp.wait_ge(moe0.y_done, moe0.steps)
                    sp.wait_ge(moe.blocks_ready, 1)
                for k in range(AHEAD):
                    load_weights(k, k)
                sp.wait_ge(moe.scattered, 16 * KT)
                for k in range(AHEAD):
                    load_tokens(k, k)
                with sp.Fori(1, moe.steps // AHEAD) as m:
                    for k in range(AHEAD):
                        s = m * AHEAD + k
                        sp.wait_ge(moe.xt_done, s - (AHEAD - 1))
                        load_tokens(s, k)
                        sp.wait_ge(moe.y_done, s - (AHEAD - 1))
                        load_weights(s, k)
                        store(s - AHEAD, k % 2)
                for s in range(moe.steps - AHEAD, moe.steps):
                    store(s, s % 2)

            def weights0(s, k):
                sp.dma_start(ew[:, k, :], t["experts0_w"][bass.ds(s, 1)].rearrange("a p f -> (a p) f")
                             ).then_inc(moe0.weights_loaded[k], 16)

            def weights1(s, k):
                for j in range(2):
                    e = sp.value_load(blk_e[0:1, bass.ds(s * 2 + j, 1)], min_val=0, max_val=E1 - 1)
                    sp.dma_start(ew[:, k, j * 384:(j + 1) * 384],
                                 t["experts1_gu"][bass.ds(e, 1)].rearrange("a p f -> (a p) f")
                                 ).then_inc(moe1.weights_loaded[k], 16)
                    sp.dma_start(ew[0:H1, k, 768 + j * D:768 + (j + 1) * D],
                                 t["experts1_d"][bass.ds(e, 1)].rearrange("a p f -> (a p) f")
                                 ).then_inc(moe1.weights_loaded[k], 16)

            if stop >= 2:
                sp.wait_ge(zero_filled, 16 * (ROWS0 // 2048 + -(-ROWS1 // 2048)))
                expert_loads(moe0, weights0)
                sp.wait_ge(moe0.sh_y_done, 4)
                sp.dma_start(shared_w[:], t["shared1_w"]).then_inc(ld_shared1, 16)
            if stop >= 4:
                expert_loads(moe1, weights1)
            if stop == 1:
                sp.wait_ge(o_taken, BATCH + 1)
            elif stop == 3:
                sp.wait_ge(z_added, 1)
            else:
                sp.wait_ge((moe0 if stop == 2 else moe1).combined, TILES)
            sp.dma_start(dst_tokens(out), xr[:]).then_inc(out_stored, 16)
            sp.wait_ge(out_stored, 16)

        @block.gpsimd
        def _(pool):
            steps = Steps(pool, pool_step)
            steps.mark(nc.gpsimd.memset(zeros[:], 0.0))
            steps.mark(nc.gpsimd.memset(ident[:], 0.0))
            steps.mark(nc.gpsimd.memset(ones_bf[:], 1.0))
            steps.wait(nc.gpsimd.memset(earlier[:], 1.0))
            nc.gpsimd.affine_select(out=ident[:], in_=ident[:], compare_op=ALU.not_equal, fill=1.0, base=0,
                                    pattern=[[-1, P]], channel_multiplier=1).then_inc(consts_set, 1)
            nc.gpsimd.affine_select(out=earlier[:], in_=earlier[:], compare_op=ALU.is_gt, fill=0.0, base=0,
                                    pattern=[[1, P]], channel_multiplier=-1).then_inc(consts_set, 1)
            nc.gpsimd.iota(iota_e[:], pattern=[[1, E0]], base=0, channel_multiplier=0,
                           allow_small_or_imprecise_dtypes=True).then_inc(consts_set, 1)
            nc.gpsimd.iota(iota_blk[:], pattern=[[BLOCK, TILES]], base=0, channel_multiplier=0,
                           allow_small_or_imprecise_dtypes=True).then_inc(consts_set, 1)
            nc.gpsimd.iota(iota_j[:], pattern=[[1, BLOCKS]], base=0, channel_multiplier=0,
                           allow_small_or_imprecise_dtypes=True).then_inc(consts_set, 1)
            nc.gpsimd.memset(eps_col[:], EPS).then_inc(consts_set, 1)
            nc.gpsimd.memset(zeros[:], 0.0).then_inc(zeros_set, 1)

            pool.wait_ge(mask_set, 1)
            pool.wait_ge(ld_ctx, 32)
            nc.gpsimd.tensor_copy(mask_cur[:], mask_all[:, 0, :]).then_inc(mask_set, 1)
            nc.gpsimd.tensor_copy(ctxN_cur[:], ctxN[:, 0:2, :]).then_inc(ctx_set, 1)
            mask_flat = mask_all[:].rearrange("p b s -> p (b s)")
            ctx_flat = ctxN[:].rearrange("p a d -> p (a d)")
            with pool.Fori(0, BATCH - 1) as b:
                pool.wait_ge(inv_ready, 8 * b + 8)
                nc.gpsimd.tensor_copy(mask_cur[:], mask_flat[:, bass.ds((b + 1) * (SEQ + 1), SEQ + 1)]
                                      ).then_inc(mask_set, 1)
                pool.wait_ge(pv_done, 8 * b + 8)
                nc.gpsimd.tensor_copy(ctxN_cur[:].rearrange("p a d -> p (a d)"),
                                      ctx_flat[:, bass.ds((b + 1) * 2 * CTX, 2 * CTX)]).then_inc(ctx_set, 1)

            def dispatch(moe):
                pool.wait_ge(moe.slots_ready, 1)
                pool.wait_ge(zero_filled, 16 * (ROWS0 // 2048 + -(-ROWS1 // 2048)))
                for k in range(TOPK):
                    for a in range(TILES):
                        c = k * TILES + a
                        nc.gpsimd.indirect_dma_start(
                            out=moe.xb, out_offset=bass.IndirectOffsetOnAxis(ap=slot_put[:, c:c + 1], axis=0),
                            in_=xn[:, a, :], in_offset=None, bounds_check=moe.rows - 1, oob_is_err=False,
                        ).then_inc(moe.scattered, 16)

            def collect(moe):
                for parity in range(2):
                    pool.wait_ge(moe.stored[parity], 16 * (moe.steps // 2))
                for a in range(TILES):
                    if a >= 2:
                        pool.wait_ge(moe.combined, a - 1)
                    for k in range(TOPK):
                        c = k * TILES + a
                        nc.gpsimd.indirect_dma_start(
                            out=yg[:, a % 2, k, :], out_offset=None, in_=moe.yb,
                            in_offset=bass.IndirectOffsetOnAxis(ap=slot_get[:, c:c + 1], axis=0),
                            bounds_check=moe.rows - 1, oob_is_err=False,
                        ).then_inc(moe.gathered[a % 2], 16)

            if stop >= 2:
                dispatch(moe0)
                collect(moe0)
            if stop >= 4:
                dispatch(moe1)
                collect(moe1)

        @block.tensor
        def _(pe):
            pe.sem_inc(t_done, 1)
            mm = nc.tensor.matmul

            pe.wait_ge(ld_ctx, 16)
            pe.wait_ge(ld_ssm, 64)
            for c in range(IC):
                for h in range(2):
                    mm(bank[4 + 2 * c + h][:], in_w[:, c * P:(c + 1) * P], ctxT[:, h * 512:(h + 1) * 512],
                       start=True, stop=True).then_inc(xin_done, 1)

            def turn_norm(n):
                for c in range(DC):
                    for h in range(2):
                        if n == 0:
                            pe.wait_ge(consts_set, CONSTS)
                            pe.wait_ge(xin_copied, 4)
                        for a in range(4):
                            tile = 4 * h + a
                            pe.wait_ge(ln_out, TILES * n + tile + 1)
                            ins = nc.tensor.transpose(bank[4 + 2 * c + h][:, a * P:(a + 1) * P],
                                                      xn[:, tile, c * P:(c + 1) * P], ident[:])
                        ins.then_inc(lnT_done, 1)

            def fold(m, buf, first):
                pe.wait_ge(ld_fold[buf], 16 * m + 16)
                if not first:
                    pe.wait_ge(m_copied, 2 * m + buf - 1)
                    pe.wait_ge(g_copied, 2 * m + buf - 1)
                w = fold_w[:, buf, :]
                wq, wk = w[:, 0:PAIR * D], w[:, PAIR * D:PAIR * D + CTX]
                wv, wo = w[:, PAIR * D + CTX:PAIR * D + 2 * CTX], w[:, PAIR * D + 2 * CTX:]
                for j in range(PAIR):
                    for c in range(DC):
                        mm(bank[2 * buf][:, (j * DC + c) * CTX:(j * DC + c + 1) * CTX],
                           wq[:, j * D + c * P:j * D + (c + 1) * P], wk, start=True, stop=True)
                for j in range(PAIR):
                    ins = mm(bank[2 * buf + 1][:, j * D:(j + 1) * D], wv, wo[:, j * D:(j + 1) * D],
                             start=True, stop=True)
                ins.then_inc(fold_done, 1)

            for g in range(2):
                fold(0, g, True)
            with pe.Fori(1, GROUPS // 2) as m:
                for g in range(2):
                    fold(m, g, False)
            turn_norm(0)

            pe.wait_ge(u_ready, 2)
            pe.wait_ge(m_copied, GROUPS)
            pe.wait_ge(g_copied, GROUPS)
            for h in range(2):
                for c in range(IC):
                    ins = mm(bank[h][0:2 * STATE + RANK, :], xproj_w[:, c, :], u_in[:, c, h * 512:(h + 1) * 512],
                             start=(c == 0), stop=(c == IC - 1))
                ins.then_inc(xdbl_done, 1)
            pe.wait_ge(lnT_copied, 4)
            for c in range(IC):
                for h in range(2):
                    pe.wait_ge(xdbl_copied, h + 1)
                    mm(bank[4 + 2 * c + h][:], dtproj_w[2 * STATE:, c * P:(c + 1) * P],
                       xdbl[2 * STATE:, h * 512:(h + 1) * 512], start=True, stop=True).then_inc(dt_done, 1)

            def queries(i, b, hp):
                for j in range(PAIR):
                    for c in range(DC):
                        ins = mm(bank[0][:, j * SEQ:(j + 1) * SEQ], qk_w[:, hp, j, c, :],
                                 xnT[:, c, bass.ds(b * SEQ, SEQ)], start=(c == 0), stop=(c == DC - 1))
                ins.then_inc(q_done, 1)

            def scores(i, b, hp):
                for j in range(4):
                    ins = mm(bank[1 + j // 2][:, j % 2 * SEQ:(j % 2 + 1) * SEQ],
                             qT[:, hp % 2, j * P:(j + 1) * P], ctxT[:, bass.ds(b * SEQ, SEQ)],
                             start=True, stop=True)
                ins.then_inc(s_done, 1)

            def output(i, hp):
                for j in range(PAIR):
                    for a in range(2):
                        ins = mm(bank[6][:, a * D:(a + 1) * D], attT[:, hp % 2, (2 * j + a) * P:(2 * j + a + 1) * P],
                                 vo_w[:, hp, j, :], start=(hp == 0 and j == 0 and a == 0),
                                 stop=(hp == GROUPS - 1 and j == PAIR - 1), skip_group_check=True)
                return ins

            def attention(b, last):
                for hp in range(GROUPS):
                    i = b * GROUPS + hp
                    more = not (last and hp == GROUPS - 1)
                    if more:
                        pe.wait_ge(q_copied, i + 2)
                        pe.wait_ge(s_masked, i + 1)
                        nb = b + (hp + 1) // GROUPS
                        scores(i + 1, nb, (hp + 1) % GROUPS)
                    pe.wait_ge(p_ready, i + 1)
                    pe.wait_ge(pt_copied, i + 1)
                    for s in range(2):
                        for j in range(4):
                            ins = nc.tensor.transpose(bank[3 + s][:, j * P:(j + 1) * P],
                                                      probs[:, hp % 2, j, s * P:(s + 1) * P], ident[:])
                    ins.then_inc(t_done, 1)
                    if not (last and hp >= GROUPS - 2):
                        pe.wait_ge(q_copied, i + 2)
                        queries(i + 2, b + (hp + 2) // GROUPS, (hp + 2) % GROUPS)
                    if hp == 0:
                        pe.wait_ge(ctx_set, b + 1)
                    pe.wait_ge(pt_copied, i + 2)
                    pe.wait_ge(u_copied, i + 1)
                    for s in range(2):
                        ins = mm(bank[5][:], ctxN_cur[:, s, :], probsT[:, hp % 2, s, :],
                                 start=(s == 0), stop=(s == 1))
                    ins.then_inc(pv_done, 1)
                    if hp == 1:
                        pe.wait_ge(o_taken, b + 1)
                    if hp > 0:
                        pe.wait_ge(u_copied, i + 1)
                        output(i - 1, hp - 1)
                pe.wait_ge(u_copied, b * GROUPS + GROUPS + 1)
                output(i, GROUPS - 1).then_inc(o_done, 1)

            pe.wait_ge(xdbl_copied, 2)
            queries(0, 0, 0)
            pe.wait_ge(q_copied, 1)
            queries(1, 0, 1)
            scores(0, 0, 0)
            with pe.Fori(0, BATCH - 1) as b:
                attention(b, False)
            attention(BATCH - 1, True)

            def route(moe):
                w, n = (route_w, E0) if moe is moe0 else (route1_w, E1 + 1)
                pe.wait_ge(ld_route, 48)
                for a in range(TILES):
                    for c in range(DC):
                        ins = mm(bank[0][:, a * n:(a + 1) * n], xnT[:, c, a * P:(a + 1) * P], w[:, c, :],
                                 start=(c == 0), stop=(c == DC - 1))
                ins.then_inc(moe.logits_done, 1)

            def count(moe):
                n = moe.experts
                pe.wait_ge(moe.chosen_ready, 1)
                for a in range(TILES):
                    for b in range(a + 1):
                        ins = mm(bank[1][:, a * n:(a + 1) * n], (earlier if b == a else ones_bf)[:],
                                 chosen[:, b * n:(b + 1) * n], start=(b == 0), stop=(b == a))
                if moe is moe1:
                    for b in range(TILES):
                        ins = mm(bank[2][:, 0:n], ones_bf[:], chosen[:, b * n:(b + 1) * n],
                                 start=(b == 0), stop=(b == TILES - 1))
                ins.then_inc(moe.cum_done, 1)

            def shared(moe, k):
                j, h = k // 2, k % 2
                if k >= 2:
                    pe.wait_ge(moe.sh_h_ready, k - 1)
                for w, first in ((0, 4), (1, 6)):
                    for c in range(DC):
                        ins = mm(bank[first + h][:], shared_w[:, w * 1024 + c * SHARED + j * P:
                                                              w * 1024 + c * SHARED + (j + 1) * P],
                                 xnT[:, c, h * 512:(h + 1) * 512], start=(c == 0), stop=(c == DC - 1))
                ins.then_inc(moe.sh_gu_done, 1)

            def shared_out(moe):
                pe.wait_ge(moe.sh_h_ready, 2 * SC)
                for a in range(TILES):
                    for j in range(SC):
                        ins = mm(bank[4 + a // 2][:, a % 2 * D:(a % 2 + 1) * D], hshT[:, j, a * P:(a + 1) * P],
                                 shared_w[:, 2048 + j * D:2048 + (j + 1) * D], start=(j == 0), stop=(j == SC - 1))
                    if a % 2:
                        ins.then_inc(moe.sh_y_done, 1)

            def experts(moe):
                hidden = P if moe is moe0 else H1
                weights_each = 16 if moe is moe0 else 64

                def turn(s, m, k, first):
                    pe.wait_ge(moe.tokens_loaded[k], 16 * m + 16)
                    if not first:
                        pe.wait_ge(moe.xt_copied, s - 1)
                    for c in range(DC):
                        for u in range(2):
                            ins = nc.tensor.transpose(bank[k % 2][:, (c * 2 + u) * P:(c * 2 + u + 1) * P],
                                                      xb[:, k, u, c * P:(c + 1) * P], ident[:])
                    ins.then_inc(moe.xt_done, 1)

                def gate_up(s, m, k, first):
                    parity = k % 2
                    pe.wait_ge(moe.weights_loaded[k], weights_each * m + weights_each)
                    pe.wait_ge(moe.xt_copied, s + 1)
                    if not first:
                        pe.wait_ge(moe.h_ready, s - 1)
                    for u in range(2):
                        for w in range(2):
                            for c in range(DC):
                                o = ((u * 2 + w) * DC + c) * hidden
                                ins = mm(bank[2 + parity][0:hidden, (w * 2 + u) * P:(w * 2 + u + 1) * P],
                                         ew[:, k, o:o + hidden], xbT[:, parity, c, u * P:(u + 1) * P],
                                         start=(c == 0), stop=(c == DC - 1))
                    ins.then_inc(moe.gu_done, 1)

                def down(s, k, first):
                    parity = k % 2
                    pe.wait_ge(moe.h_ready, s + 1)
                    if not first:
                        pe.wait_ge(moe.y_copied, s - 1)
                    o = 4 * DC * hidden
                    for u in range(2):
                        ins = mm(bank[4 + parity][:, u * D:(u + 1) * D], hT[0:hidden, parity, u, :],
                                 ew[0:hidden, k, o + u * D:o + (u + 1) * D], start=True, stop=True)
                    ins.then_inc(moe.y_done, 1)

                def steps(m, first, last):
                    for k in range(AHEAD):
                        s = m * AHEAD + k
                        if not (last and k == AHEAD - 1):
                            turn(s + 1, m + (k + 1) // AHEAD, (k + 1) % AHEAD, first and k == 0)
                        gate_up(s, m, k, first and k < 2)
                        if not (first and k == 0):
                            down(s - 1, (k - 1) % AHEAD, first and k < 3)

                pe.wait_ge(moe.sh_y_added, 4)
                pe.wait_ge(moe.cum_copied, 1)
                turn(0, 0, 0, True)
                steps(0, True, False)
                with pe.Fori(1, moe.steps // AHEAD - 1) as m:
                    steps(m, False, False)
                steps(moe.steps // AHEAD - 1, False, True)
                down(moe.steps - 1, AHEAD - 1, False)

            def feed_forward(moe, n):
                turn_norm(n)
                pe.wait_ge(lnT_copied, 4 * min(n, 2) + 4)
                route(moe)
                if moe is moe1:
                    pe.wait_ge(ld_shared1, 16)
                else:
                    pe.wait_ge(ld_shared, 16)
                for k in range(2 * SC):
                    shared(moe, k)
                    if k == 5:
                        count(moe)
                shared_out(moe)
                experts(moe)

            if stop >= 2:
                feed_forward(moe0, 1)
            if stop >= 3:
                pe.wait_ge(z_gated, 1)
                for b in range(BATCH):
                    for lc in range(2):
                        for c in range(IC):
                            ins = nc.tensor.transpose(bank[b][:, lc * D + c * P:lc * D + (c + 1) * P],
                                                      xn[:, 2 * b + c, lc * P:(lc + 1) * P], ident[:])
                ins.then_inc(zT_done, 1)
            if stop >= 4:
                feed_forward(moe1, 3)

        @block.scalar
        def _(act):
            steps = Steps(act, act_step)
            act.sem_inc(pt_copied, 1)
            act.sem_inc(u_copied, 1)

            def run(out_, in_, func, **kw):
                return nc.scalar.activation(out_, in_, func, **kw)

            def norm_std(n):
                act.wait_ge(ln_var, n + 1)
                if n == 0:
                    act.wait_ge(consts_set, CONSTS)
                run(rstd[:], moments[:, :, 1], ACT.Sqrt, bias=eps_col[:]).then_inc(ln_std, 1)

            def norm_copy(n):
                turned = 4 * min(n, 2)
                for c in range(DC):
                    for h in range(2):
                        act.wait_ge(lnT_done, turned + 2 * c + h + 1)
                        run(xnT[:, c, h * 512:(h + 1) * 512], bank[4 + 2 * c + h][:], ACT.Copy
                            ).then_inc(lnT_copied, 1)

            norm_std(0)
            act.wait_ge(ld_ssm, 64)
            run(a_neg[:], small_w[:, :, CONV + 3:], ACT.Exp).then_inc(a_exp, 1)

            qk_flat = qk_w[:].rearrange("p g j c d -> p (g j c d)")

            def copy_fold(g, buf):
                act.wait_ge(fold_done, g + 1)
                run(qk_flat[:, bass.ds(g * 512, 512)], bank[2 * buf][:], ACT.Copy).then_inc(m_copied, 1)

            with act.Fori(0, GROUPS // 2) as m:
                for g in range(2):
                    copy_fold(2 * m + g, g)
            for c in range(IC):
                act.wait_ge(conv_done, c + 1)
                run(u_in[:, c, :], u_in[:, c, :], ACT.Silu, bias=small_w[:, c, CONV:CONV + 1]).then_inc(u_ready, 1)
            norm_copy(0)
            act.wait_ge(sp_neg, 1)
            run(decay[:], decay[:], ACT.Exp).then_inc(sp_exp, 1)
            act.wait_ge(sp_one, 1)
            run(drive[:], du_sb[:], ACT.Ln).then_inc(sp_ln, 1)

            def copy_q(i, hp):
                act.wait_ge(q_done, i + 1)
                run(qT[:, hp % 2, :], bank[0][:], ACT.Copy).then_inc(q_copied, 1)

            def softmax_exp(i, hp):
                act.wait_ge(max_ready, i + 1)
                for j in range(4):
                    ins = run(probs[:, hp % 2, j, :], probs[:, hp % 2, j, :], ACT.Exp, scale=ATTN_SCALE,
                              bias=negmax[:, hp % 2, j:j + 1], accum_out=rowsum[:, hp % 2, j:j + 1])
                ins.then_inc(exp_done, 1)

            def softmax_scale(i, hp):
                act.wait_ge(inv_ready, i + 1)
                for j in range(4):
                    ins = run(probs[:, hp % 2, j, :], probs[:, hp % 2, j, :], ACT.Copy,
                              scale=rowinv[:, hp % 2, j:j + 1])
                ins.then_inc(p_ready, 1)

            a_flat = a_neg[:]

            def decays(i, b, hp):
                act.wait_ge(decay_free, i + 1)
                n, c = b * (STATE // BATCH) + hp // 2, hp % 2
                run(decay[:, hp % 2, :].rearrange("p (b l) -> p b l", b=BATCH)[:, :, 1:],
                    dt_sb[:, c, :].rearrange("p (b l) -> p b l", b=BATCH)[:, :, 1:], ACT.Exp,
                    scale=a_flat[:, c, bass.ds(n, 1)]).then_inc(decay_set, 1)

            def attention(b, last):
                for hp in range(GROUPS):
                    i = b * GROUPS + hp
                    act.wait_ge(t_done, i + 2)
                    for s in range(2):
                        ins = run(probsT[:, hp % 2, s, :], bank[3 + s][:], ACT.Copy)
                    ins.then_inc(pt_copied, 1)
                    if not (last and hp >= GROUPS - 2):
                        copy_q(i + 2, hp)
                    if not (last and hp == GROUPS - 1):
                        softmax_exp(i + 1, hp + 1)
                    act.wait_ge(pv_done, i + 1)
                    run(attT[:, hp % 2, :], bank[5][:], ACT.Copy).then_inc(u_copied, 1)
                    decays(i, b, hp)
                    if not (last and hp == GROUPS - 1):
                        softmax_scale(i + 1, hp + 1)

            copy_q(0, 0)
            copy_q(1, 1)
            softmax_exp(0, 0)
            softmax_scale(0, 0)
            act.wait_ge(dt_ready, 1)
            act.wait_ge(a_ready, 1)
            with act.Fori(0, BATCH - 1) as b:
                attention(b, False)
            attention(BATCH - 1, True)

            def feed_forward(moe, n):
                norm_std(n)
                norm_copy(n)
                act.wait_ge(moe.key_ready, 1)
                run(expl[:, :, 0:moe.experts], logits[:, :, 0:moe.experts], ACT.Exp)
                if moe is moe1:
                    run(sgate[:], sgate[:], ACT.Exp, scale=-1.0)
                run(top_e[:], top_v[:], ACT.Exp).then_inc(moe.exp_ready, 1)
                for k in range(2 * SC):
                    act.wait_ge(moe.sh_gu_done, k + 1)
                    if k >= 2:
                        act.wait_ge(moe.sh_h_ready, k - 1)
                    run(sh_silu[:, k % 2, :], bank[4 + k % 2][:], ACT.Silu).then_inc(moe.sh_silu_done, 1)
                hidden = P if moe is moe0 else H1

                def copy_turned(s, parity):
                    act.wait_ge(moe.xt_done, s + 1)
                    run(xbT[:, parity].rearrange("p c t -> p (c t)"), bank[parity][:], ACT.Copy
                        ).then_inc(moe.xt_copied, 1)

                def silu(s, parity):
                    act.wait_ge(moe.gu_done, s + 1)
                    if moe is moe0:
                        for e in range(2):
                            r = slice(e * H0, (e + 1) * H0)
                            ins = run(h_silu[r, parity, :, r],
                                      bank[2 + parity][r, 0:2 * P].rearrange("p (u t) -> p u t", u=2)[:, :, r],
                                      ACT.Silu)
                    else:
                        ins = run(h_silu[0:hidden, parity].rearrange("p u t -> p (u t)"),
                                  bank[2 + parity][0:hidden, 0:2 * P], ACT.Silu)
                    ins.then_inc(moe.silu_done, 1)

                copy_turned(0, 0)
                for s in range(AHEAD):
                    copy_turned(s + 1, (s + 1) % 2)
                    silu(s, s % 2)
                with act.Fori(1, moe.steps // AHEAD - 1) as m:
                    for k in range(AHEAD):
                        copy_turned(m * AHEAD + (k + 1), (k + 1) % 2)
                        silu(m * AHEAD + k, k % 2)
                for s in range(moe.steps - AHEAD, moe.steps):
                    if s < moe.steps - 1:
                        copy_turned(s + 1, (s + 1) % 2)
                    silu(s, s % 2)

            if stop >= 2:
                feed_forward(moe0, 1)
            if stop >= 3:
                norm_std(2)
                act.wait_ge(ln_out, TILES * 3)
                run(xn[:], xn[:], ACT.Silu).then_inc(z_ready, 1)
            if stop >= 4:
                feed_forward(moe1, 3)

        @block.vector
        def _(dve):
            steps = Steps(dve, dve_step)
            dve.sem_inc(o_taken, 1)
            dve.sem_inc(y_added, 1)
            v = nc.vector

            def norm(n):
                for a in range(TILES):
                    ins = v.bn_stats(stats[:, a, :], xr[:, a, :])
                    steps.mark(ins)
                steps.settle()
                for a in range(TILES):
                    ins = v.bn_aggr(moments[:, a, :], stats[:, a, :])
                    steps.mark(ins)
                steps.settle()
                v.tensor_copy(stats[:, :, 0], moments[:, :, 1]).then_inc(ln_var, 1)
                dve.wait_ge(ln_std, n + 1)
                steps.wait(v.reciprocal(rstd[:], rstd[:]))
                for a in range(TILES):
                    v.tensor_scalar(xn[:, a, :], xr[:, a, :], moments[:, a, 0:1], rstd[:, a:a + 1],
                                    ALU.subtract, ALU.mult).then_inc(ln_out, 1)

            dve.wait_ge(ld_mask, 16)
            steps.mark(v.tensor_scalar(mask_all[:, :, 0:SEQ], mask_u8[:], 1.0, -MASKED, ALU.subtract, ALU.mult))
            v.tensor_reduce(mask_all[:, :, SEQ], mask_u8[:], AX, ALU.max).then_inc(mask_set, 1)
            for c in range(IC):
                ins = v.memset(xpad[:, c, :, 0:PAD], 0.0)
                steps.mark(ins)
            dve.wait_ge(ld_x, 16)
            norm(0)
            for c in range(IC):
                for h in range(2):
                    dve.wait_ge(xin_done, 2 * c + h + 1)
                    v.tensor_copy(xpad[:, c, 2 * h:2 * h + 2, PAD:],
                                  bank[4 + 2 * c + h][:].rearrange("p (b l) -> p b l", b=2)).then_inc(xin_copied, 1)
            dve.wait_ge(xin_copied, 4)
            dve.wait_ge(ld_ssm, 64)
            steps.settle()

            u4 = u_in[:].rearrange("p c (b l) -> p c b l", b=BATCH)
            vo_flat = vo_w[:].rearrange("p g j d -> p (g j d)")

            for k in range(CONV):
                for c in range(IC):
                    src = xpad[:, c, :, PAD - CONV + 1 + k:PAD - CONV + 1 + k + SEQ]
                    w = small_w[:, c, k:k + 1]
                    if k == 0:
                        ins = v.tensor_scalar(u4[:, c], src, w, None, ALU.mult)
                    else:
                        ins = v.scalar_tensor_tensor(u4[:, c], src, w, u4[:, c], ALU.mult, ALU.add)
                    if k < CONV - 1:
                        steps.mark(ins)
                    else:
                        ins.then_inc(conv_done, 1)
                if k < CONV - 1:
                    steps.settle()

            def copy_fold(g, buf):
                dve.wait_ge(fold_done, g + 1)
                v.tensor_copy(vo_flat[:, bass.ds(g * 512, 512)], bank[2 * buf + 1][:]).then_inc(g_copied, 1)

            with dve.Fori(0, GROUPS // 2) as m:
                for g in range(2):
                    copy_fold(2 * m + g, g)
            for h in range(2):
                dve.wait_ge(xdbl_done, h + 1)
                v.tensor_copy(xdbl[:, h * 512:(h + 1) * 512], bank[h][0:2 * STATE + RANK, :]).then_inc(xdbl_copied, 1)
            dve.wait_ge(a_exp, 1)
            v.tensor_scalar(a_neg[:], a_neg[:], -1.0, None, ALU.mult).then_inc(a_ready, 1)
            for c in range(IC):
                for h in range(2):
                    dve.wait_ge(dt_done, 2 * c + h + 1)
                    steps.mark(v.tensor_scalar(dt_sb[:, c, h * 512:(h + 1) * 512], bank[4 + 2 * c + h][:],
                                               small_w[:, c, CONV + 1:CONV + 2], None, ALU.add))
            steps.settle()
            v.scalar_tensor_tensor(decay[:], dt_sb[:], -1.0, dt_sb[:], ALU.mult, ALU.min).then_inc(sp_neg, 1)
            dve.wait_ge(u_ready, 2)
            for c in range(IC):
                steps.mark(v.tensor_scalar(y_ssm[:, c, :], u_in[:, c, :], small_w[:, c, CONV + 2:CONV + 3], None, ALU.mult))
            dve.wait_ge(sp_exp, 1)
            v.tensor_scalar(du_sb[:], decay[:], 1.0, None, ALU.add).then_inc(sp_one, 1)
            dve.wait_ge(sp_one, 1)
            steps.wait(v.scalar_tensor_tensor(decay[:], du_sb[:], 1.0, decay[:], ALU.subtract, ALU.subtract))
            dve.wait_ge(sp_ln, 1)
            steps.wait(v.tensor_tensor(decay[:], drive[:], decay[:], ALU.subtract))
            steps.wait(v.scalar_tensor_tensor(dt_sb[:], dt_sb[:], 0.0, decay[:], ALU.max, ALU.add))
            steps.wait(v.tensor_tensor(du_sb[:], dt_sb[:], u_in[:], ALU.mult))
            for n in range(2):
                v.memset(decay[:, n, :].rearrange("p (b l) -> p b l", b=BATCH)[:, :, 0:1], 0.0).then_inc(decay_free, 1)
            dve.wait_ge(decay_free, 2)
            v.memset(rowmax[:], 0.0).then_inc(dt_ready, 1)
            dve.wait_ge(dt_ready, 1)

            def softmax_max(i, hp):
                dve.wait_ge(s_done, i + 1)
                v.memset(pace[:], 0.0)
                for j in range(4):
                    ins = v.tensor_tensor_reduce(
                        out=probs[:, hp % 2, j, :], in0=bank[1 + j // 2][:, j % 2 * SEQ:(j % 2 + 1) * SEQ],
                        in1=mask_cur[:, 0:SEQ], scale=1.0, scalar=-3e38, op0=ALU.add, op1=ALU.max,
                        accum_out=rowmax[:, hp % 2, j:j + 1])
                ins.then_inc(s_masked, 1)
                dve.wait_ge(s_masked, i + 1)
                v.tensor_scalar(negmax[:, hp % 2, :], rowmax[:, hp % 2, :], -ATTN_SCALE, None, ALU.mult
                                ).then_inc(max_ready, 1)

            def softmax_inv(i, hp):
                dve.wait_ge(exp_done, i + 1)
                v.reciprocal(rowinv[:, hp % 2, :], rowsum[:, hp % 2, :]).then_inc(inv_made, 1)
                dve.wait_ge(inv_made, i + 1)
                v.tensor_scalar(rowinv[:, hp % 2, :], rowinv[:, hp % 2, :], mask_cur[:, SEQ:SEQ + 1], None,
                                ALU.mult).then_inc(inv_ready, 1)

            def mixer_drive(i, b, hp):
                k, c = hp // 2, hp % 2
                dve.wait_ge(bc_loaded[k % 2], b * (32 * STATE // BATCH // 2) + 32 * (k // 2 + 1))
                dve.wait_ge(y_added, i + 1)
                v.tensor_tensor(drive[:, 0, :], du_sb[:, c, :], b_bc[:, k % 2, :], ALU.mult).then_inc(drive_set, 1)

            def mixer_scan(i, b, hp):
                k, c = hp // 2, hp % 2
                dve.wait_ge(decay_set, i + 1)
                dve.wait_ge(drive_set, i + 1)
                v.tensor_tensor_scan(drive[:, 1, :], decay[:, hp % 2, :], drive[:, 0, :], 0.0, ALU.mult, ALU.add
                                     ).then_inc(decay_free, 1)
                dve.wait_ge(decay_free, i + 3)
                v.tensor_tensor(drive[:, 1, :], drive[:, 1, :], c_bc[:, k % 2, :], ALU.mult).then_inc(product_set, 1)
                dve.wait_ge(product_set, i + 1)
                v.tensor_tensor(y_ssm[:, c, :], y_ssm[:, c, :], drive[:, 1, :], ALU.add).then_inc(y_added, 1)

            xr_flat = xr[:].rearrange("p a d -> p (a d)")

            def attention(b, last):
                for hp in range(GROUPS):
                    i = b * GROUPS + hp
                    more = not (last and hp == GROUPS - 1)
                    if more:
                        if hp == GROUPS - 1:
                            dve.wait_ge(mask_set, b + 3)
                        dve.wait_ge(t_done, i + 1)
                        softmax_max(i + 1, hp + 1)
                    mixer_drive(i, b, hp)
                    if more:
                        softmax_inv(i + 1, hp + 1)
                    mixer_scan(i, b, hp)
                dve.wait_ge(o_done, b + 1)
                v.tensor_tensor(xr_flat[:, bass.ds(b * 2 * D, 2 * D)], xr_flat[:, bass.ds(b * 2 * D, 2 * D)],
                                bank[6][:], ALU.add).then_inc(o_taken, 1)

            dve.wait_ge(mask_set, 2)
            softmax_max(0, 0)
            softmax_inv(0, 0)
            with dve.Fori(0, BATCH - 1) as b:
                attention(b, False)
            attention(BATCH - 1, True)
            dve.wait_ge(o_taken, BATCH + 1)

            def feed_forward(moe, n):
                norm(n)
                E = moe.experts
                lg, ex = logits[:, :, 0:E], expl[:, :, 0:E]
                hot = onehot[:].rearrange("p a e -> p (a e)")[:, 0:KT * E]
                prd = prod[:].rearrange("p a e -> p (a e)")[:, 0:KT * E]
                dve.wait_ge(moe.logits_done, 1)
                if moe is moe0:
                    steps.wait(v.tensor_tensor(lg, bank[0][:].rearrange("p (a e) -> p a e", e=E),
                                               route_bias[:].unsqueeze(1).broadcast_to([P, TILES, E]), ALU.add))
                else:
                    src = bank[0][:, 0:TILES * (E + 1)].rearrange("p (a e) -> p a e", e=E + 1)
                    steps.mark(v.tensor_copy(lg, src[:, :, 0:E]))
                    steps.wait(v.tensor_copy(sgate[:], src[:, :, E]))
                steps.wait(v.tensor_reduce(tmax[:], lg, AX, ALU.max))
                steps.wait(v.tensor_tensor(lg, lg, tmax[:].unsqueeze(2).broadcast_to([P, TILES, E]), ALU.subtract))
                steps.wait(v.tensor_scalar(lg, lg, UNDERFLOW, None, ALU.max))
                for a in range(TILES):
                    steps.mark(v.max(top_v[:, a, :], lg[:, a, :]))
                steps.settle()
                for a in range(TILES):
                    ins = v.max_index(top_i[:, a, :], top_v[:, a, :], lg[:, a, :])
                    steps.mark(ins)
                steps.settle()
                v.tensor_copy(idxf[:], top_i[:, :, 0:TOPK].rearrange("p a k -> p k a")).then_inc(moe.key_ready, 1)
                dve.wait_ge(moe.key_ready, 1)
                dve.wait_ge(consts_set, CONSTS)
                steps.wait(v.tensor_tensor(hot.rearrange("p (a e) -> p a e", e=E),
                                           iota_e[:, 0:E].unsqueeze(1).broadcast_to([P, KT, E]),
                                           idxf[:].rearrange("p k a -> p (k a)").unsqueeze(2).broadcast_to([P, KT, E]),
                                           ALU.is_equal))
                with nc.allow_low_precision(reason="sums of zeros and a one are exact"):
                    v.tensor_reduce(chosen[:, 0:TILES * E], hot.rearrange("p (k m) -> p m k", k=TOPK), AX,
                                    ALU.add).then_inc(moe.chosen_ready, 1)

                def shared_h(k):
                    dve.wait_ge(moe.sh_silu_done, k + 1)
                    v.tensor_tensor(hshT[:, k // 2, k % 2 * 512:(k % 2 + 1) * 512], sh_silu[:, k % 2, :],
                                    bank[6 + k % 2][:], ALU.mult).then_inc(moe.sh_h_ready, 1)

                for k in range(3):
                    shared_h(k)
                dve.wait_ge(moe.exp_ready, 1)
                steps.wait(v.tensor_reduce(zsum[:], ex, AX, ALU.add))
                steps.wait(v.reciprocal(zsum[:], zsum[:]))
                steps.wait(v.tensor_tensor(wts[:], top_e[:, :, 0:TOPK].rearrange("p a k -> p k a"),
                                           zsum[:].unsqueeze(1).broadcast_to([P, TOPK, TILES]), ALU.mult))
                steps.wait(v.tensor_reduce(psum4[:], wts[:].rearrange("p k a -> p a k"), AX, ALU.add))
                if moe is moe1:
                    steps.wait(v.tensor_scalar(psum4[:], psum4[:], 1e-20, None, ALU.add))
                steps.wait(v.reciprocal(psum4[:], psum4[:]))
                steps.wait(v.tensor_tensor(wts[:], wts[:], psum4[:].unsqueeze(1).broadcast_to([P, TOPK, TILES]), ALU.mult))
                for k in range(3, 6):
                    shared_h(k)
                dve.wait_ge(moe.cum_done, 1)
                cm = cum[:].rearrange("p a e -> p (a e)")[:, 0:TILES * E]
                if moe is moe0:
                    v.tensor_copy(cm, bank[1][:, 0:TILES * E]).then_inc(moe.cum_copied, 1)
                    dve.wait_ge(moe.cum_copied, 1)
                else:
                    steps.wait(v.tensor_copy(counts[:], bank[2][:, 0:E]))
                    steps.wait(v.tensor_tensor(above[:], counts[:].unsqueeze(2).broadcast_to([P, E, TILES]),
                                               iota_blk[:].unsqueeze(1).broadcast_to([P, E, TILES]), ALU.is_gt))
                    steps.mark(v.memset(ones_row[:], 1.0))
                    steps.wait(v.tensor_reduce(nblk[:], above[:], AX, ALU.add))
                    steps.wait(v.tensor_tensor_scan(blk_end[:], ones_row[:], nblk[:], 0.0, ALU.mult, ALU.add))
                    steps.wait(v.tensor_tensor(first_slot[:], blk_end[:], nblk[:], ALU.subtract))
                    steps.wait(v.tensor_scalar(first_slot[:], first_slot[:], float(BLOCK), None, ALU.mult))
                    v.tensor_tensor(cm.rearrange("p (a e) -> p a e", e=E),
                                    bank[1][:, 0:TILES * E].rearrange("p (a e) -> p a e", e=E),
                                    first_slot[:].unsqueeze(1).broadcast_to([P, TILES, E]), ALU.add
                                    ).then_inc(moe.cum_copied, 1)
                    dve.wait_ge(moe.cum_copied, 1)
                steps.wait(v.tensor_tensor(prd.rearrange("p (k m) -> p k m", k=TOPK),
                                           hot.rearrange("p (k m) -> p k m", k=TOPK),
                                           cm.unsqueeze(1).broadcast_to([P, TOPK, TILES * E]), ALU.mult))
                steps.wait(v.tensor_reduce(pos[:], prd.rearrange("p (a e) -> p a e", e=E), AX, ALU.add))
                fidx = idxf[:].rearrange("p k a -> p (k a)")
                fw = wts[:].rearrange("p k a -> p (k a)")
                if moe is moe0:
                    steps.mark(v.tensor_scalar(over[:], pos[:], float(CAP), None, ALU.is_ge))
                    steps.wait(v.tensor_scalar(slot[:], pos[:], float(CAP - 1), None, ALU.min))
                    steps.wait(v.scalar_tensor_tensor(slot[:], fidx, float(CAP), slot[:], ALU.mult, ALU.add))
                    steps.mark(v.tensor_copy(slot_get[:], slot[:]))
                    steps.wait(v.scalar_tensor_tensor(slot[:], over[:], SKIP, slot[:], ALU.mult, ALU.add))
                    steps.wait(v.tensor_scalar(over[:], over[:], -1.0, 1.0, ALU.mult, ALU.add))
                    steps.wait(v.tensor_tensor(fw, fw, over[:], ALU.mult))
                    v.tensor_copy(slot_put[:], slot[:]).then_inc(moe.slots_ready, 1)
                else:
                    steps.wait(v.tensor_copy(slot_get[:], pos[:]))
                    v.tensor_copy(slot_put[:], pos[:]).then_inc(moe.slots_ready, 1)
                    steps.wait(v.tensor_tensor(behind[:], iota_j[:].unsqueeze(2).broadcast_to([1, BLOCKS, E]),
                                               blk_end[0:1, :].unsqueeze(1).broadcast_to([1, BLOCKS, E]), ALU.is_ge))
                    steps.wait(v.tensor_reduce(blk_ef[:], behind[:], AX, ALU.add))
                    v.tensor_scalar(blk_e[:], blk_ef[:], float(E - 1), None, ALU.min).then_inc(moe.blocks_ready, 1)
                for k in range(6, 2 * SC):
                    shared_h(k)
                if moe is moe1:
                    steps.wait(v.tensor_scalar(sgate[:], sgate[:], 1.0, None, ALU.add))
                    steps.wait(v.reciprocal(sgate[:], sgate[:]))
                for q in range(4):
                    dve.wait_ge(moe.sh_y_done, q + 1)
                    if moe is moe0:
                        v.tensor_tensor(xr[:, 2 * q:2 * q + 2, :], xr[:, 2 * q:2 * q + 2, :],
                                        bank[4 + q][:].rearrange("p (a d) -> p a d", a=2), ALU.add
                                        ).then_inc(moe.sh_y_added, 1)
                    else:
                        for a in range(2):
                            ins = v.scalar_tensor_tensor(xr[:, 2 * q + a, :], bank[4 + q][:, a * D:(a + 1) * D],
                                                         sgate[:, 2 * q + a:2 * q + a + 1], xr[:, 2 * q + a, :],
                                                         ALU.mult, ALU.add)
                        ins.then_inc(moe.sh_y_added, 1)
                dve.wait_ge(moe.sh_y_added, 4)

                hidden = P if moe is moe0 else H1
                if moe is moe0:
                    steps.wait(v.memset(hT[:], 0.0))

                def product(s, parity):
                    dve.wait_ge(moe.silu_done, s + 1)
                    up = bank[2 + parity][:, 2 * P:4 * P].rearrange("p (u t) -> p u t", u=2)
                    if moe is moe0:
                        for e in range(2):
                            r = slice(e * H0, (e + 1) * H0)
                            ins = v.tensor_tensor(hT[r, parity, :, r], h_silu[r, parity, :, r], up[r, :, r], ALU.mult)
                    else:
                        ins = v.tensor_tensor(hT[0:hidden, parity], h_silu[0:hidden, parity], up[0:hidden], ALU.mult)
                    ins.then_inc(moe.h_ready, 1)

                def copy_y(s, parity, first):
                    dve.wait_ge(moe.y_done, s + 1)
                    if not first:
                        dve.wait_ge(moe.stored[parity], 8 * (s - parity))
                    v.tensor_copy(yb[:, parity].rearrange("p u d -> p (u d)"), bank[4 + parity][:]
                                  ).then_inc(moe.y_copied, 1)

                for s in range(AHEAD):
                    product(s, s % 2)
                    if s:
                        copy_y(s - 1, (s - 1) % 2, s < 3)
                with dve.Fori(1, moe.steps // AHEAD) as m:
                    for k in range(AHEAD):
                        product(m * AHEAD + k, k % 2)
                        copy_y(m * AHEAD + (k - 1), (k - 1) % 2, False)
                copy_y(moe.steps - 1, (moe.steps - 1) % 2, False)

                for a in range(TILES):
                    dve.wait_ge(moe.gathered[a % 2], 16 * TOPK * (a // 2 + 1))
                    for k in range(TOPK):
                        c = k * TILES + a
                        ins = v.scalar_tensor_tensor(xr[:, a, :], yg[:, a % 2, k, :], fw[:, c:c + 1], xr[:, a, :],
                                                     ALU.mult, ALU.add)
                        if k < TOPK - 1:
                            steps.wait(ins)
                    ins.then_inc(moe.combined, 1)
                dve.wait_ge(moe.combined, TILES)

            if stop >= 2:
                feed_forward(moe0, 1)
            if stop >= 3:
                norm(2)
                dve.wait_ge(z_ready, 1)
                x5 = xn[:].rearrange("p (b c) l -> p b c l", c=IC)
                for c in range(IC):
                    ins = v.tensor_tensor(x5[:, :, c, :], y_ssm[:, c, :].rearrange("p (b l) -> p b l", b=BATCH),
                                          x5[:, :, c, :], ALU.mult)
                    steps.mark(ins)
                steps.settle()
                v.memset(tmax[:], 0.0).then_inc(z_gated, 1)
                dve.wait_ge(zT_done, 1)
                for b in range(BATCH):
                    ins = v.tensor_tensor(xr[:, 2 * b:2 * b + 2, :], xr[:, 2 * b:2 * b + 2, :],
                                          bank[b][:].rearrange("p (a d) -> p a d", a=2), ALU.add)
                    steps.mark(ins)
                steps.settle()
                v.memset(tmax[:], 0.0).then_inc(z_added, 1)
                dve.wait_ge(z_added, 1)
            if stop >= 4:
                feed_forward(moe1, 3)


STOP = 9


def kernel(**inputs):
    import numpy as np
    import concourse.bacc as bacc
    from concourse import mybir as mb
    from concourse.bass_utils import run_bass_kernel_spmd

    a = {n: np.asarray(v) for n, v in inputs.items()}

    def down(w):
        return w.reshape(-1, P, w.shape[-1]).transpose(1, 0, 2)

    fold = []
    for g in range(GROUPS):
        parts = [a["L0_xattn_Wq"][:, h * CTX:(h + 1) * CTX].T for h in (PAIR * g, PAIR * g + 1)]
        parts += [a[n][:, g * CTX:(g + 1) * CTX].T for n in ("L0_xattn_Wk", "L0_xattn_Wv")]
        parts += [a["L0_xattn_Wo"][h * CTX:(h + 1) * CTX] for h in (PAIR * g, PAIR * g + 1)]
        fold.append(np.concatenate(parts, 1))
    small = np.concatenate([a["L1_xattn_conv_w"].reshape(INNER, CONV)]
                           + [a[n].reshape(INNER, 1) for n in
                              ("L1_xattn_conv_b", "L1_xattn_dt_proj_b", "L1_xattn_D")]
                           + [a["L1_xattn_A_log"]], 1)
    xproj = a["L1_xattn_x_proj_w"]
    xproj = np.concatenate([xproj[RANK:], xproj[:RANK]], 0)

    def shared(gate, up, out):
        return np.concatenate([down(w).reshape(P, -1) for w in (gate, up, out)], 1)

    s_in = {n: a[n].transpose(1, 0, 2).reshape(D, SHARED) for n in ("L0_ffn_Sg", "L0_ffn_Su")}
    gu = np.stack([a["L0_ffn_Wg"], a["L0_ffn_Wu"]])
    gu = gu.reshape(2, E0 // 4, 2, 2, DC, P, H0).transpose(1, 5, 2, 0, 4, 3, 6)
    wd = a["L0_ffn_Wd"].reshape(E0 // 4, 2, 2 * H0, D).transpose(0, 2, 1, 3)
    experts0 = np.concatenate([gu.reshape(E0 // 4, P, -1), wd.reshape(E0 // 4, P, -1)], 2)
    gu1 = a["L1_ffn_gate_up_proj"].reshape(E1, 2, H1, DC, P).transpose(0, 4, 1, 3, 2)

    arrays = {
        "x": a["x"].reshape(TOKENS, D),
        "ctx": a["ctx_1024"].reshape(TOKENS, CTX),
        "ctxT": a["ctx_1024"].reshape(TOKENS, CTX).T,
        "mask": a["mask_BxS2_bf1"].reshape(1, TOKENS).view(np.uint8),
        "in_w": a["L1_xattn_in_proj_w"].T,
        "small_w": down(small),
        "xproj_w": down(xproj.T),
        "dtproj_w": a["L1_xattn_dt_proj_w"].T,
        "fold_w": np.stack(fold),
        "route0_w": down(a["L0_ffn_Wr"]),
        "route0_bias": a["L0_ffn_router_bias"].reshape(1, E0),
        "route1_w": down(np.concatenate([a["L1_ffn_gate_w"], a["L1_ffn_shared_expert_gate_w"]], 0).T),
        "shared0_w": shared(s_in["L0_ffn_Sg"], s_in["L0_ffn_Su"], a["L0_ffn_Sd"].reshape(SHARED, D)),
        "shared1_w": shared(a["L1_ffn_shared_gate_w"].T, a["L1_ffn_shared_up_w"].T,
                            a["L1_ffn_shared_down_w"].T),
        "experts0_w": experts0,
        "experts1_gu": gu1.reshape(E1, P, -1),
        "experts1_d": a["L1_ffn_down_proj"].transpose(0, 2, 1),
    }
    arrays = {n: np.ascontiguousarray(v) for n, v in arrays.items()}
    nc = bacc.Bacc("TRN2", target_bir_lowering=False, num_devices=1)
    tensors = {n: nc.dram_tensor(f"in_{n}", v.shape, mb.dt.from_np(v.dtype), kind="ExternalInput").ap()
               for n, v in arrays.items()}
    out = nc.dram_tensor("out", (TOKENS, D), mb.dt.float32, kind="ExternalOutput").ap()
    program(nc, tensors, out, STOP)
    r = run_bass_kernel_spmd(nc, [{f"in_{n}": v for n, v in arrays.items()}], core_ids=[0])
    return r.results[0]["out"].reshape(BATCH, SEQ, D)
```

```python
from contextlib import ExitStack

import concourse.bass as bass
from concourse import mybir

F32 = mybir.dt.float32
BF16 = mybir.dt.bfloat16
I32 = mybir.dt.int32
U32 = mybir.dt.uint32
U8 = mybir.dt.uint8
ALU = mybir.AluOpType
ACT = mybir.ActivationFunctionType
AX = mybir.AxisListType.X

P = 128
BATCH = 4
SEQ = 256
TOKENS = BATCH * SEQ
D = 256
DC = D // P
TILES = TOKENS // P
CTX = 128
HEADS = 16
GROUPS = 8
PAIR = HEADS // GROUPS
EPS = 1e-5
MASKED = -1e9

STATE = 16
RANK = 8
CONV = 4
INNER = 256
IC = INNER // P
PAD = 4

TOPK = 4
E0, H0, CAP = 64, 64, 64
E1, H1 = 32, 96
SHARED = 512
SC = SHARED // P
ROWS0 = E0 * CAP
BLOCK = 128
BLOCKS = E1 + (TOKENS * TOPK - E1) // BLOCK
BLOCKS += -BLOCKS % 16
ROWS1 = BLOCKS * BLOCK
STEP = 2 * P
AHEAD = 8
STORES = 4
KT = TOPK * TILES
UNDERFLOW = -104.0
CONSTS = 9
SKIP = float(1 << 20)
NO_ROW = TOPK * TOKENS

FOLDS = 4
PREP_FOLD = 2 * PAIR * D + 2 * CTX
SMALL = CONV + 3 + STATE
ATTN_SCALE = float(CTX) ** -0.5


class Steps:

    def __init__(self, engine, semaphore):
        self.engine, self.semaphore, self.count = engine, semaphore, 0

    def mark(self, instruction):
        instruction.then_inc(self.semaphore, 1)
        self.count += 1
        return self.count

    def wait(self, instruction):
        self.engine.wait_ge(self.semaphore, self.mark(instruction))

    def settle(self):
        self.engine.wait_ge(self.semaphore, self.count)


def program(nc, t, out, stop=9):
    with ExitStack() as ctx:
        def sem(name):
            return ctx.enter_context(nc.semaphore(name))

        def sb(name, shape, dt=F32, stack=ctx):
            return stack.enter_context(nc.sbuf_tensor(name, shape, dt))

        def dram(name, shape, dt=F32):
            return nc.dram_tensor(name, shape, dt).ap()

        bank = [ctx.enter_context(nc.psum_tensor(f"bank{i}", [P, 512], F32)) for i in range(8)]

        bc_dram = dram("bc_dram", (2 * STATE, TOKENS))
        tokens0_dram = dram("tokens0_dram", (TOKENS, D))
        results0_dram = dram("results0_dram", (TOPK * TOKENS, D))
        tokens1_dram = dram("tokens1_dram", (TOKENS, D))
        results1_dram = dram("results1_dram", (TOPK * TOKENS, D))

        xr = sb("xr", [P, TILES, D])
        xn = sb("xn", [P, TILES, D])
        xnT = sb("xnT", [P, DC, TOKENS])
        y_ssm = sb("y_ssm", [P, IC, TOKENS])
        shared_w = sb("shared_w", [P, 3072])
        route_w = sb("route_w", [P, DC, E0])
        route_bias = sb("route_bias", [P, E0])
        route1_w = sb("route1_w", [P, DC, E1 + 1])
        ident = sb("ident", [P, P])
        earlier = sb("earlier", [P, P], BF16)
        ones_bf = sb("ones_bf", [P, P], BF16)
        zeros = sb("zeros", [P, D])
        iota_e = sb("iota_e", [P, E0])
        iota_blk = sb("iota_blk", [P, TILES])
        iota_j = sb("iota_j", [P, BLOCKS])
        iota_p = sb("iota_p", [P, P])
        row_high = sb("row_high", [P, KT])
        row_low = sb("row_low", [P, 1])
        stats = sb("stats", [P, TILES, 6])
        moments = sb("moments", [P, TILES, 2])
        rstd = sb("rstd", [P, TILES])
        eps_col = sb("eps_col", [P, 1])
        pace = sb("pace", [P, 1])

        phase1 = ctx.enter_context(ExitStack())
        ctxT = sb("ctxT", [P, TOKENS], stack=phase1)
        ctxN = sb("ctxN", [P, TILES, CTX], stack=phase1)
        ctxN_cur = sb("ctxN_cur", [P, 2, CTX], stack=phase1)
        mask_u8 = sb("mask_u8", [P, BATCH, SEQ], U8, stack=phase1)
        mask_all = sb("mask_all", [P, BATCH, SEQ + 1], stack=phase1)
        mask_cur = sb("mask_cur", [P, SEQ + 1], stack=phase1)
        qk_w = sb("qk_w", [P, GROUPS, PAIR, DC, CTX], stack=phase1)
        vo_w = sb("vo_w", [P, GROUPS, PAIR, D], stack=phase1)
        in_w = sb("in_w", [P, INNER], stack=phase1)
        xproj_w = sb("xproj_w", [P, IC, 2 * STATE + RANK], stack=phase1)
        dtproj_w = sb("dtproj_w", [2 * STATE + RANK, INNER], stack=phase1)
        small_w = sb("small_w", [P, IC, SMALL], stack=phase1)
        a_neg = sb("a_neg", [P, IC, STATE], stack=phase1)
        xpad = sb("xpad", [P, IC, BATCH, PAD + SEQ], stack=phase1)
        u_in = sb("u_in", [P, IC, TOKENS], stack=phase1)
        dt_sb = sb("dt_sb", [P, IC, TOKENS], stack=phase1)
        du_sb = sb("du_sb", [P, IC, TOKENS], stack=phase1)
        xdbl = sb("xdbl", [2 * STATE + RANK, TOKENS], stack=phase1)
        decay = sb("decay", [P, 2, TOKENS], stack=phase1)
        drive = sb("drive", [P, 2, TOKENS], stack=phase1)
        state = sb("state", [P, TOKENS], stack=phase1)
        rowmax = sb("rowmax", [P, 2, 4], stack=phase1)
        negmax = sb("negmax", [P, 2, 4], stack=phase1)
        rowsum = sb("rowsum", [P, 2, 4], stack=phase1)
        rowinv = sb("rowinv", [P, 2, 4], stack=phase1)
        with ExitStack() as before_attention:
            fold_w = sb("fold_w", [P, FOLDS, PREP_FOLD], stack=before_attention)
        b_bc = sb("b_bc", [P, 2, TOKENS], stack=phase1)
        c_bc = sb("c_bc", [P, 2, TOKENS], stack=phase1)
        qT = sb("qT", [P, 2, PAIR * SEQ], stack=phase1)
        probs = sb("probs", [P, 2, 4, SEQ], stack=phase1)
        probsT = sb("probsT", [P, 2, 2, PAIR * SEQ], stack=phase1)
        attT = sb("attT", [P, 2, PAIR * SEQ], stack=phase1)
        phase1.close()

        hshT = sb("hshT", [P, SC, TOKENS])
        sh_silu = sb("sh_silu", [P, 2, 512])
        sh_up = sb("sh_up", [P, 2, 512])
        logits = sb("logits", [P, TILES, E0])
        expl = sb("expl", [P, TILES, E0])
        tmax = sb("tmax", [P, TILES])
        top_v = sb("top_v", [P, TILES, 8])
        top_i = sb("top_i", [P, TILES, 8], U32)
        top_e = sb("top_e", [P, TILES, 8])
        zsum = sb("zsum", [P, TILES])
        psum4 = sb("psum4", [P, TILES])
        wts = sb("wts", [P, TOPK, TILES])
        idxf = sb("idxf", [P, TOPK, TILES])
        onehot = sb("onehot", [P, KT, E0])
        prod = sb("prod", [P, KT, E0])
        chosen = sb("chosen", [P, TILES * E0], BF16)
        cum = sb("cum", [P, TILES, E0])
        pos = sb("pos", [P, KT])
        over = sb("over", [P, KT])
        slot = sb("slot", [P, KT])
        slot_i = sb("slot_i", [P, KT], I32)
        part_i = sb("part_i", [P, 2, KT], I32)
        part_f = sb("part_f", [P, 2, KT])
        place_hot = sb("place_hot", [P, KT, P], BF16)
        block_hot = sb("block_hot", [P, KT, BLOCKS], BF16)
        block_rows = sb("block_rows", [P, KT, 2, BLOCKS], BF16)
        row_f = sb("row_f", [P, BLOCKS])
        row_put = sb("row_put", [P, BLOCKS], I32)
        row_get = sb("row_get", [P, BLOCKS], I32)
        counts = sb("counts", [P, E1])
        above = sb("above", [P, E1, TILES])
        nblk = sb("nblk", [P, E1])
        blk_end = sb("blk_end", [P, E1])
        first_slot = sb("first_slot", [P, E1])
        ones_row = sb("ones_row", [P, E1])
        behind = prod[0:1].rearrange("p a e -> p (a e)")[:, 0:BLOCKS * E1].rearrange("p (j e) -> p j e", e=E1)
        blk_ef = sb("blk_ef", [1, BLOCKS])
        blk_e = sb("blk_e", [1, BLOCKS], I32)
        sgate = sb("sgate", [P, TILES])
        xb = sb("xb", [P, AHEAD, 2, D])
        ew = sb("ew", [P, AHEAD, 1536])
        xbT = sb("xbT", [P, 2, DC, STEP])
        h_silu = sb("h_silu", [P, 2, 2, P])
        hT = sb("hT", [P, 2, 2, P])
        yb = sb("yb", [P, STORES, 2, D])
        yg = hshT[:].rearrange("p j t -> p (j t)").rearrange("p (n k d) -> p n k d", n=4, k=TOPK)

        ld_x, ld_ctx, ld_mask, ld_ssm, ld_route = (sem(f"ld_{n}") for n in ("x", "ctx", "mask", "ssm", "route"))
        ld_fold = [sem(f"ld_fold_{k}") for k in range(FOLDS)]
        ld_shared, ld_shared1 = sem("ld_shared"), sem("ld_shared1")
        zero_filled = sem("zero_filled")
        consts_set, zeros_set = sem("consts_set"), sem("zeros_set")
        dve_step, act_step, pool_step = sem("dve_step"), sem("act_step"), sem("pool_step")
        ln_var, ln_std, ln_out, lnT_done, lnT_copied = (
            sem(f"ln_{n}") for n in ("var", "std", "out", "transposed", "copied"))
        du_ready = sem("du_ready")
        fold_done, fold_copied, dt_copied = sem("fold_done"), sem("fold_copied"), sem("dt_copied")
        xin_done, xin_copied, conv_done, u_ready, xdbl_done, xdbl_copied, bc_stored = (
            sem(n) for n in ("xin_done", "xin_copied", "conv_done", "u_ready", "xdbl_done",
                             "xdbl_copied", "bc_stored"))
        dt_done, sp_neg, sp_exp, sp_one, sp_ln, a_exp, a_ready, dt_ready = (
            sem(n) for n in ("dt_done", "sp_neg", "sp_exp", "sp_one", "sp_ln", "a_exp", "a_ready",
                             "dt_ready"))
        bc_loaded = [sem("bc_loaded_even"), sem("bc_loaded_odd")]
        decay_free, decay_set, drive_set, product_set, y_added = (
            sem(n) for n in ("decay_free", "decay_set", "drive_set", "product_set", "y_added"))
        scan_done = sem("scan_done")
        mask_set, ctx_set, inv_made = sem("mask_set"), sem("ctx_set"), sem("inv_made")
        q_done, q_copied, s_done, s_masked, max_ready, exp_done, inv_ready, p_ready = (
            sem(n) for n in ("q_done", "q_copied", "s_done", "s_masked", "max_ready", "exp_done",
                             "inv_ready", "p_ready"))
        t_done, pt_copied, pv_done, u_copied, o_done, o_taken = (
            sem(n) for n in ("t_done", "pt_copied", "pv_done", "u_copied", "o_done", "o_taken"))
        z_ready, z_gated, zT_done, z_added = (sem(n) for n in ("z_ready", "z_gated", "zT_done", "z_added"))
        out_stored = sem("out_stored")

        class Moe:

            def __init__(self, n, experts, rows, tokens, results):
                self.experts, self.blocks, self.steps = experts, rows // P, rows // STEP
                self.tokens, self.results = tokens, results
                self.logits_done = sem(f"logits_done{n}")
                self.key_ready = sem(f"key_ready{n}")
                self.exp_ready = sem(f"exp_ready{n}")
                self.chosen_ready = sem(f"chosen_ready{n}")
                self.cum_done = sem(f"cum_done{n}")
                self.cum_copied = sem(f"cum_copied{n}")
                self.tokens_stored = sem(f"tokens_stored{n}")
                self.places_ready = sem(f"places_ready{n}")
                self.rows_done = sem(f"rows_done{n}")
                self.rows_ready = sem(f"rows_ready{n}")
                self.sh_gu_done = sem(f"sh_gu_done{n}")
                self.sh_silu_done = sem(f"sh_silu_done{n}")
                self.sh_h_ready = sem(f"sh_h_ready{n}")
                self.sh_y_done = sem(f"sh_y_done{n}")
                self.sh_y_added = sem(f"sh_y_added{n}")
                self.xt_done = sem(f"xt_done{n}")
                self.xt_copied = sem(f"xt_copied{n}")
                self.gu_done = sem(f"gu_done{n}")
                self.silu_done = sem(f"silu_done{n}")
                self.h_ready = sem(f"h_ready{n}")
                self.y_done = sem(f"y_done{n}")
                self.y_copied = sem(f"y_copied{n}")
                self.blocks_ready = sem(f"blocks_ready{n}")
                self.before = 0 if n == 0 else ROWS0 // STEP
                self.combined = sem(f"combined{n}")

        tokens_loaded = [sem(f"tokens_loaded_{k}") for k in range(AHEAD)]
        weights_loaded = [sem(f"weights_loaded_{k}") for k in range(AHEAD)]
        y_stored = [sem(f"y_stored_{k}") for k in range(STORES)]
        results_loaded = [sem(f"results_loaded_{k}") for k in range(4)]

        moe0 = Moe(0, E0, ROWS0, tokens0_dram, results0_dram)
        moe1 = Moe(1, E1, ROWS1, tokens1_dram, results1_dram)

        def dst_tokens(ap):
            return ap.rearrange("(a p) d -> p a d", p=P)

        block = ctx.enter_context(nc.Block())

        @block.sync
        def _(sp):
            sp.dma_start(xr[:], dst_tokens(t["x"])).then_inc(ld_x, 16)
            sp.dma_start(ctxT[:], t["ctxT"]).then_inc(ld_ctx, 16)
            sp.dma_start(in_w[:], t["in_w"]).then_inc(ld_ssm, 16)
            sp.dma_start(small_w[:], t["small_w"]).then_inc(ld_ssm, 16)
            sp.dma_start(xproj_w[:], t["xproj_w"]).then_inc(ld_ssm, 16)
            sp.dma_start(dtproj_w[2 * STATE:, :], t["dtproj_w"]).then_inc(ld_ssm, 16)
            sp.dma_start(mask_u8[:].rearrange("p b s -> p (b s)"),
                         t["mask"].broadcast_to([P, TOKENS])).then_inc(ld_mask, 16)

            for g in range(FOLDS):
                sp.dma_start(fold_w[:, g, :], t["fold_w"][g]).then_inc(ld_fold[g], 16)
            with sp.Fori(0, GROUPS // FOLDS - 1) as m:
                for g in range(FOLDS):
                    sp.wait_ge(fold_done, FOLDS * m + (g + 1))
                    sp.dma_start(fold_w[:, g, :], t["fold_w"][bass.ds(FOLDS * m + (g + FOLDS), 1)]
                                 .rearrange("a p f -> (a p) f")).then_inc(ld_fold[g], 16)
            sp.dma_start(ctxN[:], dst_tokens(t["ctx"])).then_inc(ld_ctx, 16)

            sp.dma_start(shared_w[:], t["shared0_w"]).then_inc(ld_shared, 16)
            sp.dma_start(route_w[:], t["route0_w"]).then_inc(ld_route, 16)
            sp.dma_start(route_bias[:], t["route0_bias"].broadcast_to([P, E0])).then_inc(ld_route, 16)
            sp.dma_start(route1_w[:], t["route1_w"]).then_inc(ld_route, 16)

            sp.wait_ge(xdbl_copied, 2)
            sp.dma_start(bc_dram, xdbl[0:2 * STATE, :]).then_inc(bc_stored, 16)
            sp.wait_ge(bc_stored, 16)

            def spread(n, parity):
                for row, dst in ((n, b_bc), (n + STATE, c_bc)):
                    sp.dma_start(dst[:, parity, :], bc_dram[bass.ds(row, 1), :].broadcast_to([P, TOKENS])
                                 ).then_inc(bc_loaded[parity], 16)

            for n in range(2):
                spread(n, n)
            sp.wait_ge(zeros_set, 1)
            for r in range(0, TOPK * TOKENS, 2048):
                sp.dma_start(dst_tokens(results0_dram[r:r + 2048, :]),
                             zeros[:].unsqueeze(1).broadcast_to([P, 2048 // P, D])).then_inc(zero_filled, 16)
            with sp.Fori(0, STATE // 2 - 1) as m:
                for n in range(2):
                    sp.wait_ge(y_added, 4 * m + (2 * n + 3))
                    spread(2 * m + (n + 2), n)

            def expert_loads(moe, load_weights, n):
                sp.wait_ge(ln_out, TILES * (n + 1))
                sp.dma_start(dst_tokens(moe.tokens), xn[:]).then_inc(moe.tokens_stored, 16)
                if moe is moe1:
                    sp.wait_ge(moe.blocks_ready, 1)
                for k in range(AHEAD):
                    load_weights(k, k)
                with sp.Fori(1, moe.steps // AHEAD) as m:
                    for k in range(AHEAD):
                        s = m * AHEAD + k
                        sp.wait_ge(moe.y_done, s - (AHEAD - 1))
                        load_weights(s, k)

            def result_loads(moe):
                for k in range(STORES):
                    sp.wait_ge(y_stored[k], 32 * ((moe.before + moe.steps) // STORES))
                by_choice = moe.results.rearrange("(k a p) d -> p k a d", p=P, a=TILES)
                for a in range(TILES):
                    if a >= 4:
                        sp.wait_ge(moe.combined, a - 3)
                    sp.dma_start(yg[:, a % 4], by_choice[:, :, a, :]).then_inc(results_loaded[a % 4], 16)

            def weights0(s, k):
                sp.dma_start(ew[:, k, :], t["experts0_w"][bass.ds(s, 1)].rearrange("a p f -> (a p) f")
                             ).then_inc(weights_loaded[k], 16)

            def weights1(s, k):
                for j in range(2):
                    e = sp.value_load(blk_e[0:1, bass.ds(s * 2 + j, 1)], min_val=0, max_val=E1 - 1)
                    sp.dma_start(ew[:, k, j * 384:(j + 1) * 384],
                                 t["experts1_gu"][bass.ds(e, 1)].rearrange("a p f -> (a p) f")
                                 ).then_inc(weights_loaded[k], 16)
                    sp.dma_start(ew[0:H1, k, 768 + j * D:768 + (j + 1) * D],
                                 t["experts1_d"][bass.ds(e, 1)].rearrange("a p f -> (a p) f")
                                 ).then_inc(weights_loaded[k], 16)

            if stop >= 2:
                expert_loads(moe0, weights0, 1)
                sp.wait_ge(moe0.sh_y_done, 4)
                sp.dma_start(shared_w[:], t["shared1_w"]).then_inc(ld_shared1, 16)
                result_loads(moe0)
            if stop >= 4:
                expert_loads(moe1, weights1, 3)
                result_loads(moe1)
            if stop == 1:
                sp.wait_ge(o_taken, BATCH + 1)
            elif stop == 3:
                sp.wait_ge(z_added, 1)
            else:
                sp.wait_ge((moe0 if stop == 2 else moe1).combined, TILES)
            sp.dma_start(dst_tokens(out), xr[:]).then_inc(out_stored, 16)
            sp.wait_ge(out_stored, 16)

        @block.gpsimd
        def _(pool):
            steps = Steps(pool, pool_step)
            steps.mark(nc.gpsimd.memset(zeros[:], 0.0))
            steps.mark(nc.gpsimd.memset(ident[:], 0.0))
            steps.mark(nc.gpsimd.memset(ones_bf[:], 1.0))
            steps.wait(nc.gpsimd.memset(earlier[:], 1.0))
            nc.gpsimd.affine_select(out=ident[:], in_=ident[:], compare_op=ALU.not_equal, fill=1.0, base=0,
                                    pattern=[[-1, P]], channel_multiplier=1).then_inc(consts_set, 1)
            nc.gpsimd.affine_select(out=earlier[:], in_=earlier[:], compare_op=ALU.is_gt, fill=0.0, base=0,
                                    pattern=[[1, P]], channel_multiplier=-1).then_inc(consts_set, 1)
            nc.gpsimd.iota(iota_e[:], pattern=[[1, E0]], base=0, channel_multiplier=0,
                           allow_small_or_imprecise_dtypes=True).then_inc(consts_set, 1)
            nc.gpsimd.iota(iota_blk[:], pattern=[[BLOCK, TILES]], base=0, channel_multiplier=0,
                           allow_small_or_imprecise_dtypes=True).then_inc(consts_set, 1)
            nc.gpsimd.iota(iota_j[:], pattern=[[1, BLOCKS]], base=0, channel_multiplier=0,
                           allow_small_or_imprecise_dtypes=True).then_inc(consts_set, 1)
            nc.gpsimd.iota(iota_p[:], pattern=[[1, P]], base=0, channel_multiplier=0,
                           allow_small_or_imprecise_dtypes=True).then_inc(consts_set, 1)
            nc.gpsimd.iota(row_high[:], pattern=[[1, KT]], base=-KT, channel_multiplier=0,
                           allow_small_or_imprecise_dtypes=True).then_inc(consts_set, 1)
            nc.gpsimd.iota(row_low[:], pattern=[[0, 1]], base=0, channel_multiplier=1,
                           allow_small_or_imprecise_dtypes=True).then_inc(consts_set, 1)
            nc.gpsimd.memset(eps_col[:], EPS).then_inc(consts_set, 1)
            nc.gpsimd.memset(zeros[:], 0.0).then_inc(zeros_set, 1)

            pool.wait_ge(mask_set, 1)
            pool.wait_ge(ld_ctx, 32)
            nc.gpsimd.tensor_copy(mask_cur[:], mask_all[:, 0, :]).then_inc(mask_set, 1)
            nc.gpsimd.tensor_copy(ctxN_cur[:], ctxN[:, 0:2, :]).then_inc(ctx_set, 1)
            mask_flat = mask_all[:].rearrange("p b s -> p (b s)")
            ctx_flat = ctxN[:].rearrange("p a d -> p (a d)")

            def mixer_drive(i, b, hp):
                k, c = hp // 2, hp % 2
                pool.wait_ge(bc_loaded[k % 2], b * (32 * STATE // BATCH // 2) + 32 * (k // 2 + 1))
                pool.wait_ge(decay_free, i + 1)
                nc.gpsimd.tensor_tensor(drive[:, hp % 2, :], du_sb[:, c, :], b_bc[:, k % 2, :], ALU.mult
                                        ).then_inc(drive_set, 1)

            pool.wait_ge(du_ready, 1)
            with pool.Fori(0, BATCH - 1) as b:
                for hp in range(GROUPS):
                    mixer_drive(b * GROUPS + hp, b, hp)
                pool.wait_ge(inv_ready, 8 * b + 8)
                nc.gpsimd.tensor_copy(mask_cur[:], mask_flat[:, bass.ds((b + 1) * (SEQ + 1), SEQ + 1)]
                                      ).then_inc(mask_set, 1)
                pool.wait_ge(pv_done, 8 * b + 8)
                nc.gpsimd.tensor_copy(ctxN_cur[:].rearrange("p a d -> p (a d)"),
                                      ctx_flat[:, bass.ds((b + 1) * 2 * CTX, 2 * CTX)]).then_inc(ctx_set, 1)
            for hp in range(GROUPS):
                mixer_drive((BATCH - 1) * GROUPS + hp, BATCH - 1, hp)

            def shared_h(moe):
                for k in range(2 * SC):
                    pool.wait_ge(moe.sh_silu_done, k + 1)
                    nc.gpsimd.tensor_tensor(hshT[:, k // 2, k % 2 * 512:(k % 2 + 1) * 512], sh_silu[:, k % 2, :],
                                            sh_up[:, k % 2, :], ALU.mult).then_inc(moe.sh_h_ready, 1)

            def expert_tokens(moe):
                def load(s):
                    for u in range(2):
                        nc.gpsimd.indirect_dma_start(
                            out=xb[:, s % AHEAD, u, :], out_offset=None, in_=moe.tokens,
                            in_offset=bass.IndirectOffsetOnAxis(ap=row_get[:, 2 * s + u:2 * s + u + 1], axis=0),
                            bounds_check=TOKENS - 1, oob_is_err=False).then_inc(tokens_loaded[s % AHEAD], 16)

                def store(s):
                    pool.wait_ge(moe.y_copied, s + 1)
                    for u in range(2):
                        nc.gpsimd.indirect_dma_start(
                            out=moe.results,
                            out_offset=bass.IndirectOffsetOnAxis(ap=row_put[:, 2 * s + u:2 * s + u + 1], axis=0),
                            in_=yb[:, s % STORES, u, :], in_offset=None,
                            bounds_check=TOPK * TOKENS - 1, oob_is_err=False).then_inc(y_stored[s % STORES], 16)

                pool.wait_ge(moe.tokens_stored, 16)
                pool.wait_ge(moe.rows_ready, 1)
                for s in range(AHEAD):
                    load(s)
                if moe is moe0:
                    pool.wait_ge(zero_filled, 16 * (TOPK * TOKENS // 2048))
                for s in range(AHEAD, moe.steps):
                    pool.wait_ge(moe.xt_done, s - AHEAD + 1)
                    load(s)
                    store(s - AHEAD)
                for s in range(moe.steps - AHEAD, moe.steps):
                    store(s)

            if stop >= 2:
                shared_h(moe0)
                expert_tokens(moe0)
            if stop >= 4:
                shared_h(moe1)
                expert_tokens(moe1)

        @block.tensor
        def _(pe):
            pe.sem_inc(t_done, 1)
            mm = nc.tensor.matmul

            pe.wait_ge(ld_ctx, 16)
            pe.wait_ge(ld_ssm, 64)
            for c in range(IC):
                for h in range(2):
                    mm(bank[4 + 2 * c + h][:], in_w[:, c * P:(c + 1) * P], ctxT[:, h * 512:(h + 1) * 512],
                       start=True, stop=True).then_inc(xin_done, 1)

            def turn_norm(n):
                for c in range(DC):
                    for h in range(2):
                        if n == 0:
                            pe.wait_ge(consts_set, CONSTS)
                            pe.wait_ge(fold_copied, GROUPS + c - 1)
                        for a in range(4):
                            tile = 4 * h + a
                            pe.wait_ge(ln_out, TILES * n + tile + 1)
                            ins = nc.tensor.transpose(bank[4 + 2 * c + h][:, a * P:(a + 1) * P],
                                                      xn[:, tile, c * P:(c + 1) * P], ident[:])
                        ins.then_inc(lnT_done, 1)

            def fold(m, buf, first):
                pe.wait_ge(ld_fold[buf], 16 * m + 16)
                if first:
                    if buf >= 2:
                        pe.wait_ge(xin_copied, 4)
                else:
                    pe.wait_ge(fold_copied, FOLDS * m + (buf + 1 - FOLDS))
                w = fold_w[:, buf, :]
                wq, wk = w[:, 0:PAIR * D], w[:, PAIR * D:PAIR * D + CTX]
                wv, wo = w[:, PAIR * D + CTX:PAIR * D + 2 * CTX], w[:, PAIR * D + 2 * CTX:]
                for j in range(PAIR):
                    for c in range(DC):
                        mm(bank[2 * buf][:, (j * DC + c) * CTX:(j * DC + c + 1) * CTX],
                           wq[:, j * D + c * P:j * D + (c + 1) * P], wk, start=True, stop=True)
                for j in range(PAIR):
                    ins = mm(bank[2 * buf + 1][:, j * D:(j + 1) * D], wv, wo[:, j * D:(j + 1) * D],
                             start=True, stop=True)
                ins.then_inc(fold_done, 1)

            for g in range(FOLDS):
                fold(0, g, True)
            with pe.Fori(1, GROUPS // FOLDS) as m:
                for g in range(FOLDS):
                    fold(m, g, False)

            pe.wait_ge(u_ready, 2)
            pe.wait_ge(fold_copied, GROUPS)
            for h in range(2):
                for c in range(IC):
                    ins = mm(bank[h][0:2 * STATE + RANK, :], xproj_w[:, c, :], u_in[:, c, h * 512:(h + 1) * 512],
                             start=(c == 0), stop=(c == IC - 1))
                ins.then_inc(xdbl_done, 1)
            turn_norm(0)
            for c in range(IC):
                for h in range(2):
                    pe.wait_ge(xdbl_copied, h + 1)
                    mm(bank[2 * c + h][:], dtproj_w[2 * STATE:, c * P:(c + 1) * P],
                       xdbl[2 * STATE:, h * 512:(h + 1) * 512], start=True, stop=True).then_inc(dt_done, 1)

            def queries(i, b, hp):
                for j in range(PAIR):
                    for c in range(DC):
                        ins = mm(bank[0][:, j * SEQ:(j + 1) * SEQ], qk_w[:, hp, j, c, :],
                                 xnT[:, c, bass.ds(b * SEQ, SEQ)], start=(c == 0), stop=(c == DC - 1))
                ins.then_inc(q_done, 1)

            def scores(i, b, hp):
                for j in range(4):
                    ins = mm(bank[1 + j // 2][:, j % 2 * SEQ:(j % 2 + 1) * SEQ],
                             qT[:, hp % 2, j * P:(j + 1) * P], ctxT[:, bass.ds(b * SEQ, SEQ)],
                             start=True, stop=True)
                ins.then_inc(s_done, 1)

            def output(i, hp):
                for j in range(PAIR):
                    for a in range(2):
                        ins = mm(bank[6][:, a * D:(a + 1) * D], attT[:, hp % 2, (2 * j + a) * P:(2 * j + a + 1) * P],
                                 vo_w[:, hp, j, :], start=(hp == 0 and j == 0 and a == 0),
                                 stop=(hp == GROUPS - 1 and j == PAIR - 1), skip_group_check=True)
                return ins

            def attention(b, last):
                for hp in range(GROUPS):
                    i = b * GROUPS + hp
                    more = not (last and hp == GROUPS - 1)
                    if more:
                        pe.wait_ge(q_copied, i + 2)
                        pe.wait_ge(s_masked, i + 1)
                        nb = b + (hp + 1) // GROUPS
                        scores(i + 1, nb, (hp + 1) % GROUPS)
                    pe.wait_ge(p_ready, i + 1)
                    pe.wait_ge(pt_copied, i + 1)
                    for s in range(2):
                        for j in range(4):
                            ins = nc.tensor.transpose(bank[3 + s][:, j * P:(j + 1) * P],
                                                      probs[:, hp % 2, j, s * P:(s + 1) * P], ident[:])
                    ins.then_inc(t_done, 1)
                    if not (last and hp >= GROUPS - 2):
                        pe.wait_ge(q_copied, i + 2)
                        queries(i + 2, b + (hp + 2) // GROUPS, (hp + 2) % GROUPS)
                    if hp == 0:
                        pe.wait_ge(ctx_set, b + 1)
                    pe.wait_ge(pt_copied, i + 2)
                    pe.wait_ge(u_copied, i + 1)
                    for s in range(2):
                        ins = mm(bank[5][:], ctxN_cur[:, s, :], probsT[:, hp % 2, s, :],
                                 start=(s == 0), stop=(s == 1))
                    ins.then_inc(pv_done, 1)
                    if hp == 1:
                        pe.wait_ge(o_taken, b + 1)
                    if hp > 0:
                        pe.wait_ge(u_copied, i + 1)
                        output(i - 1, hp - 1)
                pe.wait_ge(u_copied, b * GROUPS + GROUPS + 1)
                output(i, GROUPS - 1).then_inc(o_done, 1)

            pe.wait_ge(lnT_copied, 4)
            pe.wait_ge(dt_copied, 4)
            queries(0, 0, 0)
            pe.wait_ge(q_copied, 1)
            queries(1, 0, 1)
            scores(0, 0, 0)
            with pe.Fori(0, BATCH - 1) as b:
                attention(b, False)
            attention(BATCH - 1, True)

            def route(moe):
                w, n = (route_w, E0) if moe is moe0 else (route1_w, E1 + 1)
                pe.wait_ge(ld_route, 48)
                for a in range(TILES):
                    for c in range(DC):
                        ins = mm(bank[0][:, a * n:(a + 1) * n], xnT[:, c, a * P:(a + 1) * P], w[:, c, :],
                                 start=(c == 0), stop=(c == DC - 1))
                ins.then_inc(moe.logits_done, 1)

            def count(moe):
                n = moe.experts
                pe.wait_ge(moe.chosen_ready, 1)
                for a in range(TILES):
                    for b in range(a + 1):
                        ins = mm(bank[1][:, a * n:(a + 1) * n], (earlier if b == a else ones_bf)[:],
                                 chosen[:, b * n:(b + 1) * n], start=(b == 0), stop=(b == a))
                if moe is moe1:
                    for b in range(TILES):
                        ins = mm(bank[2][:, 0:n], ones_bf[:], chosen[:, b * n:(b + 1) * n],
                                 start=(b == 0), stop=(b == TILES - 1))
                ins.then_inc(moe.cum_done, 1)

            def shared(moe, k):
                j, h = k // 2, k % 2
                if k >= 2:
                    pe.wait_ge(moe.sh_silu_done, k - 1)
                for w, first in ((0, 4), (1, 6)):
                    for c in range(DC):
                        ins = mm(bank[first + h][:], shared_w[:, w * 1024 + c * SHARED + j * P:
                                                              w * 1024 + c * SHARED + (j + 1) * P],
                                 xnT[:, c, h * 512:(h + 1) * 512], start=(c == 0), stop=(c == DC - 1))
                ins.then_inc(moe.sh_gu_done, 1)

            def shared_out(moe):
                pe.wait_ge(moe.sh_h_ready, 2 * SC)
                for a in range(TILES):
                    for j in range(SC):
                        ins = mm(bank[4 + a // 2][:, a % 2 * D:(a % 2 + 1) * D], hshT[:, j, a * P:(a + 1) * P],
                                 shared_w[:, 2048 + j * D:2048 + (j + 1) * D], start=(j == 0), stop=(j == SC - 1))
                    if a % 2:
                        ins.then_inc(moe.sh_y_done, 1)

            def rows_of_slots(moe):
                pe.wait_ge(moe.places_ready, 3)
                n = moe.blocks
                for c in range(KT):
                    ins = mm(bank[3][:, 0:2 * n], place_hot[:, c, :], block_rows[:, c, :, 0:n],
                             start=(c == 0), stop=(c == KT - 1))
                ins.then_inc(moe.rows_done, 1)

            def experts(moe):
                hidden = P if moe is moe0 else H1
                weights_each = 16 if moe is moe0 else 64

                def turn(s, m, k, first):
                    pe.wait_ge(tokens_loaded[k], 32 * m + (32 + 32 * moe.before // AHEAD))
                    if not first:
                        pe.wait_ge(moe.xt_copied, s - 1)
                    for c in range(DC):
                        for u in range(2):
                            ins = nc.tensor.transpose(bank[k % 2][:, (c * 2 + u) * P:(c * 2 + u + 1) * P],
                                                      xb[:, k, u, c * P:(c + 1) * P], ident[:])
                    ins.then_inc(moe.xt_done, 1)

                def gate_up(s, m, k, first):
                    parity = k % 2
                    pe.wait_ge(weights_loaded[k], weights_each * m + (weights_each + 16 * moe.before // AHEAD))
                    pe.wait_ge(moe.xt_copied, s + 1)
                    if not first:
                        pe.wait_ge(moe.h_ready, s - 1)
                    for u in range(2):
                        for w in range(2):
                            for c in range(DC):
                                o = ((u * 2 + w) * DC + c) * hidden
                                ins = mm(bank[2 + parity][0:hidden, (w * 2 + u) * P:(w * 2 + u + 1) * P],
                                         ew[:, k, o:o + hidden], xbT[:, parity, c, u * P:(u + 1) * P],
                                         start=(c == 0), stop=(c == DC - 1))
                    ins.then_inc(moe.gu_done, 1)

                def down(s, k, first):
                    parity = k % 2
                    pe.wait_ge(moe.h_ready, s + 1)
                    if not first:
                        pe.wait_ge(moe.y_copied, s - 1)
                    o = 4 * DC * hidden
                    for u in range(2):
                        ins = mm(bank[4 + parity][:, u * D:(u + 1) * D], hT[0:hidden, parity, u, :],
                                 ew[0:hidden, k, o + u * D:o + (u + 1) * D], start=True, stop=True)
                    ins.then_inc(moe.y_done, 1)

                def steps(m, first, last):
                    for k in range(AHEAD):
                        s = m * AHEAD + k
                        if not (last and k == AHEAD - 1):
                            turn(s + 1, m + (k + 1) // AHEAD, (k + 1) % AHEAD, first and k == 0)
                        gate_up(s, m, k, first and k < 2)
                        if not (first and k == 0):
                            down(s - 1, (k - 1) % AHEAD, first and k < 3)

                pe.wait_ge(moe.sh_y_added, 4)
                pe.wait_ge(moe.rows_ready, 1)
                turn(0, 0, 0, True)
                steps(0, True, False)
                if moe.steps // AHEAD > 2:
                    with pe.Fori(1, moe.steps // AHEAD - 1) as m:
                        steps(m, False, False)
                steps(moe.steps // AHEAD - 1, False, True)
                down(moe.steps - 1, AHEAD - 1, False)

            def feed_forward(moe, n):
                turn_norm(n)
                pe.wait_ge(lnT_copied, 4 * min(n, 2) + 4)
                route(moe)
                if moe is moe1:
                    pe.wait_ge(ld_shared1, 16)
                else:
                    pe.wait_ge(ld_shared, 16)
                for k in range(2 * SC):
                    shared(moe, k)
                    if k == 2:
                        count(moe)
                rows_of_slots(moe)
                shared_out(moe)
                experts(moe)

            if stop >= 2:
                feed_forward(moe0, 1)
            if stop >= 3:
                pe.wait_ge(z_gated, 1)
                for b in range(BATCH):
                    for lc in range(2):
                        for c in range(IC):
                            ins = nc.tensor.transpose(bank[b][:, lc * D + c * P:lc * D + (c + 1) * P],
                                                      xn[:, 2 * b + c, lc * P:(lc + 1) * P], ident[:])
                ins.then_inc(zT_done, 1)
            if stop >= 4:
                feed_forward(moe1, 3)

        @block.scalar
        def _(act):
            steps = Steps(act, act_step)
            act.sem_inc(pt_copied, 1)
            act.sem_inc(u_copied, 1)

            def run(out_, in_, func, **kw):
                return nc.scalar.activation(out_, in_, func, **kw)

            def norm_std(n):
                act.wait_ge(ln_var, n + 1)
                if n == 0:
                    act.wait_ge(consts_set, CONSTS)
                run(rstd[:], moments[:, :, 1], ACT.Sqrt, bias=eps_col[:]).then_inc(ln_std, 1)

            def norm_copy(n):
                turned = 4 * min(n, 2)
                for c in range(DC):
                    for h in range(2):
                        act.wait_ge(lnT_done, turned + 2 * c + h + 1)
                        run(xnT[:, c, h * 512:(h + 1) * 512], bank[4 + 2 * c + h][:], ACT.Copy
                            ).then_inc(lnT_copied, 1)

            norm_std(0)
            act.wait_ge(ld_ssm, 64)
            run(a_neg[:], small_w[:, :, CONV + 3:], ACT.Exp).then_inc(a_exp, 1)

            qk_flat = qk_w[:].rearrange("p g j c d -> p (g j c d)")

            vo_flat = vo_w[:].rearrange("p g j d -> p (g j d)")
            with act.Fori(0, GROUPS // FOLDS) as m:
                for k in range(FOLDS):
                    g = FOLDS * m + k
                    act.wait_ge(fold_done, g + 1)
                    run(qk_flat[:, bass.ds(g * 512, 512)], bank[2 * k][:], ACT.Copy)
                    run(vo_flat[:, bass.ds(g * 512, 512)], bank[2 * k + 1][:], ACT.Copy).then_inc(fold_copied, 1)
            for c in range(IC):
                act.wait_ge(conv_done, c + 1)
                run(u_in[:, c, :], u_in[:, c, :], ACT.Silu, bias=small_w[:, c, CONV:CONV + 1]).then_inc(u_ready, 1)
            norm_copy(0)
            for c in range(IC):
                for h in range(2):
                    act.wait_ge(dt_done, 2 * c + h + 1)
                    run(dt_sb[:, c, h * 512:(h + 1) * 512], bank[2 * c + h][:], ACT.Identity,
                        bias=small_w[:, c, CONV + 1:CONV + 2]).then_inc(dt_copied, 1)
            def copy_q(i, hp):
                act.wait_ge(q_done, i + 1)
                run(qT[:, hp % 2, :], bank[0][:], ACT.Copy).then_inc(q_copied, 1)

            def softmax_exp(i, hp):
                act.wait_ge(max_ready, i + 1)
                for j in range(4):
                    ins = run(probs[:, hp % 2, j, :], probs[:, hp % 2, j, :], ACT.Exp, scale=ATTN_SCALE,
                              bias=negmax[:, hp % 2, j:j + 1], accum_out=rowsum[:, hp % 2, j:j + 1])
                ins.then_inc(exp_done, 1)

            def softmax_scale(i, hp):
                act.wait_ge(inv_ready, i + 1)
                for j in range(4):
                    ins = run(probs[:, hp % 2, j, :], probs[:, hp % 2, j, :], ACT.Copy,
                              scale=rowinv[:, hp % 2, j:j + 1])
                ins.then_inc(p_ready, 1)

            a_flat = a_neg[:]

            def decays(i, b, hp):
                act.wait_ge(decay_free, i + 1)
                n, c = b * (STATE // BATCH) + hp // 2, hp % 2
                run(decay[:, hp % 2, :].rearrange("p (b l) -> p b l", b=BATCH)[:, :, 1:],
                    dt_sb[:, c, :].rearrange("p (b l) -> p b l", b=BATCH)[:, :, 1:], ACT.Exp,
                    scale=a_flat[:, c, bass.ds(n, 1)]).then_inc(decay_set, 1)

            def attention(b, last):
                for hp in range(GROUPS):
                    i = b * GROUPS + hp
                    act.wait_ge(t_done, i + 2)
                    for s in range(2):
                        ins = run(probsT[:, hp % 2, s, :], bank[3 + s][:], ACT.Copy)
                    ins.then_inc(pt_copied, 1)
                    more = not (last and hp == GROUPS - 1)
                    if more:
                        softmax_exp(i + 1, hp + 1)
                    if not (last and hp >= GROUPS - 2):
                        copy_q(i + 2, hp)
                    act.wait_ge(pv_done, i + 1)
                    run(attT[:, hp % 2, :], bank[5][:], ACT.Copy).then_inc(u_copied, 1)
                    if more:
                        softmax_scale(i + 1, hp + 1)
                        decays(i + 1, b + (hp + 1) // GROUPS, (hp + 1) % GROUPS)

            for c in range(IC):
                act.wait_ge(sp_neg, c + 1)
                run(decay[:, c, :], decay[:, c, :], ACT.Exp).then_inc(sp_exp, 1)
            copy_q(0, 0)
            copy_q(1, 1)
            softmax_exp(0, 0)
            softmax_scale(0, 0)
            for c in range(IC):
                act.wait_ge(sp_one, c + 1)
                run(drive[:, c, :], du_sb[:, c, :], ACT.Ln).then_inc(sp_ln, 1)
            act.wait_ge(dt_ready, 1)
            act.wait_ge(a_ready, 1)
            decays(0, 0, 0)
            with act.Fori(0, BATCH - 1) as b:
                attention(b, False)
            attention(BATCH - 1, True)

            def feed_forward(moe, n):
                norm_std(n)
                norm_copy(n)
                act.wait_ge(moe.key_ready, 1)
                run(expl[:, :, 0:moe.experts], logits[:, :, 0:moe.experts], ACT.Exp)
                if moe is moe1:
                    run(sgate[:], sgate[:], ACT.Exp, scale=-1.0)
                run(top_e[:], top_v[:], ACT.Exp).then_inc(moe.exp_ready, 1)
                for k in range(2 * SC):
                    act.wait_ge(moe.sh_gu_done, k + 1)
                    if k >= 2:
                        act.wait_ge(moe.sh_h_ready, k - 1)
                    run(sh_up[:, k % 2, :], bank[6 + k % 2][:], ACT.Copy)
                    run(sh_silu[:, k % 2, :], bank[4 + k % 2][:], ACT.Silu).then_inc(moe.sh_silu_done, 1)
                hidden = P if moe is moe0 else H1

                def copy_turned(s, parity):
                    act.wait_ge(moe.xt_done, s + 1)
                    run(xbT[:, parity].rearrange("p c t -> p (c t)"), bank[parity][:], ACT.Copy
                        ).then_inc(moe.xt_copied, 1)

                def silu(s, parity):
                    act.wait_ge(moe.gu_done, s + 1)
                    if moe is moe0:
                        for e in range(2):
                            r = slice(e * H0, (e + 1) * H0)
                            ins = run(h_silu[r, parity, :, r],
                                      bank[2 + parity][r, 0:2 * P].rearrange("p (u t) -> p u t", u=2)[:, :, r],
                                      ACT.Silu)
                    else:
                        ins = run(h_silu[0:hidden, parity].rearrange("p u t -> p (u t)"),
                                  bank[2 + parity][0:hidden, 0:2 * P], ACT.Silu)
                    ins.then_inc(moe.silu_done, 1)

                copy_turned(0, 0)
                for s in range(AHEAD):
                    copy_turned(s + 1, (s + 1) % 2)
                    silu(s, s % 2)
                if moe.steps // AHEAD > 2:
                    with act.Fori(1, moe.steps // AHEAD - 1) as m:
                        for k in range(AHEAD):
                            copy_turned(m * AHEAD + (k + 1), (k + 1) % 2)
                            silu(m * AHEAD + k, k % 2)
                for s in range(moe.steps - AHEAD, moe.steps):
                    if s < moe.steps - 1:
                        copy_turned(s + 1, (s + 1) % 2)
                    silu(s, s % 2)

            if stop >= 2:
                feed_forward(moe0, 1)
            if stop >= 3:
                norm_std(2)
                act.wait_ge(ln_out, TILES * 3)
                run(xn[:], xn[:], ACT.Silu).then_inc(z_ready, 1)
            if stop >= 4:
                feed_forward(moe1, 3)

        @block.vector
        def _(dve):
            steps = Steps(dve, dve_step)
            dve.sem_inc(o_taken, 1)
            dve.sem_inc(y_added, 1)
            v = nc.vector

            def norm(n):
                for a in range(TILES):
                    ins = v.bn_stats(stats[:, a, :], xr[:, a, :])
                    steps.mark(ins)
                steps.settle()
                for a in range(TILES):
                    ins = v.bn_aggr(moments[:, a, :], stats[:, a, :])
                    steps.mark(ins)
                steps.settle()
                v.tensor_copy(stats[:, :, 0], moments[:, :, 1]).then_inc(ln_var, 1)
                dve.wait_ge(ln_std, n + 1)
                steps.wait(v.reciprocal(rstd[:], rstd[:]))
                for a in range(TILES):
                    v.tensor_scalar(xn[:, a, :], xr[:, a, :], moments[:, a, 0:1], rstd[:, a:a + 1],
                                    ALU.subtract, ALU.mult).then_inc(ln_out, 1)

            dve.wait_ge(ld_x, 16)
            norm(0)
            for c in range(IC):
                ins = v.memset(xpad[:, c, :, 0:PAD], 0.0)
                steps.mark(ins)
            for c in range(IC):
                for h in range(2):
                    dve.wait_ge(xin_done, 2 * c + h + 1)
                    v.tensor_copy(xpad[:, c, 2 * h:2 * h + 2, PAD:],
                                  bank[4 + 2 * c + h][:].rearrange("p (b l) -> p b l", b=2)).then_inc(xin_copied, 1)
            dve.wait_ge(xin_copied, 4)
            dve.wait_ge(ld_ssm, 64)
            steps.settle()

            u4 = u_in[:].rearrange("p c (b l) -> p c b l", b=BATCH)
            for k in range(CONV):
                for c in range(IC):
                    src = xpad[:, c, :, PAD - CONV + 1 + k:PAD - CONV + 1 + k + SEQ]
                    w = small_w[:, c, k:k + 1]
                    if k == 0:
                        ins = v.tensor_scalar(u4[:, c], src, w, None, ALU.mult)
                    else:
                        ins = v.scalar_tensor_tensor(u4[:, c], src, w, u4[:, c], ALU.mult, ALU.add)
                    if k < CONV - 1:
                        steps.mark(ins)
                    else:
                        ins.then_inc(conv_done, 1)
                if k < CONV - 1:
                    steps.settle()

            dve.wait_ge(ld_mask, 16)
            steps.mark(v.tensor_scalar(mask_all[:, :, 0:SEQ], mask_u8[:], 1.0, -MASKED, ALU.subtract, ALU.mult))
            v.tensor_reduce(mask_all[:, :, SEQ], mask_u8[:], AX, ALU.max).then_inc(mask_set, 1)
            dve.wait_ge(a_exp, 1)
            v.tensor_scalar(a_neg[:], a_neg[:], -1.0, None, ALU.mult).then_inc(a_ready, 1)
            for h in range(2):
                dve.wait_ge(xdbl_done, h + 1)
                v.tensor_copy(xdbl[:, h * 512:(h + 1) * 512], bank[h][0:2 * STATE + RANK, :]).then_inc(xdbl_copied, 1)
            def softmax_max(i, hp):
                dve.wait_ge(s_done, i + 1)
                v.memset(pace[:], 0.0)
                for j in range(4):
                    ins = v.tensor_tensor_reduce(
                        out=probs[:, hp % 2, j, :], in0=bank[1 + j // 2][:, j % 2 * SEQ:(j % 2 + 1) * SEQ],
                        in1=mask_cur[:, 0:SEQ], scale=1.0, scalar=-3e38, op0=ALU.add, op1=ALU.max,
                        accum_out=rowmax[:, hp % 2, j:j + 1])
                ins.then_inc(s_masked, 1)
                dve.wait_ge(s_masked, i + 1)
                v.tensor_scalar(negmax[:, hp % 2, :], rowmax[:, hp % 2, :], -ATTN_SCALE, None, ALU.mult
                                ).then_inc(max_ready, 1)

            def softmax_inv(i, hp):
                dve.wait_ge(exp_done, i + 1)
                v.reciprocal(rowinv[:, hp % 2, :], rowsum[:, hp % 2, :]).then_inc(inv_made, 1)
                dve.wait_ge(inv_made, i + 1)
                v.tensor_scalar(rowinv[:, hp % 2, :], rowinv[:, hp % 2, :], mask_cur[:, SEQ:SEQ + 1], None,
                                ALU.mult).then_inc(inv_ready, 1)

            def mixer_scan(i, b, hp):
                k, c = hp // 2, hp % 2
                dve.wait_ge(decay_set, i + 1)
                dve.wait_ge(drive_set, i + 1)
                dve.wait_ge(y_added, i + 1)
                v.tensor_tensor_scan(state[:], decay[:, hp % 2, :], drive[:, hp % 2, :], 0.0, ALU.mult, ALU.add
                                     ).then_inc(decay_free, 1)
                dve.wait_ge(decay_free, i + 3)
                v.tensor_tensor(state[:], state[:], c_bc[:, k % 2, :], ALU.mult).then_inc(product_set, 1)

            def mixer_add(i, hp):
                c = hp % 2
                dve.wait_ge(product_set, i + 1)
                v.tensor_tensor(y_ssm[:, c, :], y_ssm[:, c, :], state[:], ALU.add).then_inc(y_added, 1)

            xr_flat = xr[:].rearrange("p a d -> p (a d)")

            def attention(b, last):
                for hp in range(GROUPS):
                    i = b * GROUPS + hp
                    more = not (last and hp == GROUPS - 1)
                    if more:
                        if hp == GROUPS - 1:
                            dve.wait_ge(mask_set, b + 3)
                        dve.wait_ge(t_done, i + 1)
                        softmax_max(i + 1, hp + 1)
                    mixer_scan(i, b, hp)
                    if more:
                        softmax_inv(i + 1, hp + 1)
                    mixer_add(i, hp)
                dve.wait_ge(o_done, b + 1)
                v.tensor_tensor(xr_flat[:, bass.ds(b * 2 * D, 2 * D)], xr_flat[:, bass.ds(b * 2 * D, 2 * D)],
                                bank[6][:], ALU.add).then_inc(o_taken, 1)

            dve.wait_ge(u_ready, 2)
            for c in range(IC):
                steps.mark(v.tensor_scalar(y_ssm[:, c, :], u_in[:, c, :], small_w[:, c, CONV + 2:CONV + 3], None, ALU.mult))
            for c in range(IC):
                dve.wait_ge(dt_copied, 2 * c + 2)
                v.scalar_tensor_tensor(decay[:, c, :], dt_sb[:, c, :], -1.0, dt_sb[:, c, :], ALU.mult, ALU.min
                                       ).then_inc(sp_neg, 1)
            for c in range(IC):
                dve.wait_ge(sp_exp, c + 1)
                v.tensor_scalar(du_sb[:, c, :], decay[:, c, :], 1.0, None, ALU.add).then_inc(sp_one, 1)
            dve.wait_ge(mask_set, 2)
            softmax_max(0, 0)
            for c in range(IC):
                dve.wait_ge(sp_one, c + 1)
                steps.mark(v.scalar_tensor_tensor(decay[:, c, :], du_sb[:, c, :], 1.0, decay[:, c, :],
                                                  ALU.subtract, ALU.subtract))
            softmax_inv(0, 0)
            steps.settle()
            for c in range(IC):
                dve.wait_ge(sp_ln, c + 1)
                steps.mark(v.tensor_tensor(decay[:, c, :], drive[:, c, :], decay[:, c, :], ALU.subtract))
            steps.settle()
            steps.wait(v.scalar_tensor_tensor(dt_sb[:], dt_sb[:], 0.0, decay[:], ALU.max, ALU.add))
            for n in range(2):
                v.memset(decay[:, n, :].rearrange("p (b l) -> p b l", b=BATCH)[:, :, 0:1], 0.0).then_inc(decay_free, 1)
            dve.wait_ge(decay_free, 2)
            v.tensor_copy(pace[:], eps_col[:]).then_inc(dt_ready, 1)
            dve.wait_ge(dt_ready, 1)
            v.tensor_tensor(du_sb[:], dt_sb[:], u_in[:], ALU.mult).then_inc(du_ready, 1)
            with dve.Fori(0, BATCH - 1) as b:
                attention(b, False)
            attention(BATCH - 1, True)
            dve.wait_ge(o_taken, BATCH + 1)

            def feed_forward(moe, n):
                norm(n)
                E = moe.experts
                lg, ex = logits[:, :, 0:E], expl[:, :, 0:E]
                hot = onehot[:].rearrange("p a e -> p (a e)")[:, 0:KT * E]
                prd = prod[:].rearrange("p a e -> p (a e)")[:, 0:KT * E]
                dve.wait_ge(moe.logits_done, 1)
                if moe is moe0:
                    steps.wait(v.tensor_tensor(lg, bank[0][:].rearrange("p (a e) -> p a e", e=E),
                                               route_bias[:].unsqueeze(1).broadcast_to([P, TILES, E]), ALU.add))
                else:
                    src = bank[0][:, 0:TILES * (E + 1)].rearrange("p (a e) -> p a e", e=E + 1)
                    steps.mark(v.tensor_copy(lg, src[:, :, 0:E]))
                    steps.wait(v.tensor_copy(sgate[:], src[:, :, E]))
                steps.wait(v.tensor_reduce(tmax[:], lg, AX, ALU.max))
                steps.wait(v.tensor_tensor(lg, lg, tmax[:].unsqueeze(2).broadcast_to([P, TILES, E]), ALU.subtract))
                steps.wait(v.tensor_scalar(lg, lg, UNDERFLOW, None, ALU.max))
                for a in range(TILES):
                    steps.mark(v.max(top_v[:, a, :], lg[:, a, :]))
                steps.settle()
                for a in range(TILES):
                    ins = v.max_index(top_i[:, a, :], top_v[:, a, :], lg[:, a, :])
                    steps.mark(ins)
                steps.settle()
                v.tensor_copy(idxf[:], top_i[:, :, 0:TOPK].rearrange("p a k -> p k a")).then_inc(moe.key_ready, 1)
                dve.wait_ge(moe.key_ready, 1)
                dve.wait_ge(consts_set, CONSTS)
                steps.wait(v.tensor_tensor(hot.rearrange("p (a e) -> p a e", e=E),
                                           iota_e[:, 0:E].unsqueeze(1).broadcast_to([P, KT, E]),
                                           idxf[:].rearrange("p k a -> p (k a)").unsqueeze(2).broadcast_to([P, KT, E]),
                                           ALU.is_equal))
                with nc.allow_low_precision(reason="sums of zeros and a one are exact"):
                    v.tensor_reduce(chosen[:, 0:TILES * E], hot.rearrange("p (k m) -> p m k", k=TOPK), AX,
                                    ALU.add).then_inc(moe.chosen_ready, 1)

                dve.wait_ge(moe.cum_done, 1)
                cm = cum[:].rearrange("p a e -> p (a e)")[:, 0:TILES * E]
                if moe is moe0:
                    v.tensor_copy(cm, bank[1][:, 0:TILES * E]).then_inc(moe.cum_copied, 1)
                    dve.wait_ge(moe.cum_copied, 1)
                else:
                    steps.wait(v.tensor_copy(counts[:], bank[2][:, 0:E]))
                    steps.wait(v.tensor_tensor(above[:], counts[:].unsqueeze(2).broadcast_to([P, E, TILES]),
                                               iota_blk[:].unsqueeze(1).broadcast_to([P, E, TILES]), ALU.is_gt))
                    steps.mark(v.memset(ones_row[:], 1.0))
                    steps.wait(v.tensor_reduce(nblk[:], above[:], AX, ALU.add))
                    steps.wait(v.tensor_tensor_scan(blk_end[:], ones_row[:], nblk[:], 0.0, ALU.mult, ALU.add))
                    steps.wait(v.tensor_tensor(first_slot[:], blk_end[:], nblk[:], ALU.subtract))
                    steps.wait(v.tensor_scalar(first_slot[:], first_slot[:], float(BLOCK), None, ALU.mult))
                    v.tensor_tensor(cm.rearrange("p (a e) -> p a e", e=E),
                                    bank[1][:, 0:TILES * E].rearrange("p (a e) -> p a e", e=E),
                                    first_slot[:].unsqueeze(1).broadcast_to([P, TILES, E]), ALU.add
                                    ).then_inc(moe.cum_copied, 1)
                    dve.wait_ge(moe.cum_copied, 1)
                steps.wait(v.tensor_tensor(prd.rearrange("p (k m) -> p k m", k=TOPK),
                                           hot.rearrange("p (k m) -> p k m", k=TOPK),
                                           cm.unsqueeze(1).broadcast_to([P, TOPK, TILES * E]), ALU.mult))
                steps.wait(v.tensor_reduce(pos[:], prd.rearrange("p (a e) -> p a e", e=E), AX, ALU.add))
                fidx = idxf[:].rearrange("p k a -> p (k a)")
                fw = wts[:].rearrange("p k a -> p (k a)")
                if moe is moe0:
                    steps.mark(v.tensor_scalar(over[:], pos[:], float(CAP), None, ALU.is_ge))
                    steps.wait(v.scalar_tensor_tensor(slot[:], fidx, float(CAP), pos[:], ALU.mult, ALU.add))
                    steps.wait(v.scalar_tensor_tensor(slot_i[:], over[:], SKIP, slot[:], ALU.mult, ALU.add))
                else:
                    steps.wait(v.tensor_copy(slot_i[:], pos[:]))
                B = moe.blocks
                steps.mark(v.tensor_scalar(part_i[:, 0, :], slot_i[:], 7, None, ALU.logical_shift_right))
                steps.wait(v.tensor_scalar(part_i[:, 1, :], slot_i[:], P - 1, None, ALU.bitwise_and))
                steps.wait(v.tensor_copy(part_f[:], part_i[:]))
                steps.mark(v.tensor_tensor(block_hot[:, :, 0:B], iota_j[:, 0:B].unsqueeze(1).broadcast_to([P, KT, B]),
                                           part_f[:, 0, :].unsqueeze(2).broadcast_to([P, KT, B]), ALU.is_equal))
                v.tensor_tensor(place_hot[:], iota_p[:].unsqueeze(1).broadcast_to([P, KT, P]),
                                part_f[:, 1, :].unsqueeze(2).broadcast_to([P, KT, P]), ALU.is_equal
                                ).then_inc(moe.places_ready, 1)
                steps.settle()
                v.tensor_tensor(block_rows[:, :, 0, 0:B], block_hot[:, :, 0:B],
                                row_high[:].unsqueeze(2).broadcast_to([P, KT, B]), ALU.mult
                                ).then_inc(moe.places_ready, 1)
                v.tensor_scalar(block_rows[:, :, 1, 0:B], block_hot[:, :, 0:B], row_low[:], None, ALU.mult
                                ).then_inc(moe.places_ready, 1)
                if moe is moe1:
                    steps.wait(v.tensor_tensor(behind, iota_j[0:1, :].unsqueeze(2).broadcast_to([1, BLOCKS, E]),
                                               blk_end[0:1, :].unsqueeze(1).broadcast_to([1, BLOCKS, E]), ALU.is_ge))
                    steps.wait(v.tensor_reduce(blk_ef[:], behind, AX, ALU.add))
                    v.tensor_scalar(blk_e[:], blk_ef[:], float(E - 1), None, ALU.min).then_inc(moe.blocks_ready, 1)
                dve.wait_ge(moe.exp_ready, 1)
                steps.wait(v.tensor_reduce(zsum[:], ex, AX, ALU.add))
                steps.wait(v.reciprocal(zsum[:], zsum[:]))
                steps.wait(v.tensor_tensor(wts[:], top_e[:, :, 0:TOPK].rearrange("p a k -> p k a"),
                                           zsum[:].unsqueeze(1).broadcast_to([P, TOPK, TILES]), ALU.mult))
                steps.wait(v.tensor_reduce(psum4[:], wts[:].rearrange("p k a -> p a k"), AX, ALU.add))
                if moe is moe1:
                    steps.wait(v.tensor_scalar(psum4[:], psum4[:], 1e-20, None, ALU.add))
                steps.wait(v.reciprocal(psum4[:], psum4[:]))
                steps.wait(v.tensor_tensor(wts[:], wts[:], psum4[:].unsqueeze(1).broadcast_to([P, TOPK, TILES]), ALU.mult))
                dve.wait_ge(moe.rows_done, 1)
                steps.wait(v.tensor_scalar(row_f[:, 0:B], bank[3][:, 0:B], float(P), float(NO_ROW), ALU.mult, ALU.add))
                steps.wait(v.tensor_tensor(row_put[:, 0:B], bank[3][:, B:2 * B], row_f[:, 0:B], ALU.add))
                v.tensor_scalar(row_get[:, 0:B], row_put[:, 0:B], TOKENS - 1, None, ALU.bitwise_and
                                ).then_inc(moe.rows_ready, 1)
                if moe is moe1:
                    steps.wait(v.tensor_scalar(sgate[:], sgate[:], 1.0, None, ALU.add))
                    steps.wait(v.reciprocal(sgate[:], sgate[:]))
                for q in range(4):
                    dve.wait_ge(moe.sh_y_done, q + 1)
                    if moe is moe0:
                        v.tensor_tensor(xr[:, 2 * q:2 * q + 2, :], xr[:, 2 * q:2 * q + 2, :],
                                        bank[4 + q][:].rearrange("p (a d) -> p a d", a=2), ALU.add
                                        ).then_inc(moe.sh_y_added, 1)
                    else:
                        for a in range(2):
                            ins = v.scalar_tensor_tensor(xr[:, 2 * q + a, :], bank[4 + q][:, a * D:(a + 1) * D],
                                                         sgate[:, 2 * q + a:2 * q + a + 1], xr[:, 2 * q + a, :],
                                                         ALU.mult, ALU.add)
                        ins.then_inc(moe.sh_y_added, 1)
                dve.wait_ge(moe.sh_y_added, 4)

                hidden = P if moe is moe0 else H1
                if moe is moe0:
                    steps.wait(v.memset(hT[:], 0.0))

                def product(s, parity):
                    dve.wait_ge(moe.silu_done, s + 1)
                    up = bank[2 + parity][:, 2 * P:4 * P].rearrange("p (u t) -> p u t", u=2)
                    if moe is moe0:
                        for e in range(2):
                            r = slice(e * H0, (e + 1) * H0)
                            ins = v.tensor_tensor(hT[r, parity, :, r], h_silu[r, parity, :, r], up[r, :, r], ALU.mult)
                    else:
                        ins = v.tensor_tensor(hT[0:hidden, parity], h_silu[0:hidden, parity], up[0:hidden], ALU.mult)
                    ins.then_inc(moe.h_ready, 1)

                def copy_y(s, k, first):
                    parity = k % 2
                    dve.wait_ge(moe.y_done, s + 1)
                    if not first:
                        dve.wait_ge(y_stored[k % STORES], 8 * s + 8 * (moe.before - k % STORES))
                    v.tensor_copy(yb[:, k % STORES].rearrange("p u d -> p (u d)"), bank[4 + parity][:]
                                  ).then_inc(moe.y_copied, 1)

                for s in range(AHEAD):
                    product(s, s % 2)
                    if s:
                        copy_y(s - 1, s - 1, s - 1 < STORES)
                with dve.Fori(1, moe.steps // AHEAD) as m:
                    for k in range(AHEAD):
                        product(m * AHEAD + k, k % 2)
                        copy_y(m * AHEAD + (k - 1), (k - 1) % AHEAD, False)
                copy_y(moe.steps - 1, AHEAD - 1, False)

                for first in range(0, TILES, 2):
                    for k in range(TOPK):
                        for a in (first, first + 1):
                            if k == 0:
                                dve.wait_ge(results_loaded[a % 4], 16 * (a // 4 + 1) + 32 * (moe is moe1))
                            c = k * TILES + a
                            ins = v.scalar_tensor_tensor(xr[:, a, :], yg[:, a % 4, k, :], fw[:, c:c + 1], xr[:, a, :],
                                                         ALU.mult, ALU.add)
                            if k < TOPK - 1:
                                steps.mark(ins)
                            else:
                                ins.then_inc(moe.combined, 1)
                        steps.settle()
                dve.wait_ge(moe.combined, TILES)

            if stop >= 2:
                feed_forward(moe0, 1)
            if stop >= 3:
                norm(2)
                dve.wait_ge(z_ready, 1)
                x5 = xn[:].rearrange("p (b c) l -> p b c l", c=IC)
                for c in range(IC):
                    ins = v.tensor_tensor(x5[:, :, c, :], y_ssm[:, c, :].rearrange("p (b l) -> p b l", b=BATCH),
                                          x5[:, :, c, :], ALU.mult)
                    steps.mark(ins)
                steps.settle()
                v.memset(tmax[:], 0.0).then_inc(z_gated, 1)
                dve.wait_ge(zT_done, 1)
                for b in range(BATCH):
                    ins = v.tensor_tensor(xr[:, 2 * b:2 * b + 2, :], xr[:, 2 * b:2 * b + 2, :],
                                          bank[b][:].rearrange("p (a d) -> p a d", a=2), ALU.add)
                    steps.mark(ins)
                steps.settle()
                v.memset(tmax[:], 0.0).then_inc(z_added, 1)
                dve.wait_ge(z_added, 1)
            if stop >= 4:
                feed_forward(moe1, 3)


STOP = 9


def kernel(**inputs):
    import numpy as np
    import concourse.bacc as bacc
    from concourse import mybir as mb
    from concourse.bass_utils import run_bass_kernel_spmd

    a = {n: np.asarray(v) for n, v in inputs.items()}

    def down(w):
        return w.reshape(-1, P, w.shape[-1]).transpose(1, 0, 2)

    fold = []
    for g in range(GROUPS):
        parts = [a["L0_xattn_Wq"][:, h * CTX:(h + 1) * CTX].T for h in (PAIR * g, PAIR * g + 1)]
        parts += [a[n][:, g * CTX:(g + 1) * CTX].T for n in ("L0_xattn_Wk", "L0_xattn_Wv")]
        parts += [a["L0_xattn_Wo"][h * CTX:(h + 1) * CTX] for h in (PAIR * g, PAIR * g + 1)]
        fold.append(np.concatenate(parts, 1))
    small = np.concatenate([a["L1_xattn_conv_w"].reshape(INNER, CONV)]
                           + [a[n].reshape(INNER, 1) for n in
                              ("L1_xattn_conv_b", "L1_xattn_dt_proj_b", "L1_xattn_D")]
                           + [a["L1_xattn_A_log"]], 1)
    xproj = a["L1_xattn_x_proj_w"]
    xproj = np.concatenate([xproj[RANK:], xproj[:RANK]], 0)

    def shared(gate, up, out):
        return np.concatenate([down(w).reshape(P, -1) for w in (gate, up, out)], 1)

    s_in = {n: a[n].transpose(1, 0, 2).reshape(D, SHARED) for n in ("L0_ffn_Sg", "L0_ffn_Su")}
    gu = np.stack([a["L0_ffn_Wg"], a["L0_ffn_Wu"]])
    gu = gu.reshape(2, E0 // 4, 2, 2, DC, P, H0).transpose(1, 5, 2, 0, 4, 3, 6)
    wd = a["L0_ffn_Wd"].reshape(E0 // 4, 2, 2 * H0, D).transpose(0, 2, 1, 3)
    experts0 = np.concatenate([gu.reshape(E0 // 4, P, -1), wd.reshape(E0 // 4, P, -1)], 2)
    gu1 = a["L1_ffn_gate_up_proj"].reshape(E1, 2, H1, DC, P).transpose(0, 4, 1, 3, 2)

    arrays = {
        "x": a["x"].reshape(TOKENS, D),
        "ctx": a["ctx_1024"].reshape(TOKENS, CTX),
        "ctxT": a["ctx_1024"].reshape(TOKENS, CTX).T,
        "mask": a["mask_BxS2_bf1"].reshape(1, TOKENS).view(np.uint8),
        "in_w": a["L1_xattn_in_proj_w"].T,
        "small_w": down(small),
        "xproj_w": down(xproj.T),
        "dtproj_w": a["L1_xattn_dt_proj_w"].T,
        "fold_w": np.stack(fold),
        "route0_w": down(a["L0_ffn_Wr"]),
        "route0_bias": a["L0_ffn_router_bias"].reshape(1, E0),
        "route1_w": down(np.concatenate([a["L1_ffn_gate_w"], a["L1_ffn_shared_expert_gate_w"]], 0).T),
        "shared0_w": shared(s_in["L0_ffn_Sg"], s_in["L0_ffn_Su"], a["L0_ffn_Sd"].reshape(SHARED, D)),
        "shared1_w": shared(a["L1_ffn_shared_gate_w"].T, a["L1_ffn_shared_up_w"].T,
                            a["L1_ffn_shared_down_w"].T),
        "experts0_w": experts0,
        "experts1_gu": gu1.reshape(E1, P, -1),
        "experts1_d": a["L1_ffn_down_proj"].transpose(0, 2, 1),
    }
    arrays = {n: np.ascontiguousarray(v) for n, v in arrays.items()}
    nc = bacc.Bacc("TRN2", target_bir_lowering=False, num_devices=1)
    tensors = {n: nc.dram_tensor(f"in_{n}", v.shape, mb.dt.from_np(v.dtype), kind="ExternalInput").ap()
               for n, v in arrays.items()}
    out = nc.dram_tensor("out", (TOKENS, D), mb.dt.float32, kind="ExternalOutput").ap()
    program(nc, tensors, out, STOP)
    r = run_bass_kernel_spmd(nc, [{f"in_{n}": v for n, v in arrays.items()}], core_ids=[0])
    return r.results[0]["out"].reshape(BATCH, SEQ, D)
```

```python
from contextlib import ExitStack

import concourse.bass as bass
from concourse import mybir

F32 = mybir.dt.float32
BF16 = mybir.dt.bfloat16
I32 = mybir.dt.int32
U32 = mybir.dt.uint32
U8 = mybir.dt.uint8
ALU = mybir.AluOpType
ACT = mybir.ActivationFunctionType
DVE_TILES = 6
AX = mybir.AxisListType.X

P = 128
BATCH = 4
SEQ = 256
TOKENS = BATCH * SEQ
D = 256
DC = D // P
TILES = TOKENS // P
CTX = 128
HEADS = 16
GROUPS = 8
PAIR = HEADS // GROUPS
EPS = 1e-5
MASKED = -1e9

STATE = 16
RANK = 8
CONV = 4
INNER = 256
IC = INNER // P
PAD = 4

TOPK = 4
E0, H0, CAP = 64, 64, 64
E1, H1 = 32, 96
SHARED = 512
SC = SHARED // P
EARLY_H = 5, 1
ROWS0 = E0 * CAP
BLOCK = 128
BLOCKS = E1 + (TOKENS * TOPK - E1) // BLOCK
BLOCKS += -BLOCKS % 16
ROWS1 = BLOCKS * BLOCK
STEP = 2 * P
AHEAD = 8
STORES = 4
KT = TOPK * TILES
UNDERFLOW = -104.0
CONSTS = 9
SKIP = float(1 << 20)
NO_ROW = TOPK * TOKENS

FOLDS = 4
STATES_EACH = 5
UNITS_EACH = 2 * STATES_EACH
UNITS = {False: ((0,), (1,), (2,), (3, 4), (5,), (6,), (7,), (8, 9)),
         True: ((0,), (1, 2), (3,), (4, 5), (6,), (7, 8), (9, 10), (11,))}
TURN_BANKS = {0: 0, 1: 1, 3: 4}
WARM = {"first loads": 6, "last sequence's norm": 10, "mixer's norm": 30, "layer 1's norm": 28,
        "layer 1's tokens": 14}
BC_BUFS = 3
BC_BUF = (0, 1, 0, 1, 2, 0)
PREP_FOLD = 2 * PAIR * D + 2 * CTX
SMALL = CONV + 3 + STATE
ATTN_SCALE = float(CTX) ** -0.5


class Steps:

    def __init__(self, engine, semaphore):
        self.engine, self.semaphore, self.count = engine, semaphore, 0

    def mark(self, instruction):
        instruction.then_inc(self.semaphore, 1)
        self.count += 1
        return self.count

    def wait(self, instruction):
        self.engine.wait_ge(self.semaphore, self.mark(instruction))

    def settle(self):
        self.engine.wait_ge(self.semaphore, self.count)


def program(nc, t, out, stop=9):
    with ExitStack() as ctx:
        def sem(name):
            return ctx.enter_context(nc.semaphore(name))

        def sb(name, shape, dt=F32, stack=ctx):
            return stack.enter_context(nc.sbuf_tensor(name, shape, dt))

        def dram(name, shape, dt=F32):
            return nc.dram_tensor(name, shape, dt).ap()

        bank = [ctx.enter_context(nc.psum_tensor(f"bank{i}", [P, 512], F32)) for i in range(8)]

        bc_dram = dram("bc_dram", (2 * STATE, TOKENS))
        tokens0_dram = dram("tokens0_dram", (TOKENS, D))
        results0_dram = dram("results0_dram", (TOPK * TOKENS, D))
        slots1_dram = dram("slots1_dram", (ROWS1, D))
        results1_dram = dram("results1_dram", (TOPK * TOKENS, D))

        xr = sb("xr", [P, TILES, D])
        xn = sb("xn", [P, TILES, D])
        xnT = sb("xnT", [P, DC, TOKENS])
        y_ssm = sb("y_ssm", [P, IC, TOKENS])
        shared_w = sb("shared_w", [P, 3072])
        route_w = sb("route_w", [P, DC, E0])
        route_bias = sb("route_bias", [P, E0])
        route1_w = sb("route1_w", [P, DC, E1 + 1])
        ident = sb("ident", [P, P])
        earlier = sb("earlier", [P, P], BF16)
        ones_bf = sb("ones_bf", [P, P], BF16)
        zeros = sb("zeros", [P, D])
        iota_e = sb("iota_e", [P, E0])
        iota_blk = sb("iota_blk", [P, TILES])
        iota_j = sb("iota_j", [P, BLOCKS])
        iota_p = sb("iota_p", [P, P])
        row_high = sb("row_high", [P, KT])
        row_low = sb("row_low", [P, 1])
        stats = sb("stats", [P, TILES, 6])
        moments = sb("moments", [P, TILES, 2])
        rstd = sb("rstd", [P, TILES])
        eps_col = sb("eps_col", [P, 1])
        pace = sb("pace", [P, 1])

        phase1 = ctx.enter_context(ExitStack())
        ctxT = sb("ctxT", [P, TOKENS], stack=phase1)
        ctxN = sb("ctxN", [P, TILES, CTX], stack=phase1)
        ctxN_cur = sb("ctxN_cur", [P, 2, CTX], stack=phase1)
        mask_u8 = sb("mask_u8", [P, BATCH, SEQ], U8, stack=phase1)
        mask_all = sb("mask_all", [P, BATCH, SEQ + 1], stack=phase1)
        mask_cur = sb("mask_cur", [P, SEQ + 1], stack=phase1)
        qk_w = sb("qk_w", [P, GROUPS, PAIR, DC, CTX], stack=phase1)
        vo_w = sb("vo_w", [P, GROUPS, PAIR, D], stack=phase1)
        in_w = sb("in_w", [P, INNER], stack=phase1)
        xproj_w = sb("xproj_w", [P, IC, 2 * STATE + RANK], stack=phase1)
        dtproj_w = sb("dtproj_w", [2 * STATE + RANK, INNER], stack=phase1)
        small_w = sb("small_w", [P, IC, SMALL], stack=phase1)
        a_neg = sb("a_neg", [P, IC, STATE], stack=phase1)
        xpad = sb("xpad", [P, IC, BATCH, PAD + SEQ], stack=phase1)
        u_in = sb("u_in", [P, IC, TOKENS], stack=phase1)
        dt_sb = sb("dt_sb", [P, IC, TOKENS], stack=phase1)
        du_sb = sb("du_sb", [P, IC, TOKENS], stack=phase1)
        xdbl = sb("xdbl", [2 * STATE + RANK, TOKENS], stack=phase1)
        decay = sb("decay", [P, 2, TOKENS], stack=phase1)
        drive = sb("drive", [P, 2, TOKENS], stack=phase1)
        state = sb("state", [P, 2, TOKENS], stack=phase1)
        rowmax = sb("rowmax", [P, 2, 4], stack=phase1)
        negmax = sb("negmax", [P, 2, 4], stack=phase1)
        rowsum = sb("rowsum", [P, 2, 4], stack=phase1)
        rowinv = sb("rowinv", [P, 2, 4], stack=phase1)
        with ExitStack() as before_mixer:
            fold_w = sb("fold_w", [P, FOLDS, PREP_FOLD], stack=before_mixer)
        b_bc = sb("b_bc", [P, BC_BUFS, TOKENS], stack=phase1)
        c_bc = sb("c_bc", [P, BC_BUFS, TOKENS], stack=phase1)
        qT = sb("qT", [P, 2, PAIR * SEQ], stack=phase1)
        probs = sb("probs", [P, 2, 4, SEQ], stack=phase1)
        probsT = sb("probsT", [P, 2, 2, PAIR * SEQ], stack=phase1)
        attT = sb("attT", [P, 2, PAIR * SEQ], stack=phase1)
        phase1.close()

        hshT = sb("hshT", [P, SC, TOKENS])
        sh_silu = sb("sh_silu", [P, 2, 512])
        sh_up = sb("sh_up", [P, 2, 512])
        logits = sb("logits", [P, TILES, E0])
        expl = sb("expl", [P, TILES, E0])
        tmax = sb("tmax", [P, TILES])
        top_v = sb("top_v", [P, TILES, 8])
        top_i = sb("top_i", [P, TILES, 8], U32)
        top_e = sb("top_e", [P, TILES, 8])
        zsum = sb("zsum", [P, TILES])
        psum4 = sb("psum4", [P, TILES])
        wts = sb("wts", [P, TOPK, TILES])
        idxf = sb("idxf", [P, TOPK, TILES])
        onehot = sb("onehot", [P, KT, E0])
        prod = sb("prod", [P, KT, E0])
        chosen = sb("chosen", [P, TILES * E0], BF16)
        cum = sb("cum", [P, TILES, E0])
        pos = sb("pos", [P, KT])
        over = sb("over", [P, KT])
        slot = sb("slot", [P, KT])
        slot_i = sb("slot_i", [P, KT], I32)
        part_i = sb("part_i", [P, 2, KT], I32)
        part_f = sb("part_f", [P, 2, KT])
        place_hot = sb("place_hot", [P, KT, P], BF16)
        block_hot = sb("block_hot", [P, KT, BLOCKS], BF16)
        block_rows = sb("block_rows", [P, KT, 2, BLOCKS], BF16)
        row_f = sb("row_f", [P, BLOCKS])
        row_put = sb("row_put", [P, BLOCKS], I32)
        row_get = sb("row_get", [P, BLOCKS], I32)
        counts = sb("counts", [P, E1])
        above = sb("above", [P, E1, TILES])
        nblk = sb("nblk", [P, E1])
        blk_end = sb("blk_end", [P, E1])
        first_slot = sb("first_slot", [P, E1])
        ones_row = sb("ones_row", [P, E1])
        behind = prod[0:1].rearrange("p a e -> p (a e)")[:, 0:BLOCKS * E1].rearrange("p (j e) -> p j e", e=E1)
        blk_ef = sb("blk_ef", [1, BLOCKS])
        blk_e = sb("blk_e", [1, BLOCKS], I32)
        sgate = sb("sgate", [P, TILES])
        xb = sb("xb", [P, AHEAD, 2, D])
        ew = sb("ew", [P, AHEAD, 1536])
        xbT = sb("xbT", [P, 2, DC, STEP])
        h_silu = sb("h_silu", [P, 2, 2, P])
        hT = sb("hT", [P, 2, 2, P])
        yb = sb("yb", [P, STORES, 2, D])
        yg = (hshT[:].rearrange("p j t -> p (j t)").rearrange("p (n k d) -> p n k d", n=4, k=TOPK),
              xb[:].rearrange("p n u d -> p (n u d)").rearrange("p (n k d) -> p n k d", n=4, k=TOPK))

        def results(a):
            return yg[a // 4][:, a % 4]


        ld_in = sem("ld_in")
        ld_x, ld_ctx, ld_mask, ld_ssm, ld_route = (sem(f"ld_{n}") for n in ("x", "ctx", "mask", "ssm", "route"))
        ld_fold = [sem(f"ld_fold_{k}") for k in range(FOLDS)]
        ld_shared, ld_shared1 = sem("ld_shared"), sem("ld_shared1")
        zero_filled, slots_zeroed = sem("zero_filled"), sem("slots_zeroed")
        consts_set, zeros_set = sem("consts_set"), sem("zeros_set")
        dve_step, act_step, pool_step = sem("dve_step"), sem("act_step"), sem("pool_step")
        ln_var, ln_std, ln_out, lnT_done, lnT_copied = (
            sem(f"ln_{n}") for n in ("var", "std", "out", "transposed", "copied"))
        du_ready = sem("du_ready")
        fold_done, fold_copied, dt_copied = sem("fold_done"), sem("fold_copied"), sem("dt_copied")
        late_fold_copied = sem("late_fold_copied")
        xin_done, xin_copied, conv_done, u_ready, xdbl_done, xdbl_copied, bc_stored = (
            sem(n) for n in ("xin_done", "xin_copied", "conv_done", "u_ready", "xdbl_done",
                             "xdbl_copied", "bc_stored"))
        dt_done, sp_neg, sp_exp, sp_one, sp_ln, a_exp, a_ready, dt_ready = (
            sem(n) for n in ("dt_done", "sp_neg", "sp_exp", "sp_one", "sp_ln", "a_exp", "a_ready",
                             "dt_ready"))
        bc_loaded = [sem(f"bc_loaded_{k}") for k in range(BC_BUFS)]
        decay_free, decay_set, drive_set, product_set, y_added = (
            sem(n) for n in ("decay_free", "decay_set", "drive_set", "product_set", "y_added"))
        scan_done = sem("scan_done")
        mask_set, ctx_set, inv_made = sem("mask_set"), sem("ctx_set"), sem("inv_made")
        q_done, q_copied, s_done, s_masked, max_ready, exp_done, inv_ready, p_ready = (
            sem(n) for n in ("q_done", "q_copied", "s_done", "s_masked", "max_ready", "exp_done",
                             "inv_ready", "p_ready"))
        t_done, pt_copied, pv_done, u_copied, o_done, o_taken = (
            sem(n) for n in ("t_done", "pt_copied", "pv_done", "u_copied", "o_done", "o_taken"))
        z_ready, z_gated, zT_done, z_added = (sem(n) for n in ("z_ready", "z_gated", "zT_done", "z_added"))
        out_stored = sem("out_stored")

        weights_loaded = [sem(f"weights_loaded_{k}") for k in range(AHEAD)]

        class Moe:

            def __init__(self, n, experts, rows, tokens, results):
                self.experts, self.blocks, self.steps = experts, rows // P, rows // STEP
                self.tokens, self.results = tokens, results
                self.logits_done = sem(f"logits_done{n}")
                self.key_ready = sem(f"key_ready{n}")
                self.exp_ready = sem(f"exp_ready{n}")
                self.chosen_ready = sem(f"chosen_ready{n}")
                self.cum_done = sem(f"cum_done{n}")
                self.tokens_stored = sem("tokens_stored") if n == 0 else None
                self.slots_ready = sem(f"slots_ready{n}")
                self.scattered = sem("scattered") if n == 1 else None
                self.late_h_ready = sem(f"sh_late_h_ready{n}")
                self.places_ready = sem(f"places_ready{n}")
                self.rows_done = sem(f"rows_done{n}")
                self.rows_ready = sem(f"rows_ready{n}")
                self.sh_gu_done = sem(f"sh_gu_done{n}")
                self.sh_silu_done = sem(f"sh_silu_done{n}")
                self.sh_h_ready = sem(f"sh_h_ready{n}")
                self.sh_y_done = sem(f"sh_y_done{n}")
                self.sh_y_added = sem(f"sh_y_added{n}")
                self.xt_done = sem(f"xt_done{n}")
                self.xt_copied = sem(f"xt_copied{n}")
                self.gu_done = sem(f"gu_done{n}")
                self.silu_done = sem(f"silu_done{n}")
                self.h_ready = sem(f"h_ready{n}")
                self.y_done = sem(f"y_done{n}")
                self.y_copied = sem(f"y_copied{n}")
                self.blocks_ready = sem("blocks_ready") if n == 1 else None
                self.tokens_loaded = (weights_loaded if n else [sem(f"tokens_loaded_{k}") for k in range(AHEAD)])
                self.early_h = EARLY_H[n]
                self.before = 0 if n == 0 else ROWS0 // STEP
                self.combined = sem(f"combined{n}")
                self.scaled = sem(f"results_scaled{n}")
                self.late_combined = sem(f"late_combined{n}")

        y_stored = [sem(f"y_stored_{k}") for k in range(STORES)]
        results_loaded = [sem(f"results_loaded_{a}") for a in range(TILES // 2)]

        moe0 = Moe(0, E0, ROWS0, tokens0_dram, results0_dram)
        moe1 = Moe(1, E1, ROWS1, slots1_dram, results1_dram)

        def dst_tokens(ap):
            return ap.rearrange("(a p) d -> p a d", p=P)

        def load_block_weights(engine, s, k, j):
            e = engine.value_load(blk_e[0:1, bass.ds(s * 2 + j, 1)], min_val=0, max_val=E1 - 1)
            engine.dma_start(ew[:, k, j * 384:(j + 1) * 384],
                             t["experts1_gu"][bass.ds(e, 1)].rearrange("a p f -> (a p) f")
                             ).then_inc(weights_loaded[k], 16)
            engine.dma_start(ew[0:H1, k, 768 + j * D:768 + (j + 1) * D],
                             t["experts1_d"][bass.ds(e, 1)].rearrange("a p f -> (a p) f")
                             ).then_inc(weights_loaded[k], 16)

        block = ctx.enter_context(nc.Block())

        @block.sync
        def _(sp):
            sp.dma_start(ctxT[:], t["ctxT"]).then_inc(ld_ctx, 16)
            sp.dma_start(in_w[:], t["in_w"]).then_inc(ld_in, 16)
            sp.dma_start(xr[:], dst_tokens(t["x"])).then_inc(ld_x, 16)
            sp.dma_start(small_w[:], t["small_w"]).then_inc(ld_ssm, 16)
            sp.dma_start(xproj_w[:], t["xproj_w"]).then_inc(ld_ssm, 16)
            sp.dma_start(dtproj_w[2 * STATE:, :], t["dtproj_w"]).then_inc(ld_ssm, 16)
            sp.dma_start(mask_u8[:].rearrange("p b s -> p (b s)"),
                         t["mask"].broadcast_to([P, TOKENS])).then_inc(ld_mask, 16)

            for g in range(FOLDS):
                sp.dma_start(fold_w[:, g, :], t["fold_w"][g]).then_inc(ld_fold[g], 16)
            with sp.Fori(0, GROUPS // FOLDS - 1) as m:
                for g in range(FOLDS):
                    sp.wait_ge(fold_done, FOLDS * m + (g + 1))
                    sp.dma_start(fold_w[:, g, :], t["fold_w"][bass.ds(FOLDS * m + (g + FOLDS), 1)]
                                 .rearrange("a p f -> (a p) f")).then_inc(ld_fold[g], 16)
            sp.dma_start(ctxN[:], dst_tokens(t["ctx"])).then_inc(ld_ctx, 16)

            sp.dma_start(shared_w[:], t["shared0_w"]).then_inc(ld_shared, 16)
            sp.dma_start(route_w[:], t["route0_w"]).then_inc(ld_route, 16)
            sp.dma_start(route_bias[:], t["route0_bias"].broadcast_to([P, E0])).then_inc(ld_route, 16)
            sp.dma_start(route1_w[:], t["route1_w"]).then_inc(ld_route, 16)

            sp.wait_ge(zeros_set, 1)
            for r in range(0, TOPK * TOKENS, 2048):
                sp.dma_start(dst_tokens(results0_dram[r:r + 2048, :]),
                             zeros[:].unsqueeze(1).broadcast_to([P, 2048 // P, D])).then_inc(zero_filled, 16)

            sp.wait_ge(xdbl_copied, 2)
            sp.dma_start(bc_dram, xdbl[0:2 * STATE, :]).then_inc(bc_stored, 16)
            sp.wait_ge(bc_stored, 16)

            def spread(n, j):
                for row, dst in ((n, b_bc), (n + STATE, c_bc)):
                    sp.dma_start(dst[:, BC_BUF[j], :], bc_dram[bass.ds(row, 1), :].broadcast_to([P, TOKENS])
                                 ).then_inc(bc_loaded[BC_BUF[j]], 16)

            for j in (0, 1, 4):
                spread(j, j)
            for r in range(0, ROWS1, 2048):
                sp.dma_start(dst_tokens(slots1_dram[r:r + 2048, :]),
                             zeros[:].unsqueeze(1).broadcast_to([P, 2048 // P, D])).then_inc(slots_zeroed, 16)
            with sp.Fori(0, BATCH - 2) as m:
                for done, j, ahead in ((1, 2, 0), (2, 3, 0), (3, 0, 1), (4, 1, 1), (5, 4, 1)):
                    sp.wait_ge(y_added, UNITS_EACH * m + (2 * done + 2))
                    spread(STATES_EACH * m + (STATES_EACH * ahead + j), j)
            for done, j in ((1, 2), (2, 3), (3, 5)):
                sp.wait_ge(y_added, UNITS_EACH * (BATCH - 2) + 2 * done + 2)
                spread(STATES_EACH * (BATCH - 2) + j, j)

            def expert_loads(moe, load_weights, n):
                if moe is moe0:
                    sp.wait_ge(y_added, 2 * STATE + 2)
                    sp.wait_ge(ln_out, TILES * (n + 1))
                    sp.dma_start(dst_tokens(moe.tokens), xn[:]).then_inc(moe.tokens_stored, 16)
                else:
                    sp.wait_ge(moe.blocks_ready, 1)

                for k in range(AHEAD):
                    load_weights(k, k)
                    if moe is moe1:
                        load_block_weights(sp, k, k, 1)
                with sp.Fori(1, moe.steps // AHEAD) as m:
                    for k in range(AHEAD):
                        s = m * AHEAD + k
                        sp.wait_ge(moe.y_done, s - (AHEAD - 1))
                        load_weights(s, k)

            def result_loads(moe):
                for k in range(STORES):
                    sp.wait_ge(y_stored[k], 32 * ((moe.before + moe.steps) // STORES))
                by_choice = moe.results.rearrange("(k a p) d -> p k a d", p=P, a=TILES)
                for a in (0, 1, 2, 3, 6, 7, 4, 5):
                    sp.dma_start(results(a), by_choice[:, :, a, :]).then_inc(results_loaded[a // 2], 16)

            def weights0(s, k):
                sp.dma_start(ew[:, k, :], t["experts0_w"][bass.ds(s, 1)].rearrange("a p f -> (a p) f")
                             ).then_inc(weights_loaded[k], 16)

            def weights1(s, k):
                load_block_weights(sp, s, k, 0)

            if stop >= 2:
                expert_loads(moe0, weights0, 1)
                sp.wait_ge(moe0.sh_y_done, 4)
                sp.dma_start(shared_w[:], t["shared1_w"]).then_inc(ld_shared1, 16)
                result_loads(moe0)
            if stop >= 4:
                expert_loads(moe1, weights1, 3)
                result_loads(moe1)
            if stop >= 4:
                for a in range(0, TILES, 2):
                    if a < DVE_TILES:
                        sp.wait_ge(moe1.combined, a + 2)
                    else:
                        sp.wait_ge(moe1.late_combined, a + 2 - DVE_TILES)
                    sp.dma_start(dst_tokens(out)[:, a:a + 2, :], xr[:, a:a + 2, :]).then_inc(out_stored, 16)
                sp.wait_ge(out_stored, 16 * TILES // 2)
            else:
                if stop == 1:
                    sp.wait_ge(o_taken, BATCH + 1)
                elif stop == 3:
                    sp.wait_ge(z_added, BATCH)
                else:
                    sp.wait_ge(moe0.combined, DVE_TILES)
                    sp.wait_ge(moe0.late_combined, TILES - DVE_TILES)
                sp.dma_start(dst_tokens(out), xr[:]).then_inc(out_stored, 16)
                sp.wait_ge(out_stored, 16)

        @block.gpsimd
        def _(pool):
            steps = Steps(pool, pool_step)
            steps.mark(nc.gpsimd.memset(zeros[:], 0.0))
            steps.mark(nc.gpsimd.memset(ident[:], 0.0))
            steps.mark(nc.gpsimd.memset(ones_bf[:], 1.0))
            steps.wait(nc.gpsimd.memset(earlier[:], 1.0))
            nc.gpsimd.affine_select(out=ident[:], in_=ident[:], compare_op=ALU.not_equal, fill=1.0, base=0,
                                    pattern=[[-1, P]], channel_multiplier=1).then_inc(consts_set, 1)
            nc.gpsimd.affine_select(out=earlier[:], in_=earlier[:], compare_op=ALU.is_gt, fill=0.0, base=0,
                                    pattern=[[1, P]], channel_multiplier=-1).then_inc(consts_set, 1)
            nc.gpsimd.iota(iota_e[:], pattern=[[1, E0]], base=0, channel_multiplier=0,
                           allow_small_or_imprecise_dtypes=True).then_inc(consts_set, 1)
            nc.gpsimd.iota(iota_blk[:], pattern=[[BLOCK, TILES]], base=0, channel_multiplier=0,
                           allow_small_or_imprecise_dtypes=True).then_inc(consts_set, 1)
            nc.gpsimd.iota(iota_j[:], pattern=[[1, BLOCKS]], base=0, channel_multiplier=0,
                           allow_small_or_imprecise_dtypes=True).then_inc(consts_set, 1)
            nc.gpsimd.iota(iota_p[:], pattern=[[1, P]], base=0, channel_multiplier=0,
                           allow_small_or_imprecise_dtypes=True).then_inc(consts_set, 1)
            nc.gpsimd.iota(row_high[:], pattern=[[1, KT]], base=-KT, channel_multiplier=0,
                           allow_small_or_imprecise_dtypes=True).then_inc(consts_set, 1)
            nc.gpsimd.iota(row_low[:], pattern=[[0, 1]], base=0, channel_multiplier=1,
                           allow_small_or_imprecise_dtypes=True).then_inc(consts_set, 1)
            nc.gpsimd.memset(eps_col[:], EPS).then_inc(consts_set, 1)
            nc.gpsimd.memset(zeros[:], 0.0).then_inc(zeros_set, 1)

            pool.wait_ge(mask_set, 1)
            nc.gpsimd.tensor_copy(mask_cur[:], mask_all[:, 0, :]).then_inc(mask_set, 1)
            pool.wait_ge(ld_ctx, 32)
            nc.gpsimd.tensor_copy(ctxN_cur[:], ctxN[:, 0:2, :]).then_inc(ctx_set, 1)
            mask_flat = mask_all[:].rearrange("p b s -> p (b s)")
            ctx_flat = ctxN[:].rearrange("p a d -> p (a d)")

            def mixer_drive(b, u):
                j, c = u // 2, u % 2
                loads = (-32, -32, 0, 0, None, 32)[j]
                pool.wait_ge(bc_loaded[BC_BUF[j]], b * 32 if loads is None else b * 64 + loads)
                pool.wait_ge(decay_free, b * UNITS_EACH + (u + 1 - UNITS_EACH))
                nc.gpsimd.tensor_tensor(drive[:, c, :], du_sb[:, c, :], b_bc[:, BC_BUF[j], :], ALU.mult
                                        ).then_inc(drive_set, 1)

            def next_sequence(b):
                pool.wait_ge(inv_ready, 8 * b + 8)
                nc.gpsimd.tensor_copy(mask_cur[:], mask_flat[:, bass.ds((b + 1) * (SEQ + 1), SEQ + 1)]
                                      ).then_inc(mask_set, 1)
                pool.wait_ge(pv_done, 8 * b + 8)
                nc.gpsimd.tensor_copy(ctxN_cur[:].rearrange("p a d -> p (a d)"),
                                      ctx_flat[:, bass.ds((b + 1) * 2 * CTX, 2 * CTX)]).then_inc(ctx_set, 1)

            def mixer_add(b, u):
                c = u % 2
                pool.wait_ge(product_set, b * UNITS_EACH + (u + 1 - UNITS_EACH))
                nc.gpsimd.tensor_tensor(y_ssm[:, c, :], y_ssm[:, c, :], state[:, c, :], ALU.add).then_inc(y_added, 1)

            next_sequence(0)
            pool.wait_ge(du_ready, 1)
            mixer_drive(1, 0)
            with pool.Fori(1, BATCH - 1) as b:
                for u in range(1, UNITS_EACH):
                    mixer_drive(b, u)
                    if u < UNITS_EACH - 1:
                        mixer_add(b, u - 1)
                next_sequence(b)
                mixer_drive(b + 1, 0)
                mixer_add(b, UNITS_EACH - 2)
                mixer_add(b, UNITS_EACH - 1)
            last_units = 2 * STATE - UNITS_EACH * (BATCH - 2)
            for u in range(1, last_units):
                mixer_drive(BATCH - 1, u)
                mixer_add(BATCH - 1, u - 1)
            mixer_add(BATCH - 1, last_units - 1)

            def shared_h(moe):
                for k in range(moe.early_h):
                    pool.wait_ge(moe.sh_silu_done, k + 1)
                    nc.gpsimd.tensor_tensor(hshT[:, k // 2, k % 2 * 512:(k % 2 + 1) * 512], sh_silu[:, k % 2, :],
                                            sh_up[:, k % 2, :], ALU.mult).then_inc(moe.sh_h_ready, 1)

            def expert_tokens(moe):
                def load(s):
                    for u in range(2):
                        nc.gpsimd.indirect_dma_start(
                            out=xb[:, s % AHEAD, u, :], out_offset=None, in_=moe.tokens,
                            in_offset=bass.IndirectOffsetOnAxis(ap=row_get[:, 2 * s + u:2 * s + u + 1], axis=0),
                            bounds_check=TOKENS - 1, oob_is_err=False).then_inc(moe.tokens_loaded[s % AHEAD], 16)

                def store(s):
                    pool.wait_ge(moe.y_copied, s + 1)
                    for u in range(2):
                        nc.gpsimd.indirect_dma_start(
                            out=moe.results,
                            out_offset=bass.IndirectOffsetOnAxis(ap=row_put[:, 2 * s + u:2 * s + u + 1], axis=0),
                            in_=yb[:, s % STORES, u, :], in_offset=None,
                            bounds_check=TOPK * TOKENS - 1, oob_is_err=False).then_inc(y_stored[s % STORES], 16)

                if moe is moe0:
                    pool.wait_ge(moe.tokens_stored, 16)
                    pool.wait_ge(moe.rows_ready, 1)
                    for s in range(AHEAD):
                        load(s)
                    pool.wait_ge(zero_filled, 16 * (TOPK * TOKENS // 2048))
                    for s in range(AHEAD, moe.steps):
                        pool.wait_ge(moe.xt_done, s - AHEAD + 1)
                        load(s)
                        store(s - AHEAD)
                    for s in range(moe.steps - AHEAD, moe.steps):
                        store(s)
                else:
                    pool.wait_ge(moe.slots_ready, 1)
                    pool.wait_ge(slots_zeroed, 16 * (ROWS1 // 2048))
                    for k in range(TOPK):
                        if k == 1:
                            pool.wait_ge(moe.slots_ready, 2)
                        for a in range(TILES):
                            c = k * TILES + a
                            nc.gpsimd.indirect_dma_start(
                                out=moe.tokens, out_offset=bass.IndirectOffsetOnAxis(ap=slot_i[:, c:c + 1], axis=0),
                                in_=xn[:, a, :], in_offset=None, bounds_check=ROWS1 - 1, oob_is_err=False,
                            ).then_inc(moe.scattered, 16)
                    pool.wait_ge(moe.rows_ready, 1)
                    for s in range(moe.steps):
                        store(s)

            def combine(moe):
                for k in range(TOPK):
                    for a in range(DVE_TILES, TILES):
                        pool.wait_ge(moe.scaled, k * (TILES - DVE_TILES) + a - DVE_TILES + 1)
                        ins = nc.gpsimd.tensor_tensor(xr[:, a, :], xr[:, a, :], results(a)[:, k, :], ALU.add)
                        if k < TOPK - 1:
                            steps.mark(ins)
                        else:
                            ins.then_inc(moe.late_combined, 1)
                    if k < TOPK - 1:
                        steps.settle()

            if stop >= 2:
                shared_h(moe0)
                expert_tokens(moe0)
                combine(moe0)
            if stop >= 4:
                shared_h(moe1)
                expert_tokens(moe1)
                combine(moe1)

        @block.tensor
        def _(pe):
            pe.sem_inc(t_done, 1)
            mm = nc.tensor.matmul

            def keep_warm(free_bank, count):
                for _ in range(count):
                    mm(free_bank[:, 0:P], ident[:], ident[:], start=True, stop=True)

            pe.wait_ge(consts_set, 1)
            keep_warm(bank[7], WARM["first loads"])
            pe.wait_ge(ld_ctx, 16)
            pe.wait_ge(ld_in, 16)
            for c in range(IC):
                for h in range(2):
                    mm(bank[2 * c + h][:], in_w[:, c * P:(c + 1) * P], ctxT[:, h * 512:(h + 1) * 512],
                       start=True, stop=True).then_inc(xin_done, 1)

            def turn_norm(n):
                first_bank = TURN_BANKS[n]
                for h in range(2):
                    if n == 1 and h == 1:
                        keep_warm(bank[7], WARM["last sequence's norm"])
                    for c in range(DC):
                        if n == 0:
                            pe.wait_ge(consts_set, CONSTS)
                            pe.wait_ge(xin_copied, 4)
                        for a in range(4):
                            tile = 4 * h + a
                            pe.wait_ge(ln_out, TILES * n + tile + 1)
                            ins = nc.tensor.transpose(bank[first_bank + 2 * c + h][:, a * P:(a + 1) * P],
                                                      xn[:, tile, c * P:(c + 1) * P], ident[:])
                        ins.then_inc(lnT_done, 1)

            def fold(g):
                first = 4 + 2 * (g % 2)
                pe.wait_ge(ld_fold[g % FOLDS], 16 * (g // FOLDS + 1))
                if 2 <= g < FOLDS + 2:
                    pe.wait_ge(fold_copied, g - 1)
                elif g >= FOLDS + 2:
                    pe.wait_ge(late_fold_copied, g - 1 - FOLDS)
                w = fold_w[:, g % FOLDS, :]
                wq, wk = w[:, 0:PAIR * D], w[:, PAIR * D:PAIR * D + CTX]
                wv, wo = w[:, PAIR * D + CTX:PAIR * D + 2 * CTX], w[:, PAIR * D + 2 * CTX:]
                for j in range(PAIR):
                    for c in range(DC):
                        mm(bank[first][:, (j * DC + c) * CTX:(j * DC + c + 1) * CTX],
                           wq[:, j * D + c * P:j * D + (c + 1) * P], wk, start=True, stop=True)
                for j in range(PAIR):
                    ins = mm(bank[first + 1][:, j * D:(j + 1) * D], wv, wo[:, j * D:(j + 1) * D],
                             start=True, stop=True)
                ins.then_inc(fold_done, 1)

            def mixer_projection(k):
                if k < 2:
                    if k == 0:
                        pe.wait_ge(u_ready, 2)
                        pe.wait_ge(late_fold_copied, GROUPS - FOLDS)
                    else:
                        pe.wait_ge(xdbl_copied, 1)
                    for c in range(IC):
                        ins = mm(bank[7][0:2 * STATE + RANK, :], xproj_w[:, c, :],
                                 u_in[:, c, k * 512:(k + 1) * 512], start=(c == 0), stop=(c == IC - 1))
                    ins.then_inc(xdbl_done, 1)
                else:
                    c, h = (k - 2) // 2, k % 2
                    if k == 2:
                        pe.wait_ge(xdbl_copied, 2)
                    else:
                        pe.wait_ge(dt_copied, k - 2)
                    mm(bank[7][:], dtproj_w[2 * STATE:, c * P:(c + 1) * P],
                       xdbl[2 * STATE:, h * 512:(h + 1) * 512], start=True, stop=True).then_inc(dt_done, 1)

            def queries(i, b, hp):
                for j in range(PAIR):
                    for c in range(DC):
                        ins = mm(bank[0][:, j * SEQ:(j + 1) * SEQ], qk_w[:, hp, j, c, :],
                                 xnT[:, c, bass.ds(b * SEQ, SEQ)], start=(c == 0), stop=(c == DC - 1))
                ins.then_inc(q_done, 1)

            def scores(i, b, hp):
                for j in range(4):
                    ins = mm(bank[1 + j // 2][:, j % 2 * SEQ:(j % 2 + 1) * SEQ],
                             qT[:, hp % 2, j * P:(j + 1) * P], ctxT[:, bass.ds(b * SEQ, SEQ)],
                             start=True, stop=True)
                ins.then_inc(s_done, 1)

            def output(i, hp):
                for j in range(PAIR):
                    for a in range(2):
                        ins = mm(bank[6][:, a * D:(a + 1) * D], attT[:, hp % 2, (2 * j + a) * P:(2 * j + a + 1) * P],
                                 vo_w[:, hp, j, :], start=(hp == 0 and j == 0 and a == 0),
                                 stop=(hp == GROUPS - 1 and j == PAIR - 1), skip_group_check=True)
                return ins

            def add_output(i, b, hp):
                if hp == 1:
                    pe.wait_ge(o_taken, b + 1)
                pe.wait_ge(u_copied, i + 1)
                ins = output(i - 1, (hp - 1) % GROUPS)
                if hp == 0:
                    ins.then_inc(o_done, 1)

            def attention(b, last, beside_mixer=False):
                for hp in range(GROUPS):
                    i = b * GROUPS + hp
                    more = not (last and hp == GROUPS - 1)
                    if more:
                        pe.wait_ge(q_copied, i + 2)
                        pe.wait_ge(s_masked, i + 1)
                        nb = b + (hp + 1) // GROUPS
                        scores(i + 1, nb, (hp + 1) % GROUPS)
                    if beside_mixer and hp == 0:
                        pe.wait_ge(late_fold_copied, GROUPS - FOLDS - 1)
                    pe.wait_ge(p_ready, i + 1)
                    pe.wait_ge(pt_copied, i + 1)
                    for s in range(2):
                        for j in range(4):
                            ins = nc.tensor.transpose(bank[3 + s][:, j * P:(j + 1) * P],
                                                      probs[:, hp % 2, j, s * P:(s + 1) * P], ident[:])
                    ins.then_inc(t_done, 1)
                    if not (last and hp >= GROUPS - 2):
                        pe.wait_ge(q_copied, i + 2)
                        queries(i + 2, b + (hp + 2) // GROUPS, (hp + 2) % GROUPS)
                    if beside_mixer and hp < 3:
                        mixer_projection(2 * hp)
                    early = last and hp >= GROUPS - 2
                    if early:
                        add_output(i, b, hp)
                    if hp == 0:
                        pe.wait_ge(ctx_set, b + 1)
                    pe.wait_ge(pt_copied, i + 2)
                    pe.wait_ge(u_copied, i + 1)
                    for s in range(2):
                        ins = mm(bank[5][:], ctxN_cur[:, s, :], probsT[:, hp % 2, s, :],
                                 start=(s == 0), stop=(s == 1))
                    ins.then_inc(pv_done, 1)
                    if not early and not (beside_mixer and hp == 0):
                        add_output(i, b, hp)
                    if beside_mixer and hp < 3:
                        mixer_projection(2 * hp + 1)

            fold(0)
            fold(1)
            turn_norm(0)
            fold(2)
            pe.wait_ge(lnT_copied, 4)
            pe.wait_ge(fold_copied, 2)
            queries(0, 0, 0)
            fold(3)
            pe.wait_ge(q_copied, 1)
            queries(1, 0, 1)
            scores(0, 0, 0)
            for g in range(FOLDS, GROUPS):
                fold(g)
            attention(0, False, True)
            with pe.Fori(1, BATCH - 1) as b:
                attention(b, False)
            attention(BATCH - 1, True)
            add_output(BATCH * GROUPS, BATCH, 0)

            def route(moe, turned):
                w, n = (route_w, E0) if moe is moe0 else (route1_w, E1 + 1)
                pe.wait_ge(ld_route, 48)
                for a in range(TILES):
                    if a % 4 == 0:
                        pe.wait_ge(lnT_copied, turned + 2 * (a // 4) + 2)
                    for c in range(DC):
                        ins = mm(bank[0][:, a * n:(a + 1) * n], xnT[:, c, a * P:(a + 1) * P], w[:, c, :],
                                 start=(c == 0), stop=(c == DC - 1))
                ins.then_inc(moe.logits_done, 1)

            def count(moe):
                n = moe.experts
                pe.wait_ge(moe.chosen_ready, 1)
                for a in range(TILES):
                    for b in range(a + 1):
                        ins = mm(bank[1][:, a * n:(a + 1) * n], (earlier if b == a else ones_bf)[:],
                                 chosen[:, b * n:(b + 1) * n], start=(b == 0), stop=(b == a))
                if moe is moe1:
                    for b in range(TILES):
                        ins = mm(bank[2][:, 0:n], ones_bf[:], chosen[:, b * n:(b + 1) * n],
                                 start=(b == 0), stop=(b == TILES - 1))
                ins.then_inc(moe.cum_done, 1)

            def shared(moe, k):
                j, h = k // 2, k % 2
                if k >= 2:
                    pe.wait_ge(moe.sh_silu_done, k - 1)
                for w, first in ((0, 4), (1, 6)):
                    if (k, w) == ((3, 0) if moe is moe0 else (1, 1)):
                        count(moe)
                    if moe is moe0 and (k, w) == (2 * SC - 1, 0):
                        rows_of_slots(moe)
                    for c in range(DC):
                        ins = mm(bank[first + h][:], shared_w[:, w * 1024 + c * SHARED + j * P:
                                                              w * 1024 + c * SHARED + (j + 1) * P],
                                 xnT[:, c, h * 512:(h + 1) * 512], start=(c == 0), stop=(c == DC - 1))
                ins.then_inc(moe.sh_gu_done, 1)

            def shared_out(moe):
                pe.wait_ge(moe.sh_h_ready, moe.early_h)
                for a in range(TILES):
                    if a % 4 == 0:
                        pe.wait_ge(moe.late_h_ready, 2 * SC - moe.early_h - 1 + a // 4)
                    if a == 2:
                        pe.wait_ge(moe.sh_silu_done, 2 * SC)
                    for j in range(SC):
                        ins = mm(bank[4 + a // 2][:, a % 2 * D:(a % 2 + 1) * D], hshT[:, j, a * P:(a + 1) * P],
                                 shared_w[:, 2048 + j * D:2048 + (j + 1) * D], start=(j == 0), stop=(j == SC - 1))
                    if a % 2:
                        ins.then_inc(moe.sh_y_done, 1)

            def rows_of_slots(moe):
                pe.wait_ge(moe.places_ready, 3)
                n = moe.blocks
                for c in range(KT):
                    ins = mm(bank[3][:, 0:2 * n], place_hot[:, c, :], block_rows[:, c, :, 0:n],
                             start=(c == 0), stop=(c == KT - 1))
                ins.then_inc(moe.rows_done, 1)

            def experts(moe):
                hidden = P if moe is moe0 else H1
                weights_each = 16 if moe is moe0 else 80
                tokens_each = 32 if moe is moe0 else 80

                def turn(s, m, k, first):
                    pe.wait_ge(moe.tokens_loaded[k], tokens_each * m + (tokens_each + 16 * moe.before // AHEAD))
                    if not first:
                        pe.wait_ge(moe.xt_copied, s - 1)
                    for c in range(DC):
                        for u in range(2):
                            ins = nc.tensor.transpose(bank[k % 2][:, (c * 2 + u) * P:(c * 2 + u + 1) * P],
                                                      xb[:, k, u, c * P:(c + 1) * P], ident[:])
                    ins.then_inc(moe.xt_done, 1)

                def gate_up(s, m, k, first):
                    parity = k % 2
                    pe.wait_ge(weights_loaded[k], weights_each * m + (weights_each + 16 * moe.before // AHEAD))
                    pe.wait_ge(moe.xt_copied, s + 1)
                    if not first:
                        pe.wait_ge(moe.h_ready, s - 1)
                    for u in range(2):
                        for w in range(2):
                            for c in range(DC):
                                o = ((u * 2 + w) * DC + c) * hidden
                                ins = mm(bank[2 + parity][0:hidden, (w * 2 + u) * P:(w * 2 + u + 1) * P],
                                         ew[:, k, o:o + hidden], xbT[:, parity, c, u * P:(u + 1) * P],
                                         start=(c == 0), stop=(c == DC - 1))
                    ins.then_inc(moe.gu_done, 1)

                def down(s, k, first):
                    parity = k % 2
                    pe.wait_ge(moe.h_ready, s + 1)
                    if not first:
                        pe.wait_ge(moe.y_copied, s - 1)
                    o = 4 * DC * hidden
                    for u in range(2):
                        ins = mm(bank[4 + parity][:, u * D:(u + 1) * D], hT[0:hidden, parity, u, :],
                                 ew[0:hidden, k, o + u * D:o + (u + 1) * D], start=True, stop=True)
                    ins.then_inc(moe.y_done, 1)

                def steps(m, first, last):
                    for k in range(AHEAD):
                        s = m * AHEAD + k
                        if not (last and k == AHEAD - 1):
                            turn(s + 1, m + (k + 1) // AHEAD, (k + 1) % AHEAD, first and k == 0)
                        if first and k == 1:
                            pe.wait_ge(moe.sh_y_added, 4)
                            pe.wait_ge(moe.rows_ready, 1)
                        gate_up(s, m, k, first and k < 2)
                        if not (first and k == 0):
                            down(s - 1, (k - 1) % AHEAD, first and k < 3)

                turn(0, 0, 0, True)
                steps(0, True, False)
                if moe.steps // AHEAD > 2:
                    with pe.Fori(1, moe.steps // AHEAD - 1) as m:
                        steps(m, False, False)
                steps(moe.steps // AHEAD - 1, False, True)
                down(moe.steps - 1, AHEAD - 1, False)

            def feed_forward(moe, n):
                turn_norm(n)
                route(moe, 4 * min(n, 2))
                if moe is moe1:
                    pe.wait_ge(ld_shared1, 16)
                else:
                    pe.wait_ge(ld_shared, 16)
                for k in range(2 * SC):
                    shared(moe, k)
                shared_out(moe)
                if moe is moe1:
                    rows_of_slots(moe)
                    keep_warm(bank[0], WARM["layer 1's tokens"])
                experts(moe)

            if stop >= 2:
                feed_forward(moe0, 1)
            if stop >= 3:
                pe.wait_ge(results_loaded[2], 32)
                keep_warm(bank[7], WARM["mixer's norm"])
                for b in range(BATCH):
                    pe.wait_ge(z_gated, b + 1)
                    for lc in range(2):
                        for c in range(IC):
                            ins = nc.tensor.transpose(bank[b][:, lc * D + c * P:lc * D + (c + 1) * P],
                                                      xn[:, 2 * b + c, lc * P:(lc + 1) * P], ident[:])
                    ins.then_inc(zT_done, 1)
            if stop >= 4:
                keep_warm(bank[7], WARM["layer 1's norm"])
                feed_forward(moe1, 3)

        @block.scalar
        def _(act):
            steps = Steps(act, act_step)
            act.sem_inc(pt_copied, 1)
            act.sem_inc(u_copied, 1)

            def run(out_, in_, func, **kw):
                return nc.scalar.activation(out_, in_, func, **kw)

            def norm_std(part, first=0, last=TILES):
                act.wait_ge(ln_var, part + 1)
                if part == 0:
                    act.wait_ge(consts_set, CONSTS)
                run(rstd[:, first:last], moments[:, first:last, 1], ACT.Sqrt, bias=eps_col[:]).then_inc(ln_std, 1)

            def norm_copy(n, halves=(0, 1)):
                turned = 4 * min(n, 2)
                first_bank = TURN_BANKS[n]
                for h in halves:
                    for c in range(DC):
                        act.wait_ge(lnT_done, turned + 2 * h + c + 1)
                        run(xnT[:, c, h * 512:(h + 1) * 512], bank[first_bank + 2 * c + h][:], ACT.Copy
                            ).then_inc(lnT_copied, 1)

            for c in range(IC):
                for h in range(2):
                    act.wait_ge(xin_done, 2 * c + h + 1)
                    run(xpad[:, c, 2 * h:2 * h + 2, PAD:], bank[2 * c + h][:].rearrange("p (b l) -> p b l", b=2),
                        ACT.Copy).then_inc(xin_copied, 1)
            norm_std(0)
            act.wait_ge(ld_ssm, 48)
            run(a_neg[:], small_w[:, :, CONV + 3:], ACT.Exp).then_inc(a_exp, 1)

            qk_flat = qk_w[:].rearrange("p g j c d -> p (g j c d)")

            vo_flat = vo_w[:].rearrange("p g j d -> p (g j d)")

            def copy_fold(g):
                first = 4 + 2 * (g % 2)
                act.wait_ge(fold_done, g + 1)
                run(qk_flat[:, g * 512:(g + 1) * 512], bank[first][:], ACT.Copy)
                run(vo_flat[:, g * 512:(g + 1) * 512], bank[first + 1][:], ACT.Copy).then_inc(fold_copied, 1)

            def copy_dt(k):
                c, h = k // 2, k % 2
                act.wait_ge(dt_done, k + 1)
                run(dt_sb[:, c, h * 512:(h + 1) * 512], bank[7][:], ACT.Identity,
                    bias=small_w[:, c, CONV + 1:CONV + 2]).then_inc(dt_copied, 1)

            def softplus_exp(c):
                act.wait_ge(sp_neg, c + 1)
                run(decay[:, c, :], decay[:, c, :], ACT.Exp).then_inc(sp_exp, 1)

            def copy_q(i, hp):
                act.wait_ge(q_done, i + 1)
                run(qT[:, hp % 2, :], bank[0][:], ACT.Copy).then_inc(q_copied, 1)

            def softmax_exp(i, hp):
                act.wait_ge(max_ready, i + 1)
                for j in range(4):
                    ins = run(probs[:, hp % 2, j, :], probs[:, hp % 2, j, :], ACT.Exp, scale=ATTN_SCALE,
                              bias=negmax[:, hp % 2, j:j + 1], accum_out=rowsum[:, hp % 2, j:j + 1])
                ins.then_inc(exp_done, 1)

            def softmax_scale(i, hp):
                act.wait_ge(inv_ready, i + 1)
                for j in range(4):
                    ins = run(probs[:, hp % 2, j, :], probs[:, hp % 2, j, :], ACT.Copy,
                              scale=rowinv[:, hp % 2, j:j + 1])
                ins.then_inc(p_ready, 1)

            def decays(b, u):
                j, c = u // 2, u % 2
                act.wait_ge(decay_free, b * UNITS_EACH + (u + 1 - UNITS_EACH))
                run(decay[:, c, :].rearrange("p (b l) -> p b l", b=BATCH)[:, :, 1:],
                    dt_sb[:, c, :].rearrange("p (b l) -> p b l", b=BATCH)[:, :, 1:], ACT.Exp,
                    scale=a_neg[:, c, bass.ds(b * STATES_EACH + (j - STATES_EACH), 1)]).then_inc(decay_set, 1)

            def attention(b, last, beside_mixer=False):
                for hp in range(GROUPS):
                    i = b * GROUPS + hp
                    act.wait_ge(t_done, i + 2)
                    for s in range(2):
                        ins = run(probsT[:, hp % 2, s, :], bank[3 + s][:], ACT.Copy)
                    ins.then_inc(pt_copied, 1)
                    more = not (last and hp == GROUPS - 1)
                    if beside_mixer and hp in (2, 3):
                        copy_dt(2 * hp - 3)
                    if more:
                        softmax_exp(i + 1, hp + 1)
                    if not (last and hp >= GROUPS - 2):
                        copy_q(i + 2, hp)
                    if beside_mixer and hp in (1, 2):
                        copy_dt(2 * hp - 2)
                    if not more:
                        norm_std(1, 0, TILES - 2)
                    act.wait_ge(pv_done, i + 1)
                    run(attT[:, hp % 2, :], bank[5][:], ACT.Copy).then_inc(u_copied, 1)
                    if more:
                        softmax_scale(i + 1, hp + 1)
                    if beside_mixer:
                        if hp in (3, 4):
                            softplus_exp(hp - 3)
                        if hp == 5:
                            act.wait_ge(sp_one, 1)
                            run(drive[:], du_sb[:], ACT.Ln).then_inc(sp_ln, 1)
                        if hp == GROUPS - 1:
                            act.wait_ge(dt_ready, 1)
                            act.wait_ge(a_ready, 1)
                            decays(1, 0)
                    elif hp < GROUPS - 1:
                        for u in UNITS[last][hp + 1]:
                            decays(b, u)
                    elif not last:
                        decays(b + 1, 0)

            copy_fold(0)
            copy_fold(1)
            norm_copy(0)
            copy_fold(2)
            copy_q(0, 0)
            copy_fold(3)
            copy_q(1, 1)
            for c in range(IC):
                act.wait_ge(conv_done, c + 1)
                run(u_in[:, c, :], u_in[:, c, :], ACT.Silu, bias=small_w[:, c, CONV:CONV + 1]).then_inc(u_ready, 1)
            softmax_exp(0, 0)
            softmax_scale(0, 0)
            attention(0, False, True)
            with act.Fori(1, BATCH - 1) as b:
                attention(b, False)
            attention(BATCH - 1, True)

            def feed_forward(moe, n):
                if moe is moe0:
                    norm_copy(n, (0,))
                    norm_std(2, TILES - 2)
                    norm_copy(n, (1,))
                else:
                    norm_std(4)
                    norm_copy(n)
                for k in range(2 * SC):
                    act.wait_ge(moe.sh_gu_done, k + 1)
                    if k >= 2:
                        if k - 2 < moe.early_h:
                            act.wait_ge(moe.sh_h_ready, k - 1)
                        else:
                            act.wait_ge(moe.late_h_ready, k - 1 - moe.early_h)
                    run(sh_up[:, k % 2, :], bank[6 + k % 2][:], ACT.Copy)
                    run(sh_silu[:, k % 2, :], bank[4 + k % 2][:], ACT.Silu).then_inc(moe.sh_silu_done, 1)
                act.wait_ge(moe.key_ready, 1)
                run(expl[:, :, 0:moe.experts], logits[:, :, 0:moe.experts], ACT.Exp)
                if moe is moe1:
                    run(sgate[:], sgate[:], ACT.Exp, scale=-1.0)
                run(top_e[:], top_v[:], ACT.Exp).then_inc(moe.exp_ready, 1)
                hidden = P if moe is moe0 else H1

                def copy_turned(s, parity):
                    act.wait_ge(moe.xt_done, s + 1)
                    run(xbT[:, parity].rearrange("p c t -> p (c t)"), bank[parity][:], ACT.Copy
                        ).then_inc(moe.xt_copied, 1)

                def silu(s, parity):
                    act.wait_ge(moe.gu_done, s + 1)
                    if moe is moe0:
                        for e in range(2):
                            r = slice(e * H0, (e + 1) * H0)
                            ins = run(h_silu[r, parity, :, r],
                                      bank[2 + parity][r, 0:2 * P].rearrange("p (u t) -> p u t", u=2)[:, :, r],
                                      ACT.Silu)
                    else:
                        ins = run(h_silu[0:hidden, parity].rearrange("p u t -> p (u t)"),
                                  bank[2 + parity][0:hidden, 0:2 * P], ACT.Silu)
                    ins.then_inc(moe.silu_done, 1)

                def load_tokens(s, k):
                    nc.scalar.dma_start(xb[:, k], dst_tokens(moe.tokens[bass.ds(s * STEP, STEP), :])
                                        ).then_inc(moe.tokens_loaded[k], 16)

                def next_weights(s, k, first=False):
                    if not first:
                        act.wait_ge(moe.y_done, s - 1)
                        load_block_weights(nc.scalar, s + (AHEAD - 2), (k - 2) % AHEAD, 1)

                def next_loads(s, k):
                    load_tokens(s + AHEAD, k)
                    next_weights(s, k, first=isinstance(s, int) and s < 2)

                if moe is moe1:
                    act.wait_ge(moe.scattered, 16 * KT)
                    for k in range(AHEAD):
                        load_tokens(k, k)
                copy_turned(0, 0)
                for s in range(AHEAD):
                    copy_turned(s + 1, (s + 1) % 2)
                    silu(s, s % 2)
                    if moe is moe1:
                        next_loads(s, s)
                if moe.steps // AHEAD > 2:
                    with act.Fori(1, moe.steps // AHEAD - 1) as m:
                        for k in range(AHEAD):
                            copy_turned(m * AHEAD + (k + 1), (k + 1) % 2)
                            silu(m * AHEAD + k, k % 2)
                            if moe is moe1:
                                next_loads(m * AHEAD + k, k)
                for s in range(moe.steps - AHEAD, moe.steps):
                    if s < moe.steps - 1:
                        copy_turned(s + 1, (s + 1) % 2)
                    silu(s, s % 2)
                    if moe is moe1 and s < moe.steps - AHEAD + 2:
                        next_weights(s, s % AHEAD)
                act.wait_ge(moe.sh_y_added, 4)
                for k in range(TOPK):
                    for a in range(DVE_TILES, TILES):
                        if k == 0:
                            act.wait_ge(results_loaded[a // 2], 64 if moe is moe1 else 32)
                        run(results(a)[:, k, :], results(a)[:, k, :], ACT.Copy, scale=wts[:, k, a:a + 1]
                            ).then_inc(moe.scaled, 1)

            if stop >= 2:
                feed_forward(moe0, 1)
            if stop >= 3:
                norm_std(3)
                for b in range(BATCH):
                    act.wait_ge(ln_out, TILES * 2 + 2 * b + 2)
                    run(xn[:, 2 * b:2 * b + 2, :], xn[:, 2 * b:2 * b + 2, :], ACT.Silu).then_inc(z_ready, 1)
            if stop >= 4:
                feed_forward(moe1, 3)

        @block.vector
        def _(dve):
            steps = Steps(dve, dve_step)
            dve.sem_inc(o_taken, 1)
            dve.sem_inc(y_added, 2)
            v = nc.vector

            def norm_statistics(first=0, last=TILES, given=0):
                for a in range(max(first, given), last):
                    steps.mark(v.bn_stats(stats[:, a, :], xr[:, a, :]))
                steps.settle()
                for a in range(first, last):
                    steps.mark(v.bn_aggr(moments[:, a, :], stats[:, a, :]))
                steps.settle()
                v.tensor_copy(stats[:, first:last, 0], moments[:, first:last, 1]).then_inc(ln_var, 1)

            def norm_scale(part, first=0, last=TILES):
                dve.wait_ge(ln_std, part + 1)
                steps.wait(v.reciprocal(rstd[:, first:last], rstd[:, first:last]))
                for a in range(first, last):
                    v.tensor_scalar(xn[:, a, :], xr[:, a, :], moments[:, a, 0:1], rstd[:, a:a + 1],
                                    ALU.subtract, ALU.mult).then_inc(ln_out, 1)

            dve.wait_ge(ld_x, 16)
            norm_statistics()
            norm_scale(0)
            for c in range(IC):
                ins = v.memset(xpad[:, c, :, 0:PAD], 0.0)
                steps.mark(ins)
            dve.wait_ge(ld_mask, 16)
            steps.mark(v.tensor_scalar(mask_all[:, :, 0:SEQ], mask_u8[:], 1.0, -MASKED, ALU.subtract, ALU.mult))
            v.tensor_reduce(mask_all[:, :, SEQ], mask_u8[:], AX, ALU.max).then_inc(mask_set, 1)
            dve.wait_ge(xin_copied, 4)
            dve.wait_ge(ld_ssm, 48)
            steps.settle()

            u4 = u_in[:].rearrange("p c (b l) -> p c b l", b=BATCH)
            for k in range(CONV):
                for c in range(IC):
                    src = xpad[:, c, :, PAD - CONV + 1 + k:PAD - CONV + 1 + k + SEQ]
                    w = small_w[:, c, k:k + 1]
                    if k == 0:
                        ins = v.tensor_scalar(u4[:, c], src, w, None, ALU.mult)
                    else:
                        ins = v.scalar_tensor_tensor(u4[:, c], src, w, u4[:, c], ALU.mult, ALU.add)
                    if k < CONV - 1:
                        steps.mark(ins)
                    else:
                        ins.then_inc(conv_done, 1)
                if k < CONV - 1:
                    steps.settle()

            dve.wait_ge(a_exp, 1)
            v.tensor_scalar(a_neg[:], a_neg[:], -1.0, None, ALU.mult).then_inc(a_ready, 1)

            def copy_xdbl(h):
                dve.wait_ge(xdbl_done, h + 1)
                v.tensor_copy(xdbl[:, h * 512:(h + 1) * 512], bank[7][0:2 * STATE + RANK, :]).then_inc(xdbl_copied, 1)

            qk_flat = qk_w[:].rearrange("p g j c d -> p (g j c d)")
            vo_flat = vo_w[:].rearrange("p g j d -> p (g j d)")

            def copy_fold(g):
                first = 4 + 2 * (g % 2)
                dve.wait_ge(fold_done, g + 1)
                v.tensor_copy(qk_flat[:, g * 512:(g + 1) * 512], bank[first][:])
                v.tensor_copy(vo_flat[:, g * 512:(g + 1) * 512], bank[first + 1][:]).then_inc(late_fold_copied, 1)

            def softmax_max(i, hp):
                dve.wait_ge(s_done, i + 1)
                v.memset(pace[:], 0.0)
                for j in range(4):
                    ins = v.tensor_tensor_reduce(
                        out=probs[:, hp % 2, j, :], in0=bank[1 + j // 2][:, j % 2 * SEQ:(j % 2 + 1) * SEQ],
                        in1=mask_cur[:, 0:SEQ], scale=1.0, scalar=-3e38, op0=ALU.add, op1=ALU.max,
                        accum_out=rowmax[:, hp % 2, j:j + 1])
                ins.then_inc(s_masked, 1)
                dve.wait_ge(s_masked, i + 1)
                v.tensor_scalar(negmax[:, hp % 2, :], rowmax[:, hp % 2, :], -ATTN_SCALE, None, ALU.mult
                                ).then_inc(max_ready, 1)

            def softmax_inv(i, hp):
                dve.wait_ge(exp_done, i + 1)
                v.reciprocal(rowinv[:, hp % 2, :], rowsum[:, hp % 2, :]).then_inc(inv_made, 1)
                dve.wait_ge(inv_made, i + 1)
                v.tensor_scalar(rowinv[:, hp % 2, :], rowinv[:, hp % 2, :], mask_cur[:, SEQ:SEQ + 1], None,
                                ALU.mult).then_inc(inv_ready, 1)

            def mixer_scan(b, u):
                j, c = u // 2, u % 2
                U = b * UNITS_EACH + (u - UNITS_EACH)
                dve.wait_ge(decay_set, U + 1)
                dve.wait_ge(drive_set, U + 1)
                dve.wait_ge(y_added, U + 1)
                v.tensor_tensor_scan(state[:, c, :], decay[:, c, :], drive[:, c, :], 0.0, ALU.mult, ALU.add
                                     ).then_inc(decay_free, 1)
                dve.wait_ge(decay_free, U + 3)
                v.tensor_tensor(state[:, c, :], state[:, c, :], c_bc[:, BC_BUF[j], :], ALU.mult
                                ).then_inc(product_set, 1)

            def mixer_middle(hp):
                if hp == 1:
                    copy_xdbl(1)
                if hp == 5:
                    steps.settle()
                    dve.wait_ge(sp_one, 1)
                    steps.mark(v.scalar_tensor_tensor(decay[:], du_sb[:], 1.0, decay[:], ALU.subtract, ALU.subtract))
                if hp == 6:
                    dve.wait_ge(sp_ln, 1)
                    steps.settle()
                    steps.mark(v.tensor_tensor(decay[:], drive[:], decay[:], ALU.subtract))

            def mixer_end(hp):
                if hp == 0:
                    copy_xdbl(0)
                if hp == 1:
                    dve.wait_ge(u_ready, 2)
                    for c in range(IC):
                        steps.mark(v.tensor_scalar(y_ssm[:, c, :], u_in[:, c, :], small_w[:, c, CONV + 2:CONV + 3],
                                                   None, ALU.mult))
                if hp in (2, 3):
                    c = hp - 2
                    dve.wait_ge(dt_copied, 2 * c + 2)
                    v.scalar_tensor_tensor(decay[:, c, :], dt_sb[:, c, :], -1.0, dt_sb[:, c, :], ALU.mult, ALU.min
                                           ).then_inc(sp_neg, 1)
                if hp == 4:
                    dve.wait_ge(sp_exp, 2)
                    v.tensor_scalar(du_sb[:], decay[:], 1.0, None, ALU.add).then_inc(sp_one, 1)
                if hp == 6:
                    steps.settle()
                    steps.wait(v.scalar_tensor_tensor(dt_sb[:], dt_sb[:], 0.0, decay[:], ALU.max, ALU.add))
                    for n in range(2):
                        v.memset(decay[:, n, :].rearrange("p (b l) -> p b l", b=BATCH)[:, :, 0:1], 0.0
                                 ).then_inc(decay_free, 1)
                    dve.wait_ge(decay_free, 2)
                    v.tensor_copy(pace[:], eps_col[:]).then_inc(dt_ready, 1)
                    dve.wait_ge(dt_ready, 1)
                    v.tensor_tensor(du_sb[:], dt_sb[:], u_in[:], ALU.mult).then_inc(du_ready, 1)

            xr_flat = xr[:].rearrange("p a d -> p (a d)")

            def take_output(b):
                r = bass.ds(b * 2 * D - 2 * D, 2 * D)
                dve.wait_ge(o_done, b)
                v.tensor_tensor(xr_flat[:, r], xr_flat[:, r], bank[6][:], ALU.add).then_inc(o_taken, 1)

            def attention(b, last, beside_mixer=False):
                for hp in range(GROUPS):
                    i = b * GROUPS + hp
                    more = not (last and hp == GROUPS - 1)
                    units = () if beside_mixer else UNITS[last][hp]
                    if more:
                        if hp == GROUPS - 1:
                            dve.wait_ge(mask_set, b + 3)
                        dve.wait_ge(t_done, i + 1)
                        softmax_max(i + 1, hp + 1)
                    if not more:
                        norm_statistics(0, TILES - 2, given=TILES - 2)
                    if beside_mixer:
                        mixer_middle(hp)
                    else:
                        mixer_scan(b, units[0])
                    if more:
                        softmax_inv(i + 1, hp + 1)
                    if beside_mixer:
                        mixer_end(hp)
                    for u in units[1:]:
                        mixer_scan(b, u)
                    if not more:
                        norm_scale(1, 0, TILES - 2)
                    if hp == 0 and not beside_mixer:
                        take_output(b)
                    if last and hp < TILES - 2:
                        dve.wait_ge(o_taken, BATCH)
                        steps.mark(v.bn_stats(stats[:, hp, :], xr[:, hp, :]))

            dve.wait_ge(mask_set, 2)
            softmax_max(0, 0)
            copy_fold(FOLDS)
            copy_fold(FOLDS + 1)
            softmax_inv(0, 0)
            copy_fold(FOLDS + 2)
            copy_fold(FOLDS + 3)
            attention(0, False, True)
            with dve.Fori(1, BATCH - 1) as b:
                attention(b, False)
            attention(BATCH - 1, True)
            take_output(BATCH)
            dve.wait_ge(o_taken, BATCH + 1)

            def feed_forward(moe, n):
                if moe is moe0:
                    norm_statistics(TILES - 2)
                    norm_scale(2, TILES - 2)
                else:
                    norm_statistics()
                    norm_scale(4)
                E = moe.experts
                lg, ex = logits[:, :, 0:E], expl[:, :, 0:E]
                hot = onehot[:].rearrange("p a e -> p (a e)")[:, 0:KT * E]
                prd = prod[:].rearrange("p a e -> p (a e)")[:, 0:KT * E]
                dve.wait_ge(moe.logits_done, 1)
                if moe is moe0:
                    dve.wait_ge(y_added, 2 * STATE + 2)
                if moe is moe0:
                    steps.wait(v.tensor_tensor(lg, bank[0][:].rearrange("p (a e) -> p a e", e=E),
                                               route_bias[:].unsqueeze(1).broadcast_to([P, TILES, E]), ALU.add))
                else:
                    src = bank[0][:, 0:TILES * (E + 1)].rearrange("p (a e) -> p a e", e=E + 1)
                    steps.mark(v.tensor_copy(lg, src[:, :, 0:E]))
                    steps.wait(v.tensor_copy(sgate[:], src[:, :, E]))
                steps.wait(v.tensor_reduce(tmax[:], lg, AX, ALU.max))
                steps.wait(v.tensor_tensor(lg, lg, tmax[:].unsqueeze(2).broadcast_to([P, TILES, E]), ALU.subtract))
                steps.wait(v.tensor_scalar(lg, lg, UNDERFLOW, None, ALU.max))
                for a in range(TILES):
                    steps.mark(v.max(top_v[:, a, :], lg[:, a, :]))
                steps.settle()
                for a in range(TILES):
                    ins = v.max_index(top_i[:, a, :], top_v[:, a, :], lg[:, a, :])
                    steps.mark(ins)
                steps.settle()
                v.tensor_copy(idxf[:], top_i[:, :, 0:TOPK].rearrange("p a k -> p k a")).then_inc(moe.key_ready, 1)
                dve.wait_ge(moe.key_ready, 1)
                dve.wait_ge(consts_set, CONSTS)
                steps.wait(v.tensor_tensor(hot.rearrange("p (a e) -> p a e", e=E),
                                           iota_e[:, 0:E].unsqueeze(1).broadcast_to([P, KT, E]),
                                           idxf[:].rearrange("p k a -> p (k a)").unsqueeze(2).broadcast_to([P, KT, E]),
                                           ALU.is_equal))
                with nc.allow_low_precision(reason="sums of zeros and a one are exact"):
                    v.tensor_reduce(chosen[:, 0:TILES * E], hot.rearrange("p (k m) -> p m k", k=TOPK), AX,
                                    ALU.add).then_inc(moe.chosen_ready, 1)

                dve.wait_ge(moe.cum_done, 1)
                cm = cum[:].rearrange("p a e -> p (a e)")[:, 0:TILES * E]
                if moe is moe0:
                    steps.wait(v.tensor_copy(cm, bank[1][:, 0:TILES * E]))
                else:
                    steps.wait(v.tensor_copy(counts[:], bank[2][:, 0:E]))
                    steps.wait(v.tensor_tensor(above[:], counts[:].unsqueeze(2).broadcast_to([P, E, TILES]),
                                               iota_blk[:].unsqueeze(1).broadcast_to([P, E, TILES]), ALU.is_gt))
                    steps.mark(v.memset(ones_row[:], 1.0))
                    steps.wait(v.tensor_reduce(nblk[:], above[:], AX, ALU.add))
                    steps.wait(v.tensor_tensor_scan(blk_end[:], ones_row[:], nblk[:], 0.0, ALU.mult, ALU.add))
                    steps.wait(v.tensor_tensor(first_slot[:], blk_end[:], nblk[:], ALU.subtract))
                    steps.wait(v.tensor_scalar(first_slot[:], first_slot[:], float(BLOCK), None, ALU.mult))
                    steps.wait(v.tensor_tensor(cm.rearrange("p (a e) -> p a e", e=E),
                                               bank[1][:, 0:TILES * E].rearrange("p (a e) -> p a e", e=E),
                                               first_slot[:].unsqueeze(1).broadcast_to([P, TILES, E]), ALU.add))

                def place(first, last):
                    r, q = slice(first * TILES, last * TILES), slice(first * TILES * E, last * TILES * E)
                    steps.wait(v.tensor_tensor(prd[:, q].rearrange("p (k m) -> p k m", k=last - first),
                                               hot[:, q].rearrange("p (k m) -> p k m", k=last - first),
                                               cm.unsqueeze(1).broadcast_to([P, last - first, TILES * E]), ALU.mult))
                    steps.wait(v.tensor_reduce(pos[:, r], prd[:, q].rearrange("p (a e) -> p a e", e=E), AX, ALU.add))
                    if moe is moe1:
                        v.tensor_copy(slot_i[:, r], pos[:, r]).then_inc(moe.slots_ready, 1)

                fidx = idxf[:].rearrange("p k a -> p (k a)")
                fw = wts[:].rearrange("p k a -> p (k a)")
                if moe is moe0:
                    place(0, TOPK)
                    steps.mark(v.tensor_scalar(over[:], pos[:], float(CAP), None, ALU.is_ge))
                    steps.wait(v.scalar_tensor_tensor(slot[:], fidx, float(CAP), pos[:], ALU.mult, ALU.add))
                    v.scalar_tensor_tensor(slot_i[:], over[:], SKIP, slot[:], ALU.mult, ALU.add
                                           ).then_inc(moe.slots_ready, 1)
                    dve.wait_ge(moe.slots_ready, 1)
                else:
                    place(0, 1)
                    place(1, TOPK)
                    dve.wait_ge(moe.slots_ready, 2)

                def shared_h(first, last):
                    for k in range(first, last):
                        dve.wait_ge(moe.sh_silu_done, k + 1)
                        v.tensor_tensor(hshT[:, k // 2, k % 2 * 512:(k % 2 + 1) * 512], sh_silu[:, k % 2, :],
                                        sh_up[:, k % 2, :], ALU.mult).then_inc(moe.late_h_ready, 1)

                if moe is moe1:
                    shared_h(moe.early_h, moe.early_h + 2)
                    steps.wait(v.tensor_tensor(behind, iota_j[0:1, :].unsqueeze(2).broadcast_to([1, BLOCKS, E]),
                                               blk_end[0:1, :].unsqueeze(1).broadcast_to([1, BLOCKS, E]), ALU.is_ge))
                    steps.wait(v.tensor_reduce(blk_ef[:], behind, AX, ALU.add))
                    v.tensor_scalar(blk_e[:], blk_ef[:], float(E - 1), None, ALU.min).then_inc(moe.blocks_ready, 1)
                if moe is moe1:
                    shared_h(moe.early_h + 2, 2 * SC)
                B = moe.blocks
                steps.mark(v.tensor_scalar(part_i[:, 0, :], slot_i[:], 7, None, ALU.logical_shift_right))
                steps.wait(v.tensor_scalar(part_i[:, 1, :], slot_i[:], P - 1, None, ALU.bitwise_and))
                steps.wait(v.tensor_copy(part_f[:], part_i[:]))
                steps.mark(v.tensor_tensor(block_hot[:, :, 0:B], iota_j[:, 0:B].unsqueeze(1).broadcast_to([P, KT, B]),
                                           part_f[:, 0, :].unsqueeze(2).broadcast_to([P, KT, B]), ALU.is_equal))
                v.tensor_tensor(place_hot[:], iota_p[:].unsqueeze(1).broadcast_to([P, KT, P]),
                                part_f[:, 1, :].unsqueeze(2).broadcast_to([P, KT, P]), ALU.is_equal
                                ).then_inc(moe.places_ready, 1)
                steps.settle()
                v.tensor_tensor(block_rows[:, :, 0, 0:B], block_hot[:, :, 0:B],
                                row_high[:].unsqueeze(2).broadcast_to([P, KT, B]), ALU.mult
                                ).then_inc(moe.places_ready, 1)
                v.tensor_scalar(block_rows[:, :, 1, 0:B], block_hot[:, :, 0:B], row_low[:], None, ALU.mult
                                ).then_inc(moe.places_ready, 1)
                def rows():
                    dve.wait_ge(moe.rows_done, 1)
                    steps.wait(v.tensor_scalar(row_f[:, 0:B], bank[3][:, 0:B], float(P), float(NO_ROW), ALU.mult, ALU.add))
                    steps.wait(v.tensor_tensor(row_put[:, 0:B], bank[3][:, B:2 * B], row_f[:, 0:B], ALU.add))
                    v.tensor_scalar(row_get[:, 0:B], row_put[:, 0:B], TOKENS - 1, None, ALU.bitwise_and
                                    ).then_inc(moe.rows_ready, 1)

                if moe is moe0:
                    shared_h(moe.early_h, 2 * SC - 1)
                    rows()
                    shared_h(2 * SC - 1, 2 * SC)
                def shared_added():
                    if moe is moe1:
                        steps.wait(v.tensor_scalar(sgate[:], sgate[:], 1.0, None, ALU.add))
                        steps.wait(v.reciprocal(sgate[:], sgate[:]))
                    for q in range(4):
                        dve.wait_ge(moe.sh_y_done, q + 1)
                        if moe is moe0:
                            v.tensor_tensor(xr[:, 2 * q:2 * q + 2, :], xr[:, 2 * q:2 * q + 2, :],
                                            bank[4 + q][:].rearrange("p (a d) -> p a d", a=2), ALU.add
                                            ).then_inc(moe.sh_y_added, 1)
                        else:
                            for a in range(2):
                                ins = v.scalar_tensor_tensor(xr[:, 2 * q + a, :], bank[4 + q][:, a * D:(a + 1) * D],
                                                             sgate[:, 2 * q + a:2 * q + a + 1], xr[:, 2 * q + a, :],
                                                             ALU.mult, ALU.add)
                            ins.then_inc(moe.sh_y_added, 1)

                dve.wait_ge(moe.exp_ready, 1)
                steps.wait(v.tensor_reduce(zsum[:], ex, AX, ALU.add))
                steps.wait(v.reciprocal(zsum[:], zsum[:]))
                steps.wait(v.tensor_tensor(wts[:], top_e[:, :, 0:TOPK].rearrange("p a k -> p k a"),
                                           zsum[:].unsqueeze(1).broadcast_to([P, TOPK, TILES]), ALU.mult))
                steps.wait(v.tensor_reduce(psum4[:], wts[:].rearrange("p k a -> p a k"), AX, ALU.add))
                if moe is moe1:
                    steps.wait(v.tensor_scalar(psum4[:], psum4[:], 1e-20, None, ALU.add))
                steps.wait(v.reciprocal(psum4[:], psum4[:]))
                steps.wait(v.tensor_tensor(wts[:], wts[:], psum4[:].unsqueeze(1).broadcast_to([P, TOPK, TILES]), ALU.mult))
                shared_added()
                if moe is moe1:
                    rows()
                dve.wait_ge(moe.sh_y_added, 4)

                hidden = P if moe is moe0 else H1
                if moe is moe0:
                    steps.wait(v.memset(hT[:], 0.0))

                def product(s, parity):
                    dve.wait_ge(moe.silu_done, s + 1)
                    up = bank[2 + parity][:, 2 * P:4 * P].rearrange("p (u t) -> p u t", u=2)
                    if moe is moe0:
                        for e in range(2):
                            r = slice(e * H0, (e + 1) * H0)
                            ins = v.tensor_tensor(hT[r, parity, :, r], h_silu[r, parity, :, r], up[r, :, r], ALU.mult)
                    else:
                        ins = v.tensor_tensor(hT[0:hidden, parity], h_silu[0:hidden, parity], up[0:hidden], ALU.mult)
                    ins.then_inc(moe.h_ready, 1)

                def copy_y(s, k, first):
                    parity = k % 2
                    dve.wait_ge(moe.y_done, s + 1)
                    if not first:
                        dve.wait_ge(y_stored[k % STORES], 8 * s + 8 * (moe.before - k % STORES))
                    v.tensor_copy(yb[:, k % STORES].rearrange("p u d -> p (u d)"), bank[4 + parity][:]
                                  ).then_inc(moe.y_copied, 1)

                for s in range(AHEAD):
                    product(s, s % 2)
                    if s:
                        copy_y(s - 1, s - 1, s - 1 < STORES)
                with dve.Fori(1, moe.steps // AHEAD) as m:
                    for k in range(AHEAD):
                        product(m * AHEAD + k, k % 2)
                        copy_y(m * AHEAD + (k - 1), (k - 1) % AHEAD, False)
                copy_y(moe.steps - 1, AHEAD - 1, False)

                for first in range(0, DVE_TILES, 2):
                    for k in range(TOPK):
                        for a in (first, first + 1):
                            if k == 0:
                                dve.wait_ge(results_loaded[a // 2], 64 if moe is moe1 else 32)
                            c = k * TILES + a
                            ins = v.scalar_tensor_tensor(xr[:, a, :], results(a)[:, k, :], fw[:, c:c + 1], xr[:, a, :],
                                                         ALU.mult, ALU.add)
                            if k < TOPK - 1:
                                steps.mark(ins)
                            else:
                                ins.then_inc(moe.combined, 1)
                        steps.settle()
                    if moe is moe0:
                        dve.wait_ge(moe.combined, first + 2)
                        for a in (first, first + 1):
                            steps.mark(v.bn_stats(stats[:, a, :], xr[:, a, :]))
                dve.wait_ge(moe.combined, DVE_TILES)
                dve.wait_ge(moe.late_combined, TILES - DVE_TILES)

            if stop >= 2:
                feed_forward(moe0, 1)
            if stop >= 3:
                norm_statistics(given=DVE_TILES)
                norm_scale(3)
                x5 = xn[:].rearrange("p (b c) l -> p b c l", c=IC)
                for b in range(BATCH):
                    dve.wait_ge(z_ready, b + 1)
                    v.tensor_tensor(x5[:, b], y_ssm[:, :, b * SEQ:(b + 1) * SEQ], x5[:, b], ALU.mult
                                    ).then_inc(z_gated, 1)
                for b in range(BATCH):
                    dve.wait_ge(zT_done, b + 1)
                    v.tensor_tensor(xr[:, 2 * b:2 * b + 2, :], xr[:, 2 * b:2 * b + 2, :],
                                    bank[b][:].rearrange("p (a d) -> p a d", a=2), ALU.add).then_inc(z_added, 1)
                dve.wait_ge(z_added, BATCH)
            if stop >= 4:
                feed_forward(moe1, 3)


STOP = 9


def kernel(**inputs):
    import numpy as np
    import concourse.bacc as bacc
    from concourse import mybir as mb
    from concourse.bass_utils import run_bass_kernel_spmd

    a = {n: np.asarray(v) for n, v in inputs.items()}

    def down(w):
        return w.reshape(-1, P, w.shape[-1]).transpose(1, 0, 2)

    fold = []
    for g in range(GROUPS):
        parts = [a["L0_xattn_Wq"][:, h * CTX:(h + 1) * CTX].T for h in (PAIR * g, PAIR * g + 1)]
        parts += [a[n][:, g * CTX:(g + 1) * CTX].T for n in ("L0_xattn_Wk", "L0_xattn_Wv")]
        parts += [a["L0_xattn_Wo"][h * CTX:(h + 1) * CTX] for h in (PAIR * g, PAIR * g + 1)]
        fold.append(np.concatenate(parts, 1))
    small = np.concatenate([a["L1_xattn_conv_w"].reshape(INNER, CONV)]
                           + [a[n].reshape(INNER, 1) for n in
                              ("L1_xattn_conv_b", "L1_xattn_dt_proj_b", "L1_xattn_D")]
                           + [a["L1_xattn_A_log"]], 1)
    xproj = a["L1_xattn_x_proj_w"]
    xproj = np.concatenate([xproj[RANK:], xproj[:RANK]], 0)

    def shared(gate, up, out):
        return np.concatenate([down(w).reshape(P, -1) for w in (gate, up, out)], 1)

    s_in = {n: a[n].transpose(1, 0, 2).reshape(D, SHARED) for n in ("L0_ffn_Sg", "L0_ffn_Su")}
    gu = np.stack([a["L0_ffn_Wg"], a["L0_ffn_Wu"]])
    gu = gu.reshape(2, E0 // 4, 2, 2, DC, P, H0).transpose(1, 5, 2, 0, 4, 3, 6)
    wd = a["L0_ffn_Wd"].reshape(E0 // 4, 2, 2 * H0, D).transpose(0, 2, 1, 3)
    experts0 = np.concatenate([gu.reshape(E0 // 4, P, -1), wd.reshape(E0 // 4, P, -1)], 2)
    gu1 = a["L1_ffn_gate_up_proj"].reshape(E1, 2, H1, DC, P).transpose(0, 4, 1, 3, 2)

    arrays = {
        "x": a["x"].reshape(TOKENS, D),
        "ctx": a["ctx_1024"].reshape(TOKENS, CTX),
        "ctxT": a["ctx_1024"].reshape(TOKENS, CTX).T,
        "mask": a["mask_BxS2_bf1"].reshape(1, TOKENS).view(np.uint8),
        "in_w": a["L1_xattn_in_proj_w"].T,
        "small_w": down(small),
        "xproj_w": down(xproj.T),
        "dtproj_w": a["L1_xattn_dt_proj_w"].T,
        "fold_w": np.stack(fold),
        "route0_w": down(a["L0_ffn_Wr"]),
        "route0_bias": a["L0_ffn_router_bias"].reshape(1, E0),
        "route1_w": down(np.concatenate([a["L1_ffn_gate_w"], a["L1_ffn_shared_expert_gate_w"]], 0).T),
        "shared0_w": shared(s_in["L0_ffn_Sg"], s_in["L0_ffn_Su"], a["L0_ffn_Sd"].reshape(SHARED, D)),
        "shared1_w": shared(a["L1_ffn_shared_gate_w"].T, a["L1_ffn_shared_up_w"].T,
                            a["L1_ffn_shared_down_w"].T),
        "experts0_w": experts0,
        "experts1_gu": gu1.reshape(E1, P, -1),
        "experts1_d": a["L1_ffn_down_proj"].transpose(0, 2, 1),
    }
    arrays = {n: np.ascontiguousarray(v) for n, v in arrays.items()}
    nc = bacc.Bacc("TRN2", target_bir_lowering=False, num_devices=1)
    tensors = {n: nc.dram_tensor(f"in_{n}", v.shape, mb.dt.from_np(v.dtype), kind="ExternalInput").ap()
               for n, v in arrays.items()}
    out = nc.dram_tensor("out", (TOKENS, D), mb.dt.float32, kind="ExternalOutput").ap()
    program(nc, tensors, out, STOP)
    r = run_bass_kernel_spmd(nc, [{f"in_{n}": v for n, v in arrays.items()}], core_ids=[0])
    return r.results[0]["out"].reshape(BATCH, SEQ, D)
```
